# Optimizing a Trainium2 kernel written in Bass

```python
import numpy as np
import jax
import jax.numpy as jnp

def _softmax(x, axis=-1):
    return jax.nn.softmax(x, axis=axis)

def _gelu(x):
    return jax.nn.gelu(x, approximate=True)

def _silu(x):
    return jax.nn.silu(x)

def _sigmoid(x):
    return jax.nn.sigmoid(x)

def _layernorm(x, axis=-1, eps=1e-05):
    m = jnp.mean(x, axis=axis, keepdims=True)
    v = jnp.var(x, axis=axis, keepdims=True)
    return (x - m) / jnp.sqrt(v + eps)

def _scatter_add(tgt, idx, src, axis=0):
    return tgt.at[idx].add(src)

def _segment_sum(src, seg, n):
    return jax.ops.segment_sum(src, seg, n)
kernel_name = 'mk_adj_resnorm_d2_adj_r2_53a828'

def setup_inputs(seed: int=0):
    np.random.seed(seed)
    _w = jnp.asarray

    def _rec_inputs():
        import jax
        import jax.numpy as jnp
        _gk = jax.random.key(seed)
        x = -1.394e-06 + 0.9999 * jax.random.normal(jax.random.fold_in(_gk, 1), (16, 512, 256), jnp.float32)
        _a = jax.random.bernoulli(jax.random.fold_in(_gk, 2), 0.0078125, (16, 512, 512))
        adj = _a.astype(jnp.int32)
        return (x, adj)
    x, adj = _rec_inputs()

    def _L0_gnn_setup():
        import jax, jax.numpy as jnp
        import numpy as np
        NEG_INF = -1000000000.0
        NEG_SLOPE = 0.2

        def gat_layer(x, mask, W, a_src, a_dst, bias, concat):
            B, N, _ = x.shape
            H, F = a_src.shape
            xl = (x @ W).reshape(B, N, H, F)
            asrc = jnp.einsum('bnhf,hf->bnh', xl, a_src)
            adst = jnp.einsum('bnhf,hf->bnh', xl, a_dst)
            e = jax.nn.leaky_relu(asrc[:, :, None, :] + adst[:, None, :, :], NEG_SLOPE)
            e = jnp.where(mask[..., None], e, NEG_INF)
            attn = jax.nn.softmax(e, axis=1)
            out = jnp.einsum('bsdh,bshf->bdhf', attn, xl)
            if concat:
                out = out.reshape(B, N, H * F)
            else:
                out = out.mean(axis=2)
            return out + bias
        key = jax.random.key(seed)
        ks = jax.random.split(key, 10)
        B, N, Din, Fh, H, Dout = (8, 512, 256, 128, 4, 256)
        s = 0.05
        return {'adj': jax.random.randint(ks[0], (B, N, N), 0, 2, dtype=jnp.int32), 'x': jax.random.normal(ks[1], (B, N, Din), dtype=jnp.float32), 'W1': jax.random.normal(ks[2], (Din, H * Fh), dtype=jnp.float32) * s, 'att_src1': jax.random.normal(ks[3], (H, Fh), dtype=jnp.float32) * s, 'att_dst1': jax.random.normal(ks[4], (H, Fh), dtype=jnp.float32) * s, 'b1': jax.random.normal(ks[5], (H * Fh,), dtype=jnp.float32) * s, 'W2': jax.random.normal(ks[6], (H * Fh, Dout), dtype=jnp.float32) * s, 'att_src2': jax.random.normal(ks[7], (1, Dout), dtype=jnp.float32) * s, 'att_dst2': jax.random.normal(ks[8], (1, Dout), dtype=jnp.float32) * s, 'b2': jax.random.normal(ks[9], (Dout,), dtype=jnp.float32) * s}
    _L0_gnn_all = _L0_gnn_setup()
    _L0_gnn_in = {k: v for k, v in _L0_gnn_all.items() if k in ('W1', 'att_src1', 'att_dst1', 'b1', 'W2', 'att_src2', 'att_dst2', 'b2')}
    del _L0_gnn_all

    def _L1_gnn_setup():
        import jax, jax.numpy as jnp
        import numpy as np
        L = 3
        D = 256
        B, N = (8, 512)
        EPS = 1e-05

        def layernorm(x, gamma, beta):
            mu = jnp.mean(x, axis=-1, keepdims=True)
            var = jnp.var(x, axis=-1, keepdims=True)
            return (x - mu) * jax.lax.rsqrt(var + EPS) * gamma + beta
        key = jax.random.key(seed)
        ks = jax.random.split(key, 12)
        s = 1.0 / np.sqrt(D)
        node_features = jax.random.normal(ks[0], (B, N, D), dtype=jnp.float32)
        adjacency_matrix = jax.random.randint(ks[1], (B, N, N), 0, 2, dtype=jnp.int32)
        return {'node_features': node_features, 'adjacency_matrix': adjacency_matrix, 'attn_w': jax.random.normal(ks[2], (L, 2 * D), dtype=jnp.float32) * (1.0 / np.sqrt(2 * D)), 'attn_b': jax.random.normal(ks[3], (L,), dtype=jnp.float32) * 0.01, 'W1': jax.random.normal(ks[4], (L, D, 4 * D), dtype=jnp.float32) * s, 'b1': jnp.zeros((L, 4 * D), dtype=jnp.float32), 'W2': jax.random.normal(ks[5], (L, 4 * D, D), dtype=jnp.float32) * (1.0 / np.sqrt(4 * D)), 'b2': jnp.zeros((L, D), dtype=jnp.float32), 'g1': jnp.ones((L, D), dtype=jnp.float32), 'beta1': jnp.zeros((L, D), dtype=jnp.float32), 'g2': jnp.ones((L, D), dtype=jnp.float32), 'beta2': jnp.zeros((L, D), dtype=jnp.float32)}
    _L1_gnn_all = _L1_gnn_setup()
    _L1_gnn_in = {k: v for k, v in _L1_gnn_all.items() if k in ('attn_w', 'attn_b', 'W1', 'b1', 'W2', 'b2', 'g1', 'beta1', 'g2', 'beta2')}
    del _L1_gnn_all
    return {'x': x, 'adj': adj, 'L0_gnn_W1': _L0_gnn_in['W1'], 'L0_gnn_att_src1': _L0_gnn_in['att_src1'], 'L0_gnn_att_dst1': _L0_gnn_in['att_dst1'], 'L0_gnn_b1': _L0_gnn_in['b1'], 'L0_gnn_W2': _L0_gnn_in['W2'], 'L0_gnn_att_src2': _L0_gnn_in['att_src2'], 'L0_gnn_att_dst2': _L0_gnn_in['att_dst2'], 'L0_gnn_b2': _L0_gnn_in['b2'], 'L1_gnn_attn_w': _L1_gnn_in['attn_w'], 'L1_gnn_attn_b': _L1_gnn_in['attn_b'], 'L1_gnn_W1': _L1_gnn_in['W1'], 'L1_gnn_b1': _L1_gnn_in['b1'], 'L1_gnn_W2': _L1_gnn_in['W2'], 'L1_gnn_b2': _L1_gnn_in['b2'], 'L1_gnn_g1': _L1_gnn_in['g1'], 'L1_gnn_beta1': _L1_gnn_in['beta1'], 'L1_gnn_g2': _L1_gnn_in['g2'], 'L1_gnn_beta2': _L1_gnn_in['beta2']}

def reference(x, adj, L0_gnn_W1, L0_gnn_att_src1, L0_gnn_att_dst1, L0_gnn_b1, L0_gnn_W2, L0_gnn_att_src2, L0_gnn_att_dst2, L0_gnn_b2, L1_gnn_attn_w, L1_gnn_attn_b, L1_gnn_W1, L1_gnn_b1, L1_gnn_W2, L1_gnn_b2, L1_gnn_g1, L1_gnn_beta1, L1_gnn_g2, L1_gnn_beta2):
    import jax
    import jax.numpy as jnp

    def _L0_gnn_ref(adj, x, W1, att_src1, att_dst1, b1, W2, att_src2, att_dst2, b2):
        import jax, jax.numpy as jnp
        import numpy as np
        NEG_INF = -1000000000.0
        NEG_SLOPE = 0.2

        def gat_layer(x, mask, W, a_src, a_dst, bias, concat):
            B, N, _ = x.shape
            H, F = a_src.shape
            xl = (x @ W).reshape(B, N, H, F)
            asrc = jnp.einsum('bnhf,hf->bnh', xl, a_src)
            adst = jnp.einsum('bnhf,hf->bnh', xl, a_dst)
            e = jax.nn.leaky_relu(asrc[:, :, None, :] + adst[:, None, :, :], NEG_SLOPE)
            e = jnp.where(mask[..., None], e, NEG_INF)
            attn = jax.nn.softmax(e, axis=1)
            out = jnp.einsum('bsdh,bshf->bdhf', attn, xl)
            if concat:
                out = out.reshape(B, N, H * F)
            else:
                out = out.mean(axis=2)
            return out + bias
        B, N, _ = adj.shape
        mask = (adj > 0) | jnp.eye(N, dtype=bool)[None]
        h = jax.nn.elu(gat_layer(x, mask, W1, att_src1, att_dst1, b1, concat=True))
        h = gat_layer(h, mask, W2, att_src2, att_dst2, b2, concat=False)
        return h

    def _L1_gnn_ref(node_features, adjacency_matrix, attn_w, attn_b, W1, b1, W2, b2, g1, beta1, g2, beta2):
        import jax, jax.numpy as jnp
        import numpy as np
        L = 3
        D = 256
        B, N = (8, 512)
        EPS = 1e-05

        def layernorm(x, gamma, beta):
            mu = jnp.mean(x, axis=-1, keepdims=True)
            var = jnp.var(x, axis=-1, keepdims=True)
            return (x - mu) * jax.lax.rsqrt(var + EPS) * gamma + beta
        n = adjacency_matrix.shape[-1]
        mask = adjacency_matrix.astype(jnp.float32) + jnp.eye(n, dtype=jnp.float32) > 0
        x = node_features
        d = x.shape[-1]
        for l in range(attn_w.shape[0]):
            si = x @ attn_w[l, :d]
            sj = x @ attn_w[l, d:]
            scores = si[:, :, None] + sj[:, None, :] + attn_b[l]
            scores = jnp.where(scores >= 0, scores, 0.2 * scores)
            scores = jnp.where(mask, scores, -jnp.inf)
            attn = jax.nn.softmax(scores, axis=-1)
            agg = jnp.einsum('bij,bjd->bid', attn, x)
            h = layernorm(x + agg, g1[l], beta1[l])
            ff = jax.nn.gelu(h @ W1[l] + b1[l], approximate=False) @ W2[l] + b2[l]
            x = layernorm(h + ff, g2[l], beta2[l])
        return x
    x = _layernorm(x + _L0_gnn_ref(adj, x, L0_gnn_W1, L0_gnn_att_src1, L0_gnn_att_dst1, L0_gnn_b1, L0_gnn_W2, L0_gnn_att_src2, L0_gnn_att_dst2, L0_gnn_b2), axis=-1)
    x = _layernorm(x + _L1_gnn_ref(x, adj, L1_gnn_attn_w, L1_gnn_attn_b, L1_gnn_W1, L1_gnn_b1, L1_gnn_W2, L1_gnn_b2, L1_gnn_g1, L1_gnn_beta1, L1_gnn_g2, L1_gnn_beta2), axis=-1)
    return x

_drawn_inputs = setup_inputs


def setup_inputs(seed=0):
    import zlib

    import numpy as np

    out = dict(_drawn_inputs(seed))
    spreads = {'L1_gnn_b1': (0.0, 0.1),
     'L1_gnn_b2': (0.0, 0.1),
     'L1_gnn_g1': (1.0, 0.2),
     'L1_gnn_beta1': (0.0, 0.1),
     'L1_gnn_g2': (1.0, 0.2),
     'L1_gnn_beta2': (0.0, 0.1)}
    factors = {'L0_gnn_att_dst1': 3.144, 'L0_gnn_att_dst2': 19.364, 'L1_gnn_attn_b': 64.0}
    for name, (base, spread) in spreads.items():
        noise = np.random.default_rng([zlib.crc32(name.encode()), seed]).standard_normal(out[name].shape)
        drawn = base * np.exp(spread * noise) if base else spread * noise
        out[name] = jnp.asarray(drawn.astype(out[name].dtype))
    for name, factor in factors.items():
        out[name] = (out[name] * factor).astype(out[name].dtype)
    return out
```

```python
from contextlib import ExitStack

import concourse.bass as bass
from concourse import mybir

F32 = mybir.dt.float32
F32R = mybir.dt.float32r
BF16 = mybir.dt.bfloat16
I32 = mybir.dt.int32
ALU = mybir.AluOpType
ACT = mybir.ActivationFunctionType

P = 128
SLOPE = 0.2
EPS = 1e-5
MASKED = -1e30
LOWEST = -3e38


def graph_kernel(nc: bass.Bass, t):
    B, N, D = t["x"].shape
    HEADS, FH = t["att_src1"].shape
    L = t["attn_w"].shape[0]
    FF = t["ff_b1"].shape[1]
    NB = N // P
    DB = D // P
    FB = FF // P
    WCOLS = t["ff_w"].shape[2]
    W1_COLS = L * DB * FF
    assert FH == P and B % 2 == 0 and HEADS * P == N and t["ff_w"].shape[0] == B

    x1_dram = nc.dram_tensor("x1_scratch", (B, N, D), F32).ap()

    outer = ExitStack()
    with outer:
        def allocator(stack):
            def sb(name, shape, dt=F32):
                return stack.enter_context(nc.sbuf_tensor(name, shape, dt))
            return sb

        sb = allocator(outer)
        w_hi = sb("w_hi", [P, B * WCOLS], F32R)
        w_lo = sb("w_lo", [P, B * WCOLS], F32R)
        ident = sb("ident", [P, P])
        ones = sb("ones", [P, P])
        off_diag = sb("off_diag", [P, P], BF16)
        setup_done = outer.enter_context(nc.semaphore("setup_done"))

        def w1(part, layer, k, c):
            at = (layer * DB + k) * FF + c * P
            return part[:, at:at + P]

        def w2(part, layer, c):
            at = W1_COLS + (layer * FB + c) * D
            return part[:, at:at + D]

        gat_pass(nc, t, x1_dram, allocator, w_hi, w_lo, ident, ones, off_diag, setup_done)
        transformer_pass(nc, t, x1_dram, allocator, w_hi, w_lo, w1, w2, ident, ones, off_diag)


def gat_pass(nc, t, x1_dram, allocator, w_hi, w_lo, ident, ones, off_diag, setup_done):
    B, N, D = t["x"].shape
    HEADS, FH = t["att_src1"].shape
    NB, DB, WCOLS = N // P, D // P, t["ff_w"].shape[2]
    HF = HEADS * FH

    with ExitStack() as ctx:
        sb = allocator(ctx)

        def psum(name, shape, dt=F32):
            return ctx.enter_context(nc.psum_tensor(name, shape, dt))

        def sem(name):
            return ctx.enter_context(nc.semaphore(name))

        wg1 = sb("wg1", [P, DB, HF])
        wg2 = sb("wg2", [P, HEADS, D])
        att1 = sb("att1", [P, 2, HF])
        att2 = sb("att2", [P, 2, D])
        bias1 = sb("bias1", [P, HEADS])
        bias2 = sb("bias2", [P, D])
        v1 = sb("v1", [P, 2, DB, HEADS])
        v1_scrap = sb("v1_scrap", [P, FH])
        xT = sb("xT", [P, DB, N])
        x_in = sb("x_in", [P, NB, D])
        adj_in = sb("adj_in", [P, NB, N], I32)
        maskb = sb("maskb", [P, NB * (N + P)], BF16)
        xl = sb("xl", [P, NB, HF])
        hT = sb("hT", [P, HEADS, N])
        xl2 = sb("xl2", [P, NB, D])
        res = sb("res", [P, NB, D])
        wt = sb("wt_gat", [P, 3, NB, N])
        wt_two = wt[:, 2]
        low = sb("low", [P, 2, N])
        wtT = sb("wtT", [P, NB, N])
        elu_t = sb("elu_t", [P, 2, N])
        w_stage = sb("w_stage", [P, WCOLS])
        dst1 = sb("dst1", [P, NB, HEADS])
        col2 = sb("col2", [P, 2, NB])
        top = sb("top", [P, 3, NB])
        tmp = sb("tmp", [P, 3, NB])
        shift = sb("shift", [P, 3, NB])
        sh_hi = sb("sh_hi", [P, 3, NB])
        sh_lo = sb("sh_lo", [P, 3, NB])
        total = sb("total", [P, 3, NB])
        inv = sb("inv", [P, 3, NB])
        diag = sb("diag", [P, NB, P])
        dot_scrap = sb("dot_scrap", [P, D])
        stats = sb("stats", [P, NB, 6])
        mv = sb("mv", [P, NB, 2])
        var = sb("var", [P, NB])
        rstd = sb("rstd", [P, NB])
        half = sb("half", [P, NB])

        mask = maskb[:, 0:NB * N].rearrange("p (i n) -> p i n", i=NB)
        mask_diag = maskb[:, :].rearrange("p (i n) -> p i n", i=NB)[:, :, 0:P]

        def wt_head(h):
            return wt[:, h % 3]

        ps_turn = psum("ps_turn", [P, 2, N])
        ps_row = psum("ps_row", [P, 2, N])
        ps_acc = psum("ps_acc", [P, 2, N])
        ps_row2 = psum("ps_row2", [P, N])
        ps_dst = psum("ps_dst", [P, N])

        s_const = sem("s_const")
        s_v1 = sem("s_v1")
        s_xT = sem("s_xT")
        s_x = sem("s_x")
        s_adj = sem("s_adj")
        s_wst = sem("s_wst")
        s_wsp = sem("s_wsp")
        s_mask = sem("s_mask")
        s_dst_ps = sem("s_dst_ps")
        s_dst = sem("s_dst")
        s_row = sem("s_row")
        s_xl_ps = sem("s_xl_ps")
        s_xl = sem("s_xl")
        s_top = sem("s_top")
        s_shift = sem("s_shift")
        s_low = sem("s_low")
        s_arg = sem("s_arg")
        s_exp = sem("s_exp")
        s_inv = sem("s_inv")
        s_wt = sem("s_wt")
        s_turn = sem("s_turn")
        s_wtT = sem("s_wtT")
        s_mm = sem("s_mm")
        s_eluexp = sem("s_eluexp")
        s_elum = sem("s_elum")
        s_hT = sem("s_hT")
        s_xl2_ps = sem("s_xl2_ps")
        s_xl2 = sem("s_xl2")
        s_col2 = sem("s_col2")
        s_diag = sem("s_diag")
        s_row2 = sem("s_row2")
        s_top2 = sem("s_top2")
        s_shift2 = sem("s_shift2")
        s_low2 = sem("s_low2")
        s_arg2 = sem("s_arg2")
        s_exp2 = sem("s_exp2")
        s_inv2 = sem("s_inv2")
        s_turn2 = sem("s_turn2")
        s_wtT2 = sem("s_wtT2")
        s_out2 = sem("s_out2")
        s_xb = sem("s_xb")
        s_res = sem("s_res")
        s_stats = sem("s_stats")
        s_mv = sem("s_mv")
        s_var = sem("s_var")
        s_rstd = sem("s_rstd")
        s_x1 = sem("s_x1")
        s_past = sem("s_past")
        s_past_pool = sem("s_past_pool")
        s_store = sem("s_store")

        block = ctx.enter_context(nc.Block())
        N_CONST = 8

        @block.sync
        def _(sp):
            sp.dma_start(wg1[:], t["gat_w1"].rearrange("(k p) n -> p k n", p=P)).then_inc(s_const, 16)
            sp.dma_start(wg2[:], t["gat_w2"].rearrange("(k p) n -> p k n", p=P)).then_inc(s_const, 16)
            for j, name in enumerate(("att_src1", "att_dst1")):
                row = t[name].rearrange("h f -> (h f)")
                sp.dma_start(att1[:, j, :], row.partition_broadcast(P)).then_inc(s_const, 16)
            for j, name in enumerate(("att_src2", "att_dst2")):
                row = t[name].rearrange("h f -> (h f)")
                sp.dma_start(att2[:, j, :], row.partition_broadcast(P)).then_inc(s_const, 16)
            sp.dma_start(bias2[:], t["gat_b2"].partition_broadcast(P)).then_inc(s_const, 16)
            sp.dma_start(bias1[:], t["gat_b1T"]).then_inc(s_const, 16)

            def load(b, again):
                if again:
                    sp.wait_ge(s_xl_ps, NB * b)
                    sp.wait_ge(s_row, HEADS * b)
                sp.dma_start(xT[:], t["xT"][b].rearrange("(k p) n -> p k n", p=P)).then_inc(s_xT, 16)
                if again:
                    sp.wait_ge(s_mask, 2 * b)
                sp.dma_start(adj_in[:], t["adjT"][b].rearrange("(i p) n -> p i n", p=P)).then_inc(s_adj, 16)
                if again:
                    sp.wait_ge(s_wsp, 2 * b)
                sp.dma_start(w_stage[:], t["ff_w"][b]).then_inc(s_wst, 16)

            def finish(b, again):
                if again:
                    sp.wait_ge(s_xb, b)
                sp.dma_start(x_in[:], t["x"][b].rearrange("(i p) n -> p i n", p=P)).then_inc(s_x, 16)

            def store(b):
                sp.wait_ge(s_x1, NB * b + NB)
                sp.dma_start(x1_dram[b].rearrange("(i p) n -> p i n", p=P), res[:]).then_inc(s_store, 16)

            load(0, False)
            finish(0, False)
            load_next = load
            sp.wait_ge(s_xl_ps, NB)
            load_next(1, True)
            with sp.Fori(1, B - 1) as b:
                store(b - 1)
                finish(b, True)
                load_next(b + 1, True)
            store(B - 2)
            finish(B - 1, True)
            store(B - 1)
            sp.wait_ge(s_store, 16 * B)

        @block.gpsimd
        def _(pool):
            nc.gpsimd.memset(ident[:], 0.0).then_inc(setup_done, 1)
            nc.gpsimd.memset(ones[:], 1.0).then_inc(setup_done, 1)
            nc.gpsimd.memset(off_diag[:], 1.0).then_inc(setup_done, 1)
            nc.gpsimd.memset(half[:], -0.5).then_inc(setup_done, 1)
            pool.wait_ge(setup_done, 4)
            nc.gpsimd.affine_select(out=ident[:], in_=ident[:], compare_op=ALU.not_equal, fill=1.0, base=0,
                                    pattern=[[-1, P]], channel_multiplier=1).then_inc(setup_done, 1)
            nc.gpsimd.affine_select(out=off_diag[:], in_=off_diag[:], compare_op=ALU.not_equal, fill=0.0, base=0,
                                    pattern=[[-1, P]], channel_multiplier=1).then_inc(setup_done, 1)
            pool.wait_ge(s_const, 16 * N_CONST)

            def low_of(weights, j, i, slot, ready):
                pool.sem_inc(s_past_pool, 1)
                nc.gpsimd.tensor_scalar(low[:, slot, :], weights[:, i, :], SLOPE, sh_lo[:, j, i:i + 1],
                                        ALU.mult, ALU.add).then_inc(ready, 1)

            def low_head(b, h, first):
                pool.wait_ge(s_shift, 4 * (HEADS * b + h + 1))
                for i in range(NB):
                    if i >= 2:
                        pool.wait_ge(s_arg, NB * (HEADS * b + h) + i - 1)
                    elif h:
                        pool.wait_ge(s_arg, NB * (HEADS * b + h) - 1 + i)
                    elif not first:
                        pool.wait_ge(s_arg2, NB * b - 1 + i)
                    low_of(wt_head(h), h % 2, i, i % 2, s_low)

            def low_two(b):
                pool.wait_ge(s_shift2, 4 * b + 4)
                for i in range(NB):
                    if i >= 2:
                        pool.wait_ge(s_arg2, NB * b + i - 1)
                    else:
                        pool.wait_ge(s_arg, NB * HEADS * (b + 1) - 1 + i)
                    low_of(wt_two, 2, i, i % 2, s_low2)

            def normalise(b, h):
                pool.wait_ge(s_inv, HEADS * b + h + 1)
                pool.sem_inc(s_past_pool, 1)
                for i in range(NB):
                    nc.gpsimd.tensor_scalar(wt_head(h)[:, i, :], wt_head(h)[:, i, :],
                                            inv[:, h % 2, i:i + 1], 1.0, ALU.mult, ALU.mult).then_inc(s_wt, 1)

            def split_weights(b):
                pool.wait_ge(s_wst, 16 * b + 16)
                nc.gpsimd.tensor_copy(w_hi[:, bass.ds(b * WCOLS, WCOLS)], w_stage[:]).then_inc(s_wsp, 1)
                pool.wait_ge(s_wsp, 2 * b + 1)
                nc.gpsimd.tensor_tensor(w_lo[:, bass.ds(b * WCOLS, WCOLS)], w_stage[:],
                                        w_hi[:, bass.ds(b * WCOLS, WCOLS)].bitcast(F32),
                                        ALU.subtract).then_inc(s_wsp, 1)

            def add_bias(b):
                pool.wait_ge(s_x, 16 * b + 16)
                nc.gpsimd.tensor_tensor(res[:], x_in[:], bias2[:].unsqueeze(1).to_broadcast([P, NB, D]),
                                        ALU.add).then_inc(s_xb, 1)

            def inverse_deviation(b):
                pool.wait_ge(s_var, b + 1)
                nc.gpsimd.tensor_tensor(rstd[:], var[:], half[:], ALU.pow).then_inc(s_rstd, 1)

            def turn(b, two, heads, first=False):
                if two:
                    low_two(b - 1)
                if heads:
                    low_head(b, 0, first)
                    normalise(b, 0)
                    low_head(b, 1, first)
                    normalise(b, 1)
                if two:
                    add_bias(b - 1)
                if heads:
                    low_head(b, 2, first)
                if two:
                    inverse_deviation(b - 1)
                if heads:
                    normalise(b, 2)
                    low_head(b, 3, first)
                    normalise(b, 3)
                    split_weights(b)

            turn(0, False, True, first=True)
            turn(1, True, True)
            with pool.Fori(2, B) as b:
                pool.wait_ge(s_store, 16 * (b - 1))
                turn(b, True, True)
            pool.wait_ge(s_store, 16 * (B - 1))
            turn(B, True, False)

        @block.vector
        def _(dve):
            dve.wait_ge(s_const, 16 * N_CONST)
            n = 0
            for j in range(2):
                for k in range(DB):
                    for h in range(HEADS):
                        if n:
                            dve.wait_ge(s_v1, n)
                        nc.vector.tensor_tensor_reduce(
                            out=v1_scrap[:], in0=wg1[:, k, h * FH:(h + 1) * FH], in1=att1[:, j, h * FH:(h + 1) * FH],
                            scale=1.0, scalar=0.0, op0=ALU.mult, op1=ALU.add,
                            accum_out=v1[:, j, k, h:h + 1]).then_inc(s_v1, 1)
                        n += 1
            dve.wait_ge(setup_done, 6)

            def make_mask(b):
                dve.wait_ge(s_adj, 16 * b + 16)
                nc.vector.tensor_scalar(mask, adj_in[:], 0, MASKED, ALU.is_le, ALU.mult).then_inc(s_mask, 1)
                dve.wait_ge(s_mask, 2 * b + 1)
                nc.vector.tensor_tensor(mask_diag, mask_diag, off_diag[:].unsqueeze(1).to_broadcast([P, NB, P]),
                                        ALU.mult).then_inc(s_mask, 1)

            def keep_dst(b):
                dve.wait_ge(s_dst_ps, b + 1)
                nc.vector.tensor_copy(dst1[:], ps_dst[:, 0:NB * HEADS].rearrange("p (i h) -> p i h", i=NB))\
                    .then_inc(s_dst, 1)

            def biased(row, weights, j, i, done):
                nc.vector.tensor_tensor_reduce(out=weights[:, i, :], in0=row, in1=mask[:, i, :], scale=1.0,
                                               scalar=LOWEST, op0=ALU.add, op1=ALU.max,
                                               accum_out=top[:, j, i:i + 1]).then_inc(done, 1)

            def shifts(query, j, sem, at):
                nc.vector.tensor_tensor(tmp[:, j, :], top[:, j, :], query, ALU.add).then_inc(sem, 1)
                dve.wait_ge(sem, at + 1)
                nc.vector.scalar_tensor_tensor(out=shift[:, j, :], in0=tmp[:, j, :], scalar=SLOPE, in1=tmp[:, j, :],
                                               op0=ALU.mult, op1=ALU.max).then_inc(sem, 1)
                dve.wait_ge(sem, at + 2)
                nc.vector.tensor_tensor(sh_hi[:, j, :], query, shift[:, j, :], ALU.subtract).then_inc(sem, 1)
                nc.vector.scalar_tensor_tensor(out=sh_lo[:, j, :], in0=query, scalar=SLOPE, in1=shift[:, j, :],
                                               op0=ALU.mult, op1=ALU.subtract).then_inc(sem, 1)

            def exponents(weights, j, i, slot, done):
                nc.vector.scalar_tensor_tensor(out=weights[:, i, :], in0=weights[:, i, :], scalar=sh_hi[:, j, i:i + 1],
                                               in1=low[:, slot, :], op0=ALU.add, op1=ALU.max).then_inc(done, 1)

            def prepare_head(b, h, first):
                g = HEADS * b + h
                dve.wait_ge(s_row, g + 1)
                if h == 0:
                    dve.wait_ge(s_mask, 2 * b + 2)
                    dve.wait_ge(s_dst, b + 1)
                if h == 0 and not first:
                    dve.wait_ge(s_turn, NB * g)
                elif h == 2 and not first:
                    dve.wait_ge(s_turn2, NB * b)
                elif h == 3:
                    dve.wait_ge(s_turn, NB * (g - 2))
                dve.sem_inc(s_past, 1)
                for i in range(NB):
                    biased(ps_row[:, h % 2, :], wt_head(h), h % 2, i, s_top)
                dve.wait_ge(s_top, NB * g + NB)
                shifts(dst1[:, :, h], h % 2, s_shift, 4 * g)

            def exponents_head(b, h):
                g = HEADS * b + h
                dve.wait_ge(s_shift, 4 * g + 4)
                for i in range(NB):
                    dve.wait_ge(s_low, NB * g + i + 1)
                    exponents(wt_head(h), h % 2, i, i % 2, s_arg)

            def invert_head(b, h):
                g = HEADS * b + h
                dve.wait_ge(s_exp, NB * g + NB)
                nc.vector.reciprocal(inv[:, h % 2, :], total[:, h % 2, :]).then_inc(s_inv, 1)

            def elu(b, h):
                g = HEADS * b + h
                dve.wait_ge(s_eluexp, g + 1)
                nc.vector.tensor_scalar(elu_t[:, h % 2, :], elu_t[:, h % 2, :], 1.0, -1.0, ALU.min, ALU.add)\
                    .then_inc(s_elum, 1)
                dve.wait_ge(s_elum, g + 1)
                nc.vector.scalar_tensor_tensor(out=hT[:, h, :], in0=ps_acc[:, h % 2, :], scalar=bias1[:, h:h + 1],
                                               in1=elu_t[:, h % 2, :], op0=ALU.add, op1=ALU.max).then_inc(s_hT, 1)

            def dots(b):
                for i in range(NB):
                    if i % 2 == 0:
                        dve.wait_ge(s_xl2, 2 * b + i // 2 + 1)
                    for j in range(2):
                        at = 2 * NB * b + 2 * i + j
                        if i or j:
                            dve.wait_ge(s_col2, at)
                        nc.vector.tensor_tensor_reduce(out=dot_scrap[:], in0=xl2[:, i, :], in1=att2[:, j, :], scale=1.0,
                                                       scalar=0.0, op0=ALU.mult, op1=ALU.add,
                                                       accum_out=col2[:, j, i:i + 1]).then_inc(s_col2, 1)
                dve.wait_ge(s_col2, 2 * NB * (b + 1))
                for i in range(NB):
                    nc.vector.tensor_scalar(diag[:, i, :], ident[:], col2[:, 0, i:i + 1], None, ALU.mult)\
                        .then_inc(s_diag, 1)

            def prepare_two(b):
                dve.wait_ge(s_row2, b + 1)
                dve.sem_inc(s_past, 1)
                for i in range(NB):
                    biased(ps_row2[:], wt_two, 2, i, s_top2)
                dve.wait_ge(s_top2, NB * (b + 1))
                shifts(col2[:, 1, :], 2, s_shift2, 4 * b)

            def exponents_two(b):
                dve.wait_ge(s_shift2, 4 * b + 4)
                for i in range(NB):
                    dve.wait_ge(s_low2, NB * b + i + 1)
                    exponents(wt_two, 2, i, i % 2, s_arg2)

            def norm(b):
                dve.wait_ge(s_exp2, NB * (b + 1))
                nc.vector.reciprocal(inv[:, 2, :], total[:, 2, :]).then_inc(s_inv2, 1)
                dve.wait_ge(s_inv2, b + 1)
                dve.wait_ge(s_xb, b + 1)
                for i in range(NB):
                    if i % 2 == 0:
                        dve.wait_ge(s_out2, NB * b + i + 2)
                    nc.vector.scalar_tensor_tensor(out=res[:, i, :], in0=ps_acc[:, i // 2, (i % 2) * D:(i % 2 + 1) * D],
                                                   scalar=inv[:, 2, i:i + 1], in1=res[:, i, :],
                                                   op0=ALU.mult, op1=ALU.add).then_inc(s_res, 1)
                for i in range(NB):
                    dve.wait_ge(s_res, NB * b + i + 1)
                    nc.vector.bn_stats(stats[:, i, :], res[:, i, :]).then_inc(s_stats, 1)
                for i in range(NB):
                    dve.wait_ge(s_stats, NB * b + i + 1)
                    dve.sem_inc(s_past, 1)
                    nc.vector.bn_aggr(mv[:, i, :], stats[:, i, :]).then_inc(s_mv, 1)
                dve.wait_ge(s_mv, NB * (b + 1))
                nc.vector.tensor_scalar(var[:], mv[:, :, 1], EPS, None, ALU.add).then_inc(s_var, 1)

            def norm_end(b):
                dve.wait_ge(s_rstd, b + 1)
                for i in range(NB):
                    nc.vector.tensor_scalar(res[:, i, :], res[:, i, :], mv[:, i, 0:1], rstd[:, i:i + 1],
                                            ALU.subtract, ALU.mult).then_inc(s_x1, 1)

            def turn(b, two, heads, first=False):
                if two:
                    dots(b - 1)
                    prepare_two(b - 1)
                if heads:
                    make_mask(b)
                    keep_dst(b)
                    prepare_head(b, 0, first)
                if two:
                    exponents_two(b - 1)
                if heads:
                    exponents_head(b, 0)
                    prepare_head(b, 1, first)
                    invert_head(b, 0)
                    exponents_head(b, 1)
                    prepare_head(b, 2, first)
                    invert_head(b, 1)
                if two:
                    norm(b - 1)
                if heads:
                    exponents_head(b, 2)
                if two:
                    norm_end(b - 1)
                if heads:
                    prepare_head(b, 3, first)
                    invert_head(b, 2)
                    elu(b, 0)
                    exponents_head(b, 3)
                    elu(b, 1)
                    invert_head(b, 3)
                    elu(b, 2)
                    elu(b, 3)

            turn(0, False, True, first=True)
            with dve.Fori(1, B) as b:
                turn(b, True, True)
            turn(B, True, False)

        @block.scalar
        def _(act):
            act.wait_ge(s_const, 16 * N_CONST)

            def keep_xl(b, first):
                for i in range(NB):
                    act.wait_ge(s_xl_ps, NB * b + i + 1)
                    if i == 0 and not first:
                        act.wait_ge(s_mm, NB * HEADS * b)
                    nc.scalar.copy(xl[:, i, :], ps_acc[:, i % 2, :]).then_inc(s_xl, 1)

            def keep_xl2(b):
                for i in range(2):
                    act.wait_ge(s_xl2_ps, 2 * b + i + 1)
                    nc.scalar.copy(xl2[:, 2 * i:2 * i + 2, :],
                                   ps_acc[:, i, :].rearrange("p (i n) -> p i n", i=2)).then_inc(s_xl2, 1)

            def exp_block(weights, j, i, done):
                nc.scalar.activation(weights[:, i, :], weights[:, i, :], ACT.Exp,
                                     accum_out=total[:, j, i:i + 1]).then_inc(done, 1)

            def exp_head(b, h, i):
                act.wait_ge(s_arg, NB * (HEADS * b + h) + i + 1)
                exp_block(wt_head(h), h % 2, i, s_exp)

            def keep_turned(b, h, i, first):
                g = HEADS * b + h
                act.wait_ge(s_turn, NB * g + i + 1)
                if h:
                    act.wait_ge(s_mm, NB * (g - 1) + i + 1)
                elif not first:
                    act.wait_ge(s_out2, NB * b)
                nc.scalar.copy(wtT[:, i, :], ps_turn[:, i % 2, :]).then_inc(s_wtT, 1)

            def exp_two(b):
                for i in range(NB):
                    act.wait_ge(s_arg2, NB * b + i + 1)
                    exp_block(wt_two, 2, i, s_exp2)

            def keep_turned_two(b, i):
                if i == 0:
                    act.wait_ge(s_mm, NB * HEADS * (b + 1))
                act.wait_ge(s_turn2, NB * b + i + 1)
                nc.scalar.copy(wtT[:, i, :], ps_turn[:, i % 2, :]).then_inc(s_wtT2, 1)

            def elu_exp(b, h, first):
                g = HEADS * b + h
                act.wait_ge(s_mm, NB * (g + 1))
                if h >= 2 or not first:
                    act.wait_ge(s_hT, g - 1)
                nc.scalar.activation(elu_t[:, h % 2, :], ps_acc[:, h % 2, :], ACT.Exp,
                                     bias=bias1[:, h:h + 1]).then_inc(s_eluexp, 1)

            def turn(b, two, heads, first=False):
                if two:
                    keep_xl2(b - 1)
                if heads:
                    keep_xl(b, first)
                if two:
                    exp_two(b - 1)
                if heads:
                    for i in range(NB):
                        exp_head(b, 0, i)
                for i in range(NB):
                    if two:
                        keep_turned_two(b - 1, i)
                    if heads:
                        exp_head(b, 1, i)
                if heads:
                    for h in range(HEADS):
                        for i in range(NB):
                            keep_turned(b, h, i, first)
                            if h + 2 < HEADS:
                                exp_head(b, h + 2, i)
                        elu_exp(b, h, first)

            turn(0, False, True, first=True)
            with act.Fori(1, B) as b:
                turn(b, True, True)
            turn(B, True, False)

        @block.tensor
        def _(pe):
            pe.wait_ge(s_const, 16 * N_CONST)
            pe.wait_ge(s_v1, 2 * DB * HEADS)
            pe.wait_ge(setup_done, 6)

            def dst_terms(b):
                pe.wait_ge(s_xT, 16 * b + 16)
                for i in range(NB):
                    for k in range(DB):
                        mm = nc.tensor.matmul(ps_dst[:, HEADS * i:HEADS * (i + 1)], xT[:, k, i * P:(i + 1) * P],
                                              v1[:, 1, k, :], start=(k == 0), stop=(k == DB - 1))
                mm.then_inc(s_dst_ps, 1)

            def head_row(b, h, first):
                g = HEADS * b + h
                if h >= 2 or not first:
                    pe.wait_ge(s_top, NB * (g - 1))
                for k in range(DB):
                    mm = nc.tensor.matmul(ps_row[:, h % 2, :], v1[:, 0, k, h:h + 1].to_broadcast([P, P]), xT[:, k, :],
                                          start=(k == 0), stop=(k == DB - 1))
                mm.then_inc(s_row, 1)

            def project(b, two):
                for i in range(NB):
                    if i >= 2:
                        pe.wait_ge(s_xl, NB * b + i - 1)
                    elif two:
                        pe.wait_ge(s_xl2, 2 * b - 1 + i)
                    for k in range(DB):
                        mm = nc.tensor.matmul(ps_acc[:, i % 2, :], xT[:, k, i * P:(i + 1) * P], wg1[:, k, :],
                                              start=(k == 0), stop=(k == DB - 1))
                    mm.then_inc(s_xl_ps, 1)

            def project_two(b):
                pe.wait_ge(s_hT, HEADS * (b + 1))
                for i in range(NB):
                    for h in range(HEADS):
                        mm = nc.tensor.matmul(ps_acc[:, i // 2, (i % 2) * D:(i % 2 + 1) * D],
                                              hT[:, h, i * P:(i + 1) * P], wg2[:, h, :],
                                              start=(h == 0), stop=(h == HEADS - 1))
                    if i % 2:
                        mm.then_inc(s_xl2_ps, 1)

            def row_two(b):
                pe.wait_ge(s_diag, NB * (b + 1))
                for i in range(NB):
                    mm = nc.tensor.matmul(ps_row2[:, i * P:(i + 1) * P], ones[:], diag[:, i, :], start=True, stop=True)
                mm.then_inc(s_row2, 1)

            def turn_tile(weights, j, done):
                for i in range(NB):
                    mm = nc.tensor.transpose(ps_turn[:, j % 2, i * P:(i + 1) * P], weights[:, i, j * P:(j + 1) * P],
                                             ident[:])
                mm.then_inc(done, 1)

            def layer_two(b, heads):
                pe.wait_ge(s_exp2, NB * (b + 1))
                for j in range(NB):
                    if j >= 2:
                        pe.wait_ge(s_wtT2, NB * b + j - 1)
                    turn_tile(wt_two, j, s_turn2)
                pe.wait_ge(s_wtT2, NB * (b + 1))
                if heads:
                    pe.wait_ge(s_xl, NB * (b + 2))
                for i in range(NB):
                    for j in range(NB):
                        mm = nc.tensor.matmul(ps_acc[:, i // 2, (i % 2) * D:(i % 2 + 1) * D],
                                              wtT[:, j, i * P:(i + 1) * P], xl2[:, j, :],
                                              start=(j == 0), stop=(j == NB - 1))
                    mm.then_inc(s_out2, 1)

            def head(b, h, two):
                g = HEADS * b + h
                pe.wait_ge(s_wt, NB * (g + 1))

                def turn_j(j):
                    if j >= 2:
                        pe.wait_ge(s_wtT, NB * g + j - 1)
                    elif h:
                        pe.wait_ge(s_wtT, NB * g - 1 + j)
                    turn_tile(wt_head(h), j, s_turn)

                if h == 0:
                    pe.wait_ge(s_xl, NB * (b + 1))
                turn_j(0)
                turn_j(1)
                if h >= 2:
                    pe.wait_ge(s_hT, g - 1)
                elif two:
                    pe.wait_ge(s_res, NB * b - 2 + 2 * h)
                for j in range(NB):
                    pe.wait_ge(s_wtT, NB * g + j + 1)
                    nc.tensor.matmul(ps_acc[:, h % 2, :], xl[:, j, h * FH:(h + 1) * FH], wtT[:, j, :],
                                     start=(j == 0), stop=(j == NB - 1)).then_inc(s_mm, 1)
                    if j + 2 < NB:
                        turn_j(j + 2)

            def turn(b, two, heads, first=False):
                if two:
                    project_two(b - 1)
                if heads:
                    dst_terms(b)
                    head_row(b, 0, first)
                    head_row(b, 1, first)
                if two:
                    row_two(b - 1)
                if heads:
                    project(b, two)
                if two:
                    layer_two(b - 1, heads)
                if heads:
                    for h in range(HEADS):
                        if h == 0:
                            head_row(b, 2, first)
                        head(b, h, two)
                        if h == 0:
                            head_row(b, 3, first)

            turn(0, False, True, first=True)
            with pe.Fori(1, B) as b:
                turn(b, True, True)
            turn(B, True, False)


def transformer_pass(nc, t, x1_dram, allocator, w_hi, w_lo, w1, w2, ident, ones, off_diag):
    B, N, D = t["x"].shape
    L, FF = t["ff_b1"].shape
    NB, DB, FB = N // P, D // P, FF // P
    STEPS = 2 * L
    TURNS = B // 2

    def thread(s):
        return s % 2

    def layer(s):
        return s % STEPS // 2

    with ExitStack() as ctx:
        sb = allocator(ctx)

        def psum(name, shape, dt=F32):
            return ctx.enter_context(nc.psum_tensor(name, shape, dt))

        def sem(name):
            return ctx.enter_context(nc.semaphore(name))

        att_w = sb("att_w", [P, L, 2, D])
        att_b = sb("att_b", [P, L])
        g1r = sb("g1r", [P, L, D])
        b1r = sb("b1r", [P, L, D])
        g2r = sb("g2r", [P, L, D])
        b2r = sb("b2r", [P, L, D])
        g1c = sb("g1c", [P, L * DB])
        b1c = sb("b1c", [P, L * DB])
        ffb = sb("ffb", [P, L * FB])
        x = sb("x_state", [P, 2, NB, D])
        maskb = sb("mask_bias", [P, 2 * NB * N + NB * P], BF16)
        fin = sb("fin", [P, NB, D])
        adj_in = sb("adj_blocks", [P, 2, N], I32)
        wt = sb("wt", [P, NB, N])
        low = sb("low_part", [P, 2, N])
        wtT = sb("wt_turned", [P, NB, N])
        h_hi = sb("h_hi", [P, DB, N], F32R)
        h_lo = sb("h_lo", [P, DB, N], F32R)
        whole = sb("whole", [P, 2, N])
        g_hi = sb("g_hi", [P, FB, N], F32R)
        g_lo = sb("g_lo", [P, FB, N], F32R)
        col = sb("col", [P, 2, 2, NB])
        query = sb("query", [P, NB])
        top = sb("top_q", [P, NB])
        tmp = sb("tmp_q", [P, NB])
        shift = sb("shift_q", [P, NB])
        sh_hi = sb("sh_hi_q", [P, NB])
        sh_lo = sb("sh_lo_q", [P, NB])
        total = sb("total_q", [P, NB])
        inv = sb("inv_q", [P, NB])
        scrap = sb("scrap", [P, D])
        stats = sb("stats_q", [P, 3, NB, 6])
        mv = sb("mv_q", [P, 3, NB, 2])
        var = sb("var_q", [P, 3, NB])
        rstd = sb("rstd_q", [P, 3, NB])
        half = sb("half_q", [P, NB])

        b2_in = wt[:, 0:2, :].rearrange("p i n -> p (i n)")[:, 0:L * D]
        sums = wt[:, 0:2, :].rearrange("p i n -> p (i n)").rearrange("p (i n) -> p i n", i=NB)
        diag = low[:, 0, :].rearrange("p (i n) -> p i n", i=NB)
        mask = [maskb[:, a * NB * N:(a + 1) * NB * N].rearrange("p (i n) -> p i n", i=NB) for a in range(2)]
        mask_diag = [maskb[:, a * NB * N:a * NB * N + NB * (N + P)].rearrange("p (i n) -> p i n", i=NB)[:, :, 0:P]
                     for a in range(2)]

        ps_ff = psum("ps_ff", [P, 2, N])
        ps_y = psum("ps_y", [P, 2, N])
        ps_agg = psum("ps_agg", [P, 2, N])
        ps_turn = psum("ps_turned", [P, 2, N])

        q_const = sem("q_const")
        q_half = sem("q_half")
        q_b1r = sem("q_b1r")
        q_x = [sem(f"q_x{a}") for a in range(2)]
        q_adj = [sem(f"q_adj{i}") for i in range(2)]
        q_fin = sem("q_fin")
        q_mask = sem("q_mask")
        q_dot = sem("q_dot")
        q_diag = sem("q_diag")
        q_query = sem("q_query")
        q_row = sem("q_row")
        q_top = sem("q_top")
        q_shift = sem("q_shift")
        q_low = sem("q_low")
        q_arg = sem("q_arg")
        q_exp = sem("q_exp")
        q_inv = sem("q_inv")
        q_turn = sem("q_turn")
        q_wtT = sem("q_wtT")
        q_agg = sem("q_agg")
        q_r1 = sem("q_r1")
        q_st1 = sem("q_st1")
        q_mv1 = sem("q_mv1")
        q_var1 = sem("q_var1")
        q_rstd1 = sem("q_rstd1")
        q_n1 = sem("q_n1")
        q_nT = sem("q_nT")
        q_whole = sem("q_whole")
        q_hhi = sem("q_hhi")
        q_hlo = sem("q_hlo")
        q_h = sem("q_h")
        q_ff = sem("q_ff")
        q_gelu = sem("q_gelu")
        q_glo = sem("q_glo")
        q_y = sem("q_y")
        q_r2 = sem("q_r2")
        q_st2 = sem("q_st2")
        q_mv2 = sem("q_mv2")
        q_var2 = sem("q_var2")
        q_rstd2 = sem("q_rstd2")
        q_n2 = sem("q_n2")
        q_xn = sem("q_xn")
        q_r3 = sem("q_r3")
        q_st3 = sem("q_st3")
        q_mv3 = sem("q_mv3")
        q_var3 = sem("q_var3")
        q_rstd3 = sem("q_rstd3")
        q_out = sem("q_out")
        q_past = sem("q_past")
        q_past_pool = sem("q_past_pool")
        q_store = sem("q_store")

        block = ctx.enter_context(nc.Block())
        VECTORS = 10

        @block.sync
        def _(sp):
            sp.dma_start(att_w[:].rearrange("p l j d -> p (l j d)"),
                         t["attn_w"].rearrange("l d -> (l d)").partition_broadcast(P)).then_inc(q_const, 16)
            sp.dma_start(att_b[:], t["attn_b"].partition_broadcast(P)).then_inc(q_const, 16)
            for dst, name in ((g1r, "g1"), (b1r, "beta1"), (g2r, "g2"), (b2r, "beta2")):
                sp.dma_start(dst[:].rearrange("p l d -> p (l d)"),
                             t[name].rearrange("l d -> (l d)").partition_broadcast(P)).then_inc(q_const, 16)
            sp.dma_start(b2_in, t["ff_b2"].rearrange("l d -> (l d)").partition_broadcast(P)).then_inc(q_const, 16)
            for dst, name in ((g1c, "g1T"), (b1c, "beta1T"), (ffb, "ff_b1T")):
                sp.dma_start(dst[:], t[name]).then_inc(q_const, 16)

            def load_x(b, a):
                sp.dma_start(x[:, a], x1_dram[b].rearrange("(i p) n -> p i n", p=P)).then_inc(q_x[a], 16)

            def load_adj(b, blocks, first=False):
                for i in blocks:
                    if i >= 2:
                        sp.wait_ge(q_mask, (NB + 1) * b + i - 1)
                    elif not first:
                        sp.wait_ge(q_mask, (NB + 1) * b - 2 + i)
                    sp.dma_start(adj_in[:, i % 2, :], t["adj"][b, i * P:(i + 1) * P, :])\
                        .then_inc(q_adj[i % 2], 16)

            def load_fin(b):
                sp.dma_start(fin[:], x1_dram[b].rearrange("(i p) n -> p i n", p=P)).then_inc(q_fin, 16)

            def store(b):
                sp.wait_ge(q_out, NB * b + NB)
                sp.dma_start(t["out"][b].rearrange("(i p) n -> p i n", p=P), fin[:]).then_inc(q_store, 16)

            def turn(n, last):
                for a in range(2):
                    b = 2 * n + a
                    if not last:
                        load_adj(b + 2, range(0, 2))
                        sp.wait_ge(q_r3, 2 * b + 2)
                        load_x(b + 2, a)
                        load_adj(b + 2, range(2, NB))
                    store(b)
                    if not (last and a):
                        sp.wait_ge(q_store, 16 * (b + 1))
                        load_fin(b + 1)

            load_x(0, 0)
            load_adj(0, range(NB), first=True)
            load_x(1, 1)
            load_adj(1, range(NB))
            load_fin(0)
            with sp.Fori(0, TURNS - 1) as n:
                turn(n, False)
            turn(TURNS - 1, True)
            sp.wait_ge(q_store, 16 * B)

        @block.gpsimd
        def _(pool):
            nc.gpsimd.memset(half[:], -0.5).then_inc(q_half, 1)
            pool.wait_ge(q_half, 1)

            def low_parts(q):
                pool.wait_ge(q_shift, 4 * q + 4)
                for i in range(NB):
                    if i >= 2:
                        pool.wait_ge(q_arg, NB * q + i - 1)
                    pool.sem_inc(q_past_pool, 1)
                    nc.gpsimd.tensor_scalar(low[:, i % 2, :], wt[:, i, :], SLOPE, sh_lo[:, i:i + 1],
                                            ALU.mult, ALU.add).then_inc(q_low, 1)

            def gelu_lo(q, c):
                pool.wait_ge(q_gelu, 2 * (FB * q + c + 1))
                nc.gpsimd.tensor_tensor(g_lo[:, c, :], whole[:, c % 2, :], g_hi[:, c, :].bitcast(F32),
                                        ALU.subtract).then_inc(q_glo, 1)

            def inverse_deviation(which, blocks, ready, value, done):
                pool.wait_ge(ready, value)
                nc.gpsimd.tensor_tensor(rstd[:, which, blocks], var[:, which, blocks], half[:, blocks], ALU.pow)\
                    .then_inc(done, 1)

            def feed_forward_half(q, s, b, f):
                blocks = slice(2 * f, 2 * f + 2)
                inverse_deviation(1, blocks, q_var2, 2 * q + f + 1, q_rstd2)
                if layer(s) == L - 1:
                    inverse_deviation(2, blocks, q_var3, 2 * b + f + 1, q_rstd3)

            def attention_norm(q):
                for f in range(2):
                    inverse_deviation(0, slice(2 * f, 2 * f + 2), q_var1, 2 * q + f + 1, q_rstd1)

            def turn(n, last):
                for s in range(STEPS):
                    q, b = STEPS * n + s, 2 * n + thread(s)
                    more = not (last and s == STEPS - 1)
                    for c in range(FB):
                        gelu_lo(q, c)
                    if more:
                        low_parts(q + 1)
                    feed_forward_half(q, s, b, 0)
                    if more:
                        attention_norm(q + 1)
                    feed_forward_half(q, s, b, 1)

            low_parts(0)
            attention_norm(0)
            with pool.Fori(0, TURNS - 1) as n:
                turn(n, False)
            turn(TURNS - 1, True)

        @block.vector
        def _(dve):
            dve.wait_ge(q_const, 16 * VECTORS)
            nc.vector.tensor_tensor(b1r[:].rearrange("p l d -> p (l d)"), b1r[:].rearrange("p l d -> p (l d)"), b2_in,
                                    ALU.add).then_inc(q_b1r, 1)

            def make_mask(b, a):
                for i in range(NB):
                    dve.wait_ge(q_adj[i % 2], 16 * (NB // 2 * b + i // 2 + 1))
                    nc.vector.tensor_scalar(mask[a][:, i, :], adj_in[:, i % 2, :], 0, MASKED, ALU.is_le, ALU.mult)\
                        .then_inc(q_mask, 1)
                dve.wait_ge(q_mask, (NB + 1) * b + NB)
                nc.vector.tensor_tensor(mask_diag[a], mask_diag[a], off_diag[:].unsqueeze(1).to_broadcast([P, NB, P]),
                                        ALU.mult).then_inc(q_mask, 1)

            def dots(q, s, f):
                a, l = thread(s), layer(s)
                for i in range(2 * f, 2 * f + 2):
                    for j in range(2):
                        at = 2 * NB * q + 2 * i + j
                        if 2 * i + j:
                            dve.wait_ge(q_dot, at)
                        nc.vector.tensor_tensor_reduce(out=scrap[:], in0=x[:, a, i, :], in1=att_w[:, l, j, :], scale=1.0,
                                                       scalar=0.0, op0=ALU.mult, op1=ALU.add,
                                                       accum_out=col[:, a, j, i:i + 1]).then_inc(q_dot, 1)

            def diagonal(q, s):
                a, l = thread(s), layer(s)
                dve.wait_ge(q_dot, 2 * NB * (q + 1))
                for i in range(NB):
                    nc.vector.tensor_scalar(diag[:, i, :], ident[:], col[:, a, 1, i:i + 1], None, ALU.mult)\
                        .then_inc(q_diag, 1)
                nc.vector.tensor_scalar(query[:], col[:, a, 0, :], att_b[:, l:l + 1], None, ALU.add).then_inc(q_query, 1)

            def first_terms(q, s, n):
                a = thread(s)
                b = 2 * n + a
                make_mask(b, a)
                dve.wait_ge(q_x[a], 16 * (n + 1))
                dots(q, s, 0)
                dots(q, s, 1)
                dve.wait_ge(q_mask, (NB + 1) * (b + 1))
                diagonal(q, s)

            def prepare(q, s):
                a = thread(s)
                dve.wait_ge(q_row, q + 1)
                dve.sem_inc(q_past, 1)
                for i in range(NB):
                    nc.vector.tensor_tensor_reduce(out=wt[:, i, :], in0=ps_turn[:, 0, :], in1=mask[a][:, i, :], scale=1.0,
                                                   scalar=LOWEST, op0=ALU.add, op1=ALU.max,
                                                   accum_out=top[:, i:i + 1]).then_inc(q_top, 1)
                dve.wait_ge(q_top, NB * (q + 1))
                dve.wait_ge(q_query, q + 1)
                nc.vector.tensor_tensor(tmp[:], top[:], query[:], ALU.add).then_inc(q_shift, 1)
                dve.wait_ge(q_shift, 4 * q + 1)
                nc.vector.scalar_tensor_tensor(out=shift[:], in0=tmp[:], scalar=SLOPE, in1=tmp[:],
                                               op0=ALU.mult, op1=ALU.max).then_inc(q_shift, 1)
                dve.wait_ge(q_shift, 4 * q + 2)
                nc.vector.scalar_tensor_tensor(out=sh_lo[:], in0=query[:], scalar=SLOPE, in1=shift[:],
                                               op0=ALU.mult, op1=ALU.subtract).then_inc(q_shift, 1)
                nc.vector.tensor_tensor(sh_hi[:], query[:], shift[:], ALU.subtract).then_inc(q_shift, 1)

            def exponents(q):
                dve.wait_ge(q_shift, 4 * q + 4)
                for i in range(NB):
                    dve.wait_ge(q_low, NB * q + i + 1)
                    nc.vector.scalar_tensor_tensor(out=wt[:, i, :], in0=wt[:, i, :], scalar=sh_hi[:, i:i + 1],
                                                   in1=low[:, i % 2, :], op0=ALU.add, op1=ALU.max).then_inc(q_arg, 1)

            def moments(data, which, blocks, before, ready, st, mvs, vs):
                for n, i in enumerate(blocks):
                    dve.wait_ge(ready[0], ready[1](n))
                    nc.vector.bn_stats(stats[:, which, i, :], data[:, i, :]).then_inc(st, 1)
                for n, i in enumerate(blocks):
                    dve.wait_ge(st, before + n + 1)
                    dve.sem_inc(q_past, 1)
                    nc.vector.bn_aggr(mv[:, which, i, :], stats[:, which, i, :]).then_inc(mvs, 1)
                dve.wait_ge(mvs, before + len(blocks))
                cols = slice(blocks[0], blocks[-1] + 1)
                nc.vector.tensor_scalar(var[:, which, cols], mv[:, which, cols, 1], EPS, None, ALU.add).then_inc(vs, 1)

            def scaled(out, which, blocks, done, data=None):
                data = out if data is None else data
                for i in blocks:
                    nc.vector.tensor_scalar(out[:, i, :], data[:, i, :], mv[:, which, i, 0:1], rstd[:, which, i:i + 1],
                                            ALU.subtract, ALU.mult).then_inc(done, 1)

            def attention_residual(q, s):
                a = thread(s)
                dve.wait_ge(q_exp, NB * (q + 1))
                nc.vector.reciprocal(inv[:], total[:]).then_inc(q_inv, 1)
                dve.wait_ge(q_inv, q + 1)
                for f in range(2):
                    blocks = range(2 * f, 2 * f + 2)
                    dve.wait_ge(q_agg, 2 * q + f + 1)
                    for i in blocks:
                        nc.vector.scalar_tensor_tensor(out=sums[:, i, :],
                                                       in0=ps_agg[:, i // 2, (i % 2) * D:(i % 2 + 1) * D],
                                                       scalar=inv[:, i:i + 1], in1=x[:, a, i, :],
                                                       op0=ALU.mult, op1=ALU.add).then_inc(q_r1, 1)
                    moments(sums, 0, blocks, NB * q + 2 * f, (q_r1, lambda n: NB * q + 2 * f + n + 1),
                            q_st1, q_mv1, q_var1)

            def attention_norm(q, s):
                a = thread(s)
                for f in range(2):
                    dve.wait_ge(q_rstd1, 2 * q + f + 1)
                    scaled(x[:, a], 0, range(2 * f, 2 * f + 2), q_n1, sums)

            def h_parts(q, s):
                l = layer(s)
                for k in range(DB):
                    dve.wait_ge(q_nT, DB * q + k + 1)
                    nc.vector.tensor_scalar(whole[:, k, :], ps_turn[:, (k + 1) % 2, :], g1c[:, l * DB + k:l * DB + k + 1],
                                            b1c[:, l * DB + k:l * DB + k + 1], ALU.mult, ALU.add).then_inc(q_whole, 1)
                    dve.wait_ge(q_whole, DB * q + k + 1)
                    dve.wait_ge(q_hhi, DB * q + k + 1)
                    nc.vector.tensor_tensor(h_lo[:, k, :], whole[:, k, :], h_hi[:, k, :].bitcast(F32),
                                            ALU.subtract).then_inc(q_hlo, 1)

            def residual_h(q, s):
                a, l = thread(s), layer(s)
                dve.wait_ge(q_nT, DB * (q + 1))
                nc.vector.tensor_tensor(x[:, a], x[:, a], g1r[:, l:l + 1, :].to_broadcast([P, NB, D]), ALU.mult)\
                    .then_inc(q_h, 1)
                dve.wait_ge(q_h, 2 * q + 1)
                nc.vector.tensor_tensor(x[:, a], x[:, a], b1r[:, l:l + 1, :].to_broadcast([P, NB, D]), ALU.add)\
                    .then_inc(q_h, 1)

            def feed_forward_half(q, s, b, f):
                a, l = thread(s), layer(s)
                blocks = range(2 * f, 2 * f + 2)
                rows = slice(2 * f, 2 * f + 2)
                dve.wait_ge(q_y, 2 * q + f + 1)
                dve.wait_ge(q_h, 2 * q + 2)
                nc.vector.tensor_tensor(x[:, a, rows, :], ps_y[:, f, :].rearrange("p (i n) -> p i n", i=2),
                                        x[:, a, rows, :], ALU.add).then_inc(q_r2, 1)
                moments(x[:, a], 1, blocks, NB * q + 2 * f, (q_r2, lambda n: 2 * q + f + 1), q_st2, q_mv2, q_var2)
                dve.wait_ge(q_rstd2, 2 * q + f + 1)
                scaled(x[:, a], 1, blocks, q_n2)
                dve.wait_ge(q_n2, NB * q + 2 * f + 2)
                nc.vector.tensor_tensor(x[:, a, rows, :], x[:, a, rows, :],
                                        g2r[:, l:l + 1, :].to_broadcast([P, 2, D]), ALU.mult).then_inc(q_xn, 1)
                dve.wait_ge(q_xn, 4 * q + 2 * f + 1)
                nc.vector.tensor_tensor(x[:, a, rows, :], x[:, a, rows, :],
                                        b2r[:, l:l + 1, :].to_broadcast([P, 2, D]), ALU.add).then_inc(q_xn, 1)
                dve.wait_ge(q_xn, 4 * q + 2 * f + 2)
                if l == L - 1:
                    dve.wait_ge(q_fin, 16 * (b + 1))
                    nc.vector.tensor_tensor(fin[:, rows, :], fin[:, rows, :], x[:, a, rows, :], ALU.add).then_inc(q_r3, 1)
                    moments(fin, 2, blocks, NB * b + 2 * f, (q_r3, lambda n: 2 * b + f + 1), q_st3, q_mv3, q_var3)
                    dve.wait_ge(q_rstd3, 2 * b + f + 1)
                    scaled(fin, 2, blocks, q_out)

            def turn(n, last):
                for s in range(STEPS):
                    q, b = STEPS * n + s, 2 * n + thread(s)
                    more = not (last and s == STEPS - 1)
                    again = layer(s) < L - 1
                    if more:
                        prepare(q + 1, s + 1)
                        exponents(q + 1)
                    feed_forward_half(q, s, b, 0)
                    if again:
                        dots(q + 2, s + 2, 0)
                    if more:
                        attention_residual(q + 1, s + 1)
                        attention_norm(q + 1, s + 1)
                        h_parts(q + 1, s + 1)
                    feed_forward_half(q, s, b, 1)
                    if again:
                        dots(q + 2, s + 2, 1)
                        diagonal(q + 2, s + 2)
                    elif not last:
                        first_terms(q + 2, s + 2, n + 1)
                    if more:
                        residual_h(q + 1, s + 1)

            first_terms(0, 0, 0)
            prepare(0, 0)
            exponents(0)
            attention_residual(0, 0)
            attention_norm(0, 0)
            h_parts(0, 0)
            first_terms(1, 1, 0)
            dve.wait_ge(q_b1r, 1)
            residual_h(0, 0)
            with dve.Fori(0, TURNS - 1) as n:
                turn(n, False)
            turn(TURNS - 1, True)

        @block.scalar
        def _(act):
            act.wait_ge(q_const, 16 * VECTORS)

            def exps(q):
                for i in range(NB):
                    act.wait_ge(q_arg, NB * q + i + 1)
                    nc.scalar.activation(wt[:, i, :], wt[:, i, :], ACT.Exp, accum_out=total[:, i:i + 1]).then_inc(q_exp, 1)

            def keep_turned(q):
                for j in range(NB):
                    act.wait_ge(q_turn, NB * q + j + 1)
                    nc.scalar.copy(wtT[:, j, :], ps_turn[:, (j + 1) % 2, :]).then_inc(q_wtT, 1)

            def keep_h(q):
                for k in range(DB):
                    act.wait_ge(q_whole, DB * q + k + 1)
                    nc.scalar.copy(h_hi[:, k, :], whole[:, k, :]).then_inc(q_hhi, 1)

            def gelu(q, s, c):
                l = layer(s)
                act.wait_ge(q_ff, FB * q + c + 1)
                if c >= 2:
                    act.wait_ge(q_glo, FB * q + c - 1)
                for out in (whole[:, c % 2, :], g_hi[:, c, :]):
                    nc.scalar.activation(out, ps_ff[:, c % 2, :], ACT.Gelu,
                                         bias=ffb[:, l * FB + c:l * FB + c + 1]).then_inc(q_gelu, 1)

            def turn(n, last):
                for s in range(STEPS):
                    q = STEPS * n + s
                    for c in range(FB):
                        gelu(q, s, c)
                    if not (last and s == STEPS - 1):
                        exps(q + 1)
                        keep_turned(q + 1)
                        keep_h(q + 1)

            exps(0)
            keep_turned(0)
            keep_h(0)
            with act.Fori(0, TURNS - 1) as n:
                turn(n, False)
            turn(TURNS - 1, True)

        @block.tensor
        def _(pe):
            def key_row(q):
                pe.wait_ge(q_diag, NB * (q + 1))
                for i in range(NB):
                    mm = nc.tensor.matmul(ps_turn[:, 0, i * P:(i + 1) * P], ones[:], diag[:, i, :], start=True, stop=True)
                mm.then_inc(q_row, 1)

            def attend(q, s):
                a = thread(s)
                pe.wait_ge(q_exp, NB * (q + 1))
                for j in range(NB):
                    if j >= 2:
                        pe.wait_ge(q_wtT, NB * q + j - 1)
                    for i in range(NB):
                        mm = nc.tensor.transpose(ps_turn[:, (j + 1) % 2, i * P:(i + 1) * P], wt[:, i, j * P:(j + 1) * P],
                                                 ident[:])
                    mm.then_inc(q_turn, 1)
                pe.wait_ge(q_wtT, NB * (q + 1))
                for i in range(NB):
                    for j in range(NB):
                        mm = nc.tensor.matmul(ps_agg[:, i // 2, (i % 2) * D:(i % 2 + 1) * D],
                                              wtT[:, j, i * P:(i + 1) * P], x[:, a, j, :],
                                              start=(j == 0), stop=(j == NB - 1))
                    if i % 2:
                        mm.then_inc(q_agg, 1)

            def turn_n(q, s):
                a = thread(s)
                pe.wait_ge(q_n1, NB * (q + 1))
                for k in range(DB):
                    for i in range(NB):
                        mm = nc.tensor.transpose(ps_turn[:, (k + 1) % 2, i * P:(i + 1) * P], x[:, a, i, k * P:(k + 1) * P],
                                                 ident[:])
                    mm.then_inc(q_nT, 1)

            def first_product(q, s, c):
                l = layer(s)
                if c >= 2:
                    pe.wait_ge(q_gelu, 2 * (FB * q + c - 1))
                for k in range(DB):
                    if c == 0:
                        pe.wait_ge(q_hhi, DB * q + k + 1)
                    for w in (w_hi, w_lo):
                        nc.tensor.matmul(ps_ff[:, c % 2, :], w1(w, l, k, c), h_hi[:, k, :],
                                         start=(k == 0 and w is w_hi), stop=False)
                for k in range(DB):
                    if c == 0:
                        pe.wait_ge(q_hlo, DB * q + k + 1)
                    mm = nc.tensor.matmul(ps_ff[:, c % 2, :], w1(w_hi, l, k, c), h_lo[:, k, :],
                                          start=False, stop=(k == DB - 1))
                mm.then_inc(q_ff, 1)

            def second_product(q, s, f):
                l = layer(s)
                for i in range(2 * f, 2 * f + 2):
                    for c in range(FB):
                        if i == 0:
                            pe.wait_ge(q_glo, FB * q + c + 1)
                        for n, (g, w) in enumerate([(g_hi, w_hi), (g_hi, w_lo), (g_lo, w_hi)]):
                            mm = nc.tensor.matmul(ps_y[:, f, (i % 2) * D:(i % 2 + 1) * D],
                                                  g[:, c, i * P:(i + 1) * P], w2(w, l, c),
                                                  start=(c == 0 and n == 0), stop=(c == FB - 1 and n == 2))
                mm.then_inc(q_y, 1)

            def turn(n, last):
                for s in range(STEPS):
                    q = STEPS * n + s
                    more = not (last and s == STEPS - 1)
                    for c in range(FB):
                        if c == FB - 2 and more:
                            key_row(q + 1)
                        first_product(q, s, c)
                    second_product(q, s, 0)
                    if more:
                        attend(q + 1, s + 1)
                    second_product(q, s, 1)
                    if more:
                        turn_n(q + 1, s + 1)

            key_row(0)
            attend(0, 0)
            turn_n(0, 0)
            with pe.Fori(0, TURNS - 1) as n:
                turn(n, False)
            turn(TURNS - 1, True)


_INS = ("x", "xT", "adj", "adjT", "gat_w1", "att_src1", "att_dst1", "gat_b1T", "gat_w2", "att_src2", "att_dst2",
        "gat_b2", "attn_w", "attn_b", "ff_w", "ff_b1", "ff_b1T", "ff_b2", "g1", "beta1", "g1T", "beta1T", "g2", "beta2")


def layouts(a):
    import numpy as np
    L, D = a["L1_gnn_g1"].shape
    B = a["x"].shape[0]
    heads = a["L0_gnn_att_src1"].shape[0]
    FF = a["L1_gnn_b1"].shape[1]

    def on_partitions(v):
        v = v.reshape(v.shape[:-1] + (-1, P))
        return v.reshape(-1, P).T

    w1 = a["L1_gnn_W1"].reshape(L, D // P, P, FF).transpose(2, 0, 1, 3).reshape(P, -1)
    w2 = a["L1_gnn_W2"].reshape(L, FF // P, P, D).transpose(2, 0, 1, 3).reshape(P, -1)
    ff_w = np.concatenate([w1, w2], axis=1).reshape(P, B, -1).transpose(1, 0, 2)
    return {
        "x": a["x"], "xT": a["x"].transpose(0, 2, 1), "adj": a["adj"], "adjT": a["adj"].transpose(0, 2, 1),
        "gat_w1": a["L0_gnn_W1"], "att_src1": a["L0_gnn_att_src1"], "att_dst1": a["L0_gnn_att_dst1"],
        "gat_b1T": on_partitions(a["L0_gnn_b1"]), "gat_w2": a["L0_gnn_W2"],
        "att_src2": a["L0_gnn_att_src2"], "att_dst2": a["L0_gnn_att_dst2"], "gat_b2": a["L0_gnn_b2"],
        "attn_w": a["L1_gnn_attn_w"], "attn_b": a["L1_gnn_attn_b"], "ff_w": ff_w,
        "ff_b1": a["L1_gnn_b1"], "ff_b1T": on_partitions(a["L1_gnn_b1"]), "ff_b2": a["L1_gnn_b2"],
        "g1": a["L1_gnn_g1"], "beta1": a["L1_gnn_beta1"], "g1T": on_partitions(a["L1_gnn_g1"]),
        "beta1T": on_partitions(a["L1_gnn_beta1"]), "g2": a["L1_gnn_g2"], "beta2": a["L1_gnn_beta2"],
    }


def kernel(**inputs):
    import numpy as np
    import concourse.bacc as bacc
    from concourse.bass_utils import run_bass_kernel_spmd

    nc = bacc.Bacc("TRN2", target_bir_lowering=False, num_devices=1)
    arrays, tensors = {}, {}
    laid_out = layouts({k: np.asarray(v) for k, v in inputs.items()})
    for name in _INS:
        a = np.ascontiguousarray(laid_out[name])
        arrays["in_" + name] = a
        tensors[name] = nc.dram_tensor("in_" + name, a.shape, mybir.dt.from_np(a.dtype), kind="ExternalInput").ap()
    shape = laid_out["x"].shape
    tensors["out"] = nc.dram_tensor("out_0", shape, F32, kind="ExternalOutput").ap()
    graph_kernel(nc, tensors)
    r = run_bass_kernel_spmd(nc, [arrays], core_ids=[0])
    return r.results[0]["out_0"]
```

```python
from contextlib import ExitStack

import concourse.bass as bass
from concourse import mybir

F32 = mybir.dt.float32
F32R = mybir.dt.float32r
BF16 = mybir.dt.bfloat16
I32 = mybir.dt.int32
ALU = mybir.AluOpType
ACT = mybir.ActivationFunctionType

P = 128
SLOPE = 0.2
EPS = 1e-5
MASKED = -1e30
LOWEST = -3e38


def graph_kernel(nc: bass.Bass, t):
    B, N, D = t["x"].shape
    HEADS, FH = t["att_src1"].shape
    L = t["attn_w"].shape[0]
    FF = t["ff_b1"].shape[1]
    NB = N // P
    DB = D // P
    FB = FF // P
    WCOLS = t["ff_w"].shape[2]
    W1_COLS = L * DB * FF
    assert FH == P and B % 2 == 0 and HEADS * P == N and t["ff_w"].shape[0] == B

    x1_dram = nc.dram_tensor("x1_scratch", (B, N, D), F32).ap()

    outer = ExitStack()
    with outer:
        def allocator(stack):
            def sb(name, shape, dt=F32):
                return stack.enter_context(nc.sbuf_tensor(name, shape, dt))
            return sb

        sb = allocator(outer)
        w_hi = sb("w_hi", [P, B * WCOLS], F32R)
        w_lo = sb("w_lo", [P, B * WCOLS], F32R)
        ident = sb("ident", [P, P])
        ones = sb("ones", [P, P])
        off_diag = sb("off_diag", [P, P], BF16)
        setup_done = outer.enter_context(nc.semaphore("setup_done"))

        def w1(part, layer, k, c):
            at = (layer * DB + k) * FF + c * P
            return part[:, at:at + P]

        def w2(part, layer, c):
            at = W1_COLS + (layer * FB + c) * D
            return part[:, at:at + D]

        gat_pass(nc, t, x1_dram, allocator, w_hi, w_lo, ident, ones, off_diag, setup_done)
        transformer_pass(nc, t, x1_dram, allocator, w_hi, w_lo, w1, w2, ident, ones, off_diag)


def gat_pass(nc, t, x1_dram, allocator, w_hi, w_lo, ident, ones, off_diag, setup_done):
    B, N, D = t["x"].shape
    HEADS, FH = t["att_src1"].shape
    NB, DB, WCOLS = N // P, D // P, t["ff_w"].shape[2]
    HF = HEADS * FH
    LO_AT = 32

    with ExitStack() as ctx:
        sb = allocator(ctx)

        def psum(name, shape, dt=F32):
            return ctx.enter_context(nc.psum_tensor(name, shape, dt))

        def sem(name):
            return ctx.enter_context(nc.semaphore(name))

        wg1 = sb("wg1", [P, DB, HF])
        wg2 = sb("wg2", [P, HEADS, D + 2])
        att1 = sb("att1", [P, 2, HF])
        att2 = sb("att2", [P, 2, D])
        bias1 = sb("bias1", [P, HEADS])
        bias2 = sb("bias2", [P, D])
        v1 = sb("v1", [P, 2, DB, HEADS])
        scrap = sb("scrap_gat", [P, D])
        pick = sb("pick", [LO_AT + HEADS, HEADS], F32R)
        xT = sb("xT", [P, DB, N])
        x_in = sb("x_in", [P, NB, D])
        adj_in = sb("adj_in", [P, 2, N], I32)
        maskb = sb("maskb", [P, 2 * NB * N + NB * P], BF16)
        source = sb("source", [LO_AT + HEADS, N], F32R)
        xl = sb("xl", [P, NB, HF])
        hT = sb("hT", [P, HEADS, N])
        xl2 = sb("xl2", [P, NB, D + 2])
        res = sb("res", [P, NB, D])
        wt = sb("wt_gat", [P, 3, NB, N])
        wt_two = wt[:, 1]
        low = sb("low", [P, 2, N])
        wtT = sb("wtT", [P, NB, N])
        elu_t = sb("elu_t", [P, 2, N])
        w_stage = sb("w_stage", [P, WCOLS])
        dst1 = sb("dst1", [P, NB, HEADS])
        top = sb("top", [P, 3, NB])
        tmp = sb("tmp", [P, 3, NB])
        shift = sb("shift", [P, 3, NB])
        sh_hi = sb("sh_hi", [P, 3, NB])
        sh_lo = sb("sh_lo", [P, 3, NB])
        total = sb("total", [P, 3, NB])
        inv = sb("inv", [P, 3, NB])
        stats = sb("stats", [P, NB, 6])
        mv = sb("mv", [P, NB, 2])
        var = sb("var", [P, NB])
        rstd = sb("rstd", [P, NB])
        half = sb("half", [P, NB])

        mask = [maskb[:, a * NB * N:(a + 1) * NB * N].rearrange("p (i n) -> p i n", i=NB) for a in range(2)]
        mask_diag = [maskb[:, a * NB * N:a * NB * N + NB * (N + P)].rearrange("p (i n) -> p i n", i=NB)[:, :, 0:P]
                     for a in range(2)]

        def wt_head(h):
            return wt[:, (0, 2, 0, 1)[h]]

        ps_turn = psum("ps_turn", [P, 2, N])
        ps_row = psum("ps_row", [P, 2, N])
        ps_acc = psum("ps_acc", [P, 2, N])
        ps_two = psum("ps_two", [P, 2, N])
        ps_row2 = ps_two[:, 0]
        ps_dst = ps_two[:, 1, 0:NB * HEADS]

        s_const = sem("s_const")
        s_v = sem("s_v")
        s_zero = sem("s_zero")
        s_xT = sem("s_xT")
        s_x = sem("s_x")
        s_adj = [sem(f"s_adj{i}") for i in range(2)]
        s_wst = sem("s_wst")
        s_wsp = sem("s_wsp")
        s_mask = sem("s_mask")
        s_dst_ps = sem("s_dst_ps")
        s_dst = sem("s_dst")
        s_src_ps = sem("s_src_ps")
        s_src_hi = sem("s_src_hi")
        s_src_lo = sem("s_src_lo")
        s_row = sem("s_row")
        s_xl_ps = sem("s_xl_ps")
        s_xl = sem("s_xl")
        s_top = sem("s_top")
        s_shift = sem("s_shift")
        s_low = sem("s_low")
        s_arg = sem("s_arg")
        s_exp = sem("s_exp")
        s_inv = sem("s_inv")
        s_wt = sem("s_wt")
        s_turn = sem("s_turn")
        s_wtT = sem("s_wtT")
        s_mm = sem("s_mm")
        s_eluexp = sem("s_eluexp")
        s_elum = sem("s_elum")
        s_hT = sem("s_hT")
        s_xl2_ps = sem("s_xl2_ps")
        s_xl2 = sem("s_xl2")
        s_row2 = sem("s_row2")
        s_top2 = sem("s_top2")
        s_shift2 = sem("s_shift2")
        s_low2 = sem("s_low2")
        s_arg2 = sem("s_arg2")
        s_exp2 = sem("s_exp2")
        s_inv2 = sem("s_inv2")
        s_turn2 = sem("s_turn2")
        s_wtT2 = sem("s_wtT2")
        s_out2 = sem("s_out2")
        s_xb = sem("s_xb")
        s_res = sem("s_res")
        s_stats = sem("s_stats")
        s_mv = sem("s_mv")
        s_var = sem("s_var")
        s_rstd = sem("s_rstd")
        s_x1 = sem("s_x1")
        s_past = sem("s_past")
        s_past_pool = sem("s_past_pool")
        s_store = sem("s_store")

        block = ctx.enter_context(nc.Block())
        N_CONST = 8
        N_V = 2 * (DB * HEADS + HEADS)
        FIRST, LAST = dict(two=False, heads=True, more=True), dict(two=True, heads=True, more=False)
        INNER, END = dict(two=True, heads=True, more=True), dict(two=True, heads=False, more=False)

        def turns(engine, turn):
            turn(0, 0, **FIRST)
            with engine.Fori(0, B // 2 - 1) as m:
                for a in (1, 0):
                    turn(2 * m + 2 - a, a, **INNER)
            turn(B - 1, 1, **LAST)
            turn(B, 0, **END)

        @block.sync
        def _(sp):
            def load_xT(b):
                sp.dma_start(xT[:], t["xT"][b].rearrange("(k p) n -> p k n", p=P)).then_inc(s_xT, 16)

            def load_adj(b, blocks, first=False):
                for i in blocks:
                    if i >= 2:
                        sp.wait_ge(s_mask, (NB + 1) * b + i - 1)
                    elif not first:
                        sp.wait_ge(s_mask, (NB + 1) * b - 2 + i)
                    sp.dma_start(adj_in[:, i % 2, :], t["adjT"][b, i * P:(i + 1) * P, :]).then_inc(s_adj[i % 2], 16)

            sp.dma_start(wg1[:], t["gat_w1"].rearrange("(k p) n -> p k n", p=P)).then_inc(s_const, 16)
            for j, name in enumerate(("att_src1", "att_dst1")):
                row = t[name].rearrange("h f -> (h f)")
                sp.dma_start(att1[:, j, :], row.partition_broadcast(P)).then_inc(s_const, 16)
            sp.dma_start(wg2[:, :, 0:D], t["gat_w2"].rearrange("(k p) n -> p k n", p=P)).then_inc(s_const, 16)
            for j, name in enumerate(("att_dst2", "att_src2")):
                row = t[name].rearrange("h f -> (h f)")
                sp.dma_start(att2[:, j, :], row.partition_broadcast(P)).then_inc(s_const, 16)
            sp.dma_start(bias2[:], t["gat_b2"].partition_broadcast(P)).then_inc(s_const, 16)
            sp.dma_start(bias1[:], t["gat_b1T"]).then_inc(s_const, 16)
            load_xT(0)
            load_adj(0, range(NB), first=True)

            def turn(b, a, two, heads, more):
                if more:
                    load_adj(b + 1, range(0, 2))
                if more:
                    sp.wait_ge(s_xl_ps, NB * b + NB)
                    load_xT(b + 1)
                if heads:
                    if two:
                        sp.wait_ge(s_xb, b)
                    sp.dma_start(x_in[:], t["x"][b].rearrange("(i p) n -> p i n", p=P)).then_inc(s_x, 16)
                    if two:
                        sp.wait_ge(s_wsp, 2 * b)
                    sp.dma_start(w_stage[:], t["ff_w"][b]).then_inc(s_wst, 16)
                if more:
                    load_adj(b + 1, range(2, NB))
                if two:
                    sp.wait_ge(s_x1, NB * b)
                    sp.dma_start(x1_dram[b - 1].rearrange("(i p) n -> p i n", p=P), res[:]).then_inc(s_store, 16)

            turns(sp, turn)
            sp.wait_ge(s_store, 16 * B)

        @block.gpsimd
        def _(pool):
            nc.gpsimd.memset(ident[:], 0.0).then_inc(setup_done, 1)
            nc.gpsimd.memset(ones[:], 1.0).then_inc(setup_done, 1)
            nc.gpsimd.memset(off_diag[:], 1.0).then_inc(setup_done, 1)
            nc.gpsimd.memset(half[:], -0.5).then_inc(setup_done, 1)
            pool.wait_ge(setup_done, 4)
            nc.gpsimd.affine_select(out=ident[:], in_=ident[:], compare_op=ALU.not_equal, fill=1.0, base=0,
                                    pattern=[[-1, P]], channel_multiplier=1).then_inc(setup_done, 1)
            nc.gpsimd.affine_select(out=off_diag[:], in_=off_diag[:], compare_op=ALU.not_equal, fill=0.0, base=0,
                                    pattern=[[-1, P]], channel_multiplier=1).then_inc(setup_done, 1)
            pool.wait_ge(s_const, 16 * N_CONST)

            def low_of(weights, j, i, slot, ready):
                pool.sem_inc(s_past_pool, 1)
                nc.gpsimd.tensor_scalar(low[:, slot, :], weights[:, i, :], SLOPE, sh_lo[:, j, i:i + 1],
                                        ALU.mult, ALU.add).then_inc(ready, 1)

            def low_head(b, h, two, first=False):
                g = HEADS * b + h
                pool.wait_ge(s_shift, 4 * g + 4)
                for i in range(NB):
                    if i >= 2:
                        pool.wait_ge(s_arg, NB * g + i - 1)
                    elif h == 2 and two:
                        pool.wait_ge(s_arg2, NB * b - 1 + i)
                    elif not first:
                        pool.wait_ge(s_arg, NB * g - 1 + i)
                    low_of(wt_head(h), h % 2, i, i % 2, s_low)

            def low_two(b, heads):
                pool.wait_ge(s_shift2, 4 * b + 4)
                for i in range(NB):
                    if i >= 2:
                        pool.wait_ge(s_arg2, NB * b + i - 1)
                    elif heads:
                        pool.wait_ge(s_arg, NB * (HEADS * (b + 1) + 2) - 1 + i)
                    low_of(wt_two, 2, i, i % 2, s_low2)

            def normalise(b, h):
                pool.wait_ge(s_inv, HEADS * b + h + 1)
                pool.sem_inc(s_past_pool, 1)
                for i in range(NB):
                    nc.gpsimd.tensor_scalar(wt_head(h)[:, i, :], wt_head(h)[:, i, :],
                                            inv[:, h % 2, i:i + 1], 1.0, ALU.mult, ALU.mult).then_inc(s_wt, 1)

            def split_weights(b):
                pool.wait_ge(s_wst, 16 * b + 16)
                nc.gpsimd.tensor_copy(w_hi[:, bass.ds(b * WCOLS, WCOLS)], w_stage[:]).then_inc(s_wsp, 1)
                pool.wait_ge(s_wsp, 2 * b + 1)
                nc.gpsimd.tensor_tensor(w_lo[:, bass.ds(b * WCOLS, WCOLS)], w_stage[:],
                                        w_hi[:, bass.ds(b * WCOLS, WCOLS)].bitcast(F32),
                                        ALU.subtract).then_inc(s_wsp, 1)

            def add_bias(b):
                pool.wait_ge(s_x, 16 * b + 16)
                nc.gpsimd.tensor_tensor(res[:], x_in[:], bias2[:].unsqueeze(1).to_broadcast([P, NB, D]),
                                        ALU.add).then_inc(s_xb, 1)

            def inverse_deviation(b):
                pool.wait_ge(s_var, b + 1)
                nc.gpsimd.tensor_tensor(rstd[:], var[:], half[:], ALU.pow).then_inc(s_rstd, 1)

            def turn(b, a, two, heads, more, stored=True):
                if heads:
                    normalise(b, 0)
                    low_head(b, 1, two)
                if two:
                    low_two(b - 1, heads)
                if heads:
                    normalise(b, 1)
                    low_head(b, 2, two)
                if two:
                    if stored:
                        pool.wait_ge(s_store, 16 * (b - 1))
                    add_bias(b - 1)
                if heads:
                    low_head(b, 3, two)
                    normalise(b, 2)
                if two:
                    inverse_deviation(b - 1)
                if heads:
                    normalise(b, 3)
                    split_weights(b)
                if more:
                    low_head(b + 1, 0, two)

            low_head(0, 0, False, first=True)
            turn(0, 0, **FIRST)
            turn(1, 1, **INNER, stored=False)
            with pool.Fori(2, B - 1) as b:
                turn(b, 0, **INNER)
            turn(B - 1, 1, **LAST)
            turn(B, 0, **END)

        @block.vector
        def _(dve):
            nc.vector.memset(source[:].bitcast(F32), 0.0).then_inc(s_zero, 1)
            nc.vector.memset(pick[:].bitcast(F32), 0.0).then_inc(s_zero, 1)
            dve.wait_ge(setup_done, 6)
            dve.wait_ge(s_zero, 2)
            for at in (0, LO_AT):
                nc.vector.tensor_copy(pick[at:at + HEADS, :], ident[at:at + HEADS, at:at + HEADS]).then_inc(s_zero, 1)
            dve.wait_ge(s_const, 16 * N_CONST)
            n = 0
            for j in range(2):
                for h in range(HEADS):
                    products = [(v1[:, j, k, h:h + 1], wg1[:, k, h * FH:(h + 1) * FH], att1[:, j, h * FH:(h + 1) * FH])
                                for k in range(DB)]
                    products += [(wg2[:, h, D + j:D + j + 1], wg2[:, h, 0:D], att2[:, j, :])]
                    for out, weights, att in products:
                        if n:
                            dve.wait_ge(s_v, n)
                        nc.vector.tensor_tensor_reduce(out=scrap[:, 0:att.shape[-1]], in0=weights, in1=att, scale=1.0,
                                                       scalar=0.0, op0=ALU.mult, op1=ALU.add,
                                                       accum_out=out).then_inc(s_v, 1)
                        n += 1

            def make_mask(b, a):
                for i in range(NB):
                    dve.wait_ge(s_adj[i % 2], 16 * (NB // 2 * b + i // 2 + 1))
                    nc.vector.tensor_scalar(mask[a][:, i, :], adj_in[:, i % 2, :], 0, MASKED, ALU.is_le, ALU.mult)\
                        .then_inc(s_mask, 1)

            def clear_diagonal(b, a):
                dve.wait_ge(s_mask, (NB + 1) * b + NB)
                nc.vector.tensor_tensor(mask_diag[a], mask_diag[a], off_diag[:].unsqueeze(1).to_broadcast([P, NB, P]),
                                        ALU.mult).then_inc(s_mask, 1)

            def keep_terms(b):
                dve.wait_ge(s_dst_ps, b + 1)
                nc.vector.tensor_copy(dst1[:], ps_dst.rearrange("p (i h) -> p i h", i=NB)).then_inc(s_dst, 1)
                dve.wait_ge(s_src_hi, b + 1)
                nc.vector.tensor_tensor(source[LO_AT:LO_AT + HEADS, :], ps_row[0:HEADS, 0, :],
                                        source[0:HEADS, :].bitcast(F32), ALU.subtract).then_inc(s_src_lo, 1)

            def biased(row, weights, j, a, i, done):
                nc.vector.tensor_tensor_reduce(out=weights[:, i, :], in0=row, in1=mask[a][:, i, :], scale=1.0,
                                               scalar=LOWEST, op0=ALU.add, op1=ALU.max,
                                               accum_out=top[:, j, i:i + 1]).then_inc(done, 1)

            def shifts(query, j, sem, at):
                nc.vector.tensor_tensor(tmp[:, j, :], top[:, j, :], query, ALU.add).then_inc(sem, 1)
                dve.wait_ge(sem, at + 1)
                nc.vector.scalar_tensor_tensor(out=shift[:, j, :], in0=tmp[:, j, :], scalar=SLOPE, in1=tmp[:, j, :],
                                               op0=ALU.mult, op1=ALU.max).then_inc(sem, 1)
                dve.wait_ge(sem, at + 2)
                nc.vector.scalar_tensor_tensor(out=sh_lo[:, j, :], in0=query, scalar=SLOPE, in1=shift[:, j, :],
                                               op0=ALU.mult, op1=ALU.subtract).then_inc(sem, 1)
                nc.vector.tensor_tensor(sh_hi[:, j, :], query, shift[:, j, :], ALU.subtract).then_inc(sem, 1)

            def exponents(weights, j, i, slot, done):
                nc.vector.scalar_tensor_tensor(out=weights[:, i, :], in0=weights[:, i, :], scalar=sh_hi[:, j, i:i + 1],
                                               in1=low[:, slot, :], op0=ALU.add, op1=ALU.max).then_inc(done, 1)

            def prepare_head(b, a, h, two, first=False):
                g = HEADS * b + h
                dve.wait_ge(s_row, g + 1)
                if h == 0:
                    dve.wait_ge(s_mask, (NB + 1) * (b + 1))
                    dve.wait_ge(s_dst, b + 1)
                if h == 0 and not first:
                    dve.wait_ge(s_turn, NB * (g - 1))
                elif h == 1 and two:
                    dve.wait_ge(s_turn, NB * (g - HEADS + 1))
                elif h == 2:
                    dve.wait_ge(s_turn, NB * (g - 1))
                elif h == 3 and two:
                    dve.wait_ge(s_turn2, NB * b)
                dve.sem_inc(s_past, 1)
                for i in range(NB):
                    biased(ps_row[:, h % 2, :], wt_head(h), h % 2, a, i, s_top)
                dve.wait_ge(s_top, NB * g + NB)
                shifts(dst1[:, :, h], h % 2, s_shift, 4 * g)

            def exponents_head(b, h):
                g = HEADS * b + h
                dve.wait_ge(s_shift, 4 * g + 4)
                for i in range(NB):
                    dve.wait_ge(s_low, NB * g + i + 1)
                    exponents(wt_head(h), h % 2, i, i % 2, s_arg)

            def invert_head(b, h):
                g = HEADS * b + h
                dve.wait_ge(s_exp, NB * g + NB)
                if h == 3:
                    dve.wait_ge(s_wt, NB * (g - 1))
                nc.vector.reciprocal(inv[:, h % 2, :], total[:, h % 2, :]).then_inc(s_inv, 1)

            def elu(b, h):
                g = HEADS * b + h
                dve.wait_ge(s_eluexp, g + 1)
                nc.vector.tensor_scalar(elu_t[:, h % 2, :], elu_t[:, h % 2, :], 1.0, -1.0, ALU.min, ALU.add)\
                    .then_inc(s_elum, 1)
                dve.wait_ge(s_elum, g + 1)
                nc.vector.scalar_tensor_tensor(out=hT[:, h, :], in0=ps_acc[:, h % 2, :], scalar=bias1[:, h:h + 1],
                                               in1=elu_t[:, h % 2, :], op0=ALU.add, op1=ALU.max).then_inc(s_hT, 1)

            def biased_two(b, a):
                dve.wait_ge(s_row2, b + 1)
                dve.sem_inc(s_past, 1)
                for i in range(NB):
                    biased(ps_row2, wt_two, 2, a, i, s_top2)

            def shifts_two(b):
                dve.wait_ge(s_top2, NB * (b + 1))
                dve.wait_ge(s_xl2, NB * (b + 1))
                shifts(xl2[:, :, D], 2, s_shift2, 4 * b)

            def exponents_two(b):
                dve.wait_ge(s_shift2, 4 * b + 4)
                for i in range(NB):
                    dve.wait_ge(s_low2, NB * b + i + 1)
                    exponents(wt_two, 2, i, i % 2, s_arg2)

            def norm(b):
                dve.wait_ge(s_exp2, NB * (b + 1))
                nc.vector.reciprocal(inv[:, 2, :], total[:, 2, :]).then_inc(s_inv2, 1)
                dve.wait_ge(s_inv2, b + 1)
                dve.wait_ge(s_xb, b + 1)
                for i in range(NB):
                    if i % 2 == 0:
                        dve.wait_ge(s_out2, NB * b + i + 2)
                    nc.vector.scalar_tensor_tensor(out=res[:, i, :], in0=ps_two[:, i // 2, (i % 2) * D:(i % 2 + 1) * D],
                                                   scalar=inv[:, 2, i:i + 1], in1=res[:, i, :],
                                                   op0=ALU.mult, op1=ALU.add).then_inc(s_res, 1)
                for i in range(NB):
                    dve.wait_ge(s_res, NB * b + i + 1)
                    nc.vector.bn_stats(stats[:, i, :], res[:, i, :]).then_inc(s_stats, 1)
                for i in range(NB):
                    dve.wait_ge(s_stats, NB * b + i + 1)
                    dve.sem_inc(s_past, 1)
                    nc.vector.bn_aggr(mv[:, i, :], stats[:, i, :]).then_inc(s_mv, 1)
                dve.wait_ge(s_mv, NB * (b + 1))
                nc.vector.tensor_scalar(var[:], mv[:, :, 1], EPS, None, ALU.add).then_inc(s_var, 1)

            def norm_end(b):
                dve.wait_ge(s_rstd, b + 1)
                for i in range(NB):
                    nc.vector.tensor_scalar(res[:, i, :], res[:, i, :], mv[:, i, 0:1], rstd[:, i:i + 1],
                                            ALU.subtract, ALU.mult).then_inc(s_x1, 1)

            def turn(b, a, two, heads, more):
                if two:
                    elu(b - 1, 3)
                    biased_two(b - 1, 1 - a)
                if heads:
                    invert_head(b, 0)
                    prepare_head(b, a, 1, two)
                    exponents_head(b, 1)
                if two:
                    shifts_two(b - 1)
                    exponents_two(b - 1)
                if heads:
                    invert_head(b, 1)
                    prepare_head(b, a, 2, two)
                    exponents_head(b, 2)
                    elu(b, 0)
                    prepare_head(b, a, 3, two)
                    invert_head(b, 2)
                    exponents_head(b, 3)
                if two:
                    norm(b - 1)
                if heads:
                    invert_head(b, 3)
                if more:
                    make_mask(b + 1, 1 - a)
                    clear_diagonal(b + 1, 1 - a)
                if two:
                    norm_end(b - 1)
                if heads:
                    elu(b, 1)
                if more:
                    keep_terms(b + 1)
                    prepare_head(b + 1, 1 - a, 0, two)
                    exponents_head(b + 1, 0)
                if heads:
                    elu(b, 2)

            make_mask(0, 0)
            clear_diagonal(0, 0)
            keep_terms(0)
            prepare_head(0, 0, 0, False, first=True)
            exponents_head(0, 0)
            turns(dve, turn)

        @block.scalar
        def _(act):
            act.wait_ge(s_const, 16 * N_CONST)

            def keep_source(b):
                act.wait_ge(s_src_ps, b + 1)
                nc.scalar.copy(source[0:HEADS, :], ps_row[0:HEADS, 0, :]).then_inc(s_src_hi, 1)

            def keep_xl(b, i, two):
                act.wait_ge(s_xl_ps, NB * b + i + 1)
                if i == 0 and two:
                    act.wait_ge(s_mm, NB * HEADS * b)
                nc.scalar.copy(xl[:, i, :], ps_acc[:, i % 2, :]).then_inc(s_xl, 1)

            def keep_xl2(b, i):
                act.wait_ge(s_xl2_ps, NB * b + i + 1)
                nc.scalar.copy(xl2[:, i, :], ps_acc[:, (i + 1) % 2, 0:D + 2]).then_inc(s_xl2, 1)

            def exp_block(weights, j, i, done):
                nc.scalar.activation(weights[:, i, :], weights[:, i, :], ACT.Exp,
                                     accum_out=total[:, j, i:i + 1]).then_inc(done, 1)

            def exp_head(b, h, i):
                act.wait_ge(s_arg, NB * (HEADS * b + h) + i + 1)
                exp_block(wt_head(h), h % 2, i, s_exp)

            def exp_two(b, i):
                act.wait_ge(s_arg2, NB * b + i + 1)
                exp_block(wt_two, 2, i, s_exp2)

            def keep_turned(b, h, i, two):
                g = HEADS * b + h
                act.wait_ge(s_turn, NB * g + i + 1)
                if h == 1 and two:
                    act.wait_ge(s_out2, NB * b)
                elif h or two:
                    act.wait_ge(s_mm, NB * (g - 1) + i + 1)
                nc.scalar.copy(wtT[:, i, :], ps_turn[:, i % 2, :]).then_inc(s_wtT, 1)

            def keep_turned_two(b, i, heads):
                if heads:
                    act.wait_ge(s_mm, NB * HEADS * (b + 1) + i + 1)
                act.wait_ge(s_turn2, NB * b + i + 1)
                nc.scalar.copy(wtT[:, i, :], ps_turn[:, i % 2, :]).then_inc(s_wtT2, 1)

            def elu_exp(b, h, two):
                g = HEADS * b + h
                act.wait_ge(s_mm, NB * (g + 1))
                if h >= 2 or two:
                    act.wait_ge(s_hT, g - 1)
                nc.scalar.activation(elu_t[:, h % 2, :], ps_acc[:, h % 2, :], ACT.Exp,
                                     bias=bias1[:, h:h + 1]).then_inc(s_eluexp, 1)

            def turn(b, a, two, heads, more):
                if two:
                    elu_exp(b - 1, 3, two)
                if heads:
                    keep_xl(b, 0, two)
                    for i in range(NB):
                        exp_head(b, 0, i)
                if two:
                    for i in range(NB):
                        keep_xl2(b - 1, i)
                if heads:
                    for i in range(1, NB):
                        keep_xl(b, i, two)
                        exp_head(b, 1, i - 1)
                    exp_head(b, 1, NB - 1)
                for i in range(NB):
                    if heads:
                        keep_turned(b, 0, i, two)
                    if two:
                        exp_two(b - 1, i)
                if heads:
                    elu_exp(b, 0, two)
                if two:
                    for i in range(NB):
                        keep_turned_two(b - 1, i, heads)
                if heads:
                    for i in range(NB):
                        exp_head(b, 2, i)
                    for i in range(NB):
                        keep_turned(b, 1, i, two)
                    elu_exp(b, 1, two)
                    for i in range(NB):
                        exp_head(b, 3, i)
                if more:
                    keep_source(b + 1)
                if heads:
                    for i in range(NB):
                        keep_turned(b, 2, i, two)
                    elu_exp(b, 2, two)
                    for i in range(NB):
                        keep_turned(b, 3, i, two)

            keep_source(0)
            turns(act, turn)

        @block.tensor
        def _(pe):
            pe.wait_ge(s_const, 16 * N_CONST)
            pe.wait_ge(s_v, N_V)
            pe.wait_ge(s_zero, 4)
            pe.wait_ge(setup_done, 6)

            def terms(b, two, first=False):
                pe.wait_ge(s_xT, 16 * b + 16)
                if not first:
                    pe.wait_ge(s_top, NB * (HEADS * b - 1))
                for k in range(DB):
                    mm = nc.tensor.matmul(ps_row[0:HEADS, 0, :], v1[:, 0, k, :], xT[:, k, :],
                                          start=(k == 0), stop=(k == DB - 1))
                mm.then_inc(s_src_ps, 1)
                if two:
                    pe.wait_ge(s_res, NB * (b - 1))
                elif not first:
                    pe.wait_ge(s_dst, b)
                for i in range(NB):
                    for k in range(DB):
                        mm = nc.tensor.matmul(ps_dst[:, HEADS * i:HEADS * (i + 1)], xT[:, k, i * P:(i + 1) * P],
                                              v1[:, 1, k, :], start=(k == 0), stop=(k == DB - 1))
                mm.then_inc(s_dst_ps, 1)

            def head_row(b, h, first=False):
                g = HEADS * b + h
                if h == 0:
                    pe.wait_ge(s_src_lo, b + 1)
                elif h > 1 or not first:
                    pe.wait_ge(s_top, NB * (g - 1))
                nc.tensor.matmul(ps_row[:, h % 2, :], pick[:, h:h + 1].to_broadcast([LO_AT + HEADS, P]), source[:],
                                 start=True, stop=True).then_inc(s_row, 1)

            def project(b, i, two):
                if two:
                    if i == 0:
                        pe.wait_ge(s_hT, HEADS * b - 1)
                    elif i < 3:
                        pe.wait_ge(s_xl2, NB * b - 2 + i)
                    else:
                        pe.wait_ge(s_xl, NB * b + i - 1)
                elif i >= 2:
                    pe.wait_ge(s_xl, NB * b + i - 1)
                for k in range(DB):
                    mm = nc.tensor.matmul(ps_acc[:, i % 2, :], xT[:, k, i * P:(i + 1) * P], wg1[:, k, :],
                                          start=(k == 0), stop=(k == DB - 1))
                mm.then_inc(s_xl_ps, 1)

            def row_two(b, h, two):
                pe.wait_ge(s_hT, HEADS * b + h + 1)
                if h == 0 and two:
                    pe.wait_ge(s_res, NB * b - 2)
                mm = nc.tensor.matmul(ps_row2, wg2[:, h, D + 1:D + 2].to_broadcast([P, P]), hT[:, h, :],
                                      start=(h == 0), stop=(h == HEADS - 1))
                if h == HEADS - 1:
                    mm.then_inc(s_row2, 1)

            def project_two(b, heads):
                for i in range(NB):
                    if i >= 2:
                        pe.wait_ge(s_xl2, NB * b + i - 1)
                    elif i == 1 and heads:
                        pe.wait_ge(s_xl, NB * (b + 1) + 1)
                    for h in range(HEADS):
                        mm = nc.tensor.matmul(ps_acc[:, (i + 1) % 2, 0:D + 2], hT[:, h, i * P:(i + 1) * P], wg2[:, h, :],
                                              start=(h == 0), stop=(h == HEADS - 1))
                    mm.then_inc(s_xl2_ps, 1)

            def turn_tile(weights, j, done):
                for i in range(NB):
                    mm = nc.tensor.transpose(ps_turn[:, j % 2, i * P:(i + 1) * P], weights[:, i, j * P:(j + 1) * P],
                                             ident[:])
                mm.then_inc(done, 1)

            def layer_two(b, heads):
                pe.wait_ge(s_exp2, NB * (b + 1))
                for j in range(NB):
                    if j >= 2:
                        pe.wait_ge(s_wtT2, NB * b + j - 1)
                    elif heads:
                        pe.wait_ge(s_wtT, NB * HEADS * (b + 1) + 3 + j)
                    turn_tile(wt_two, j, s_turn2)
                pe.wait_ge(s_wtT2, NB * (b + 1))
                if heads:
                    pe.wait_ge(s_top2, NB * (b + 1))
                for i in range(NB):
                    for j in range(NB):
                        mm = nc.tensor.matmul(ps_two[:, i // 2, (i % 2) * D:(i % 2 + 1) * D],
                                              wtT[:, j, i * P:(i + 1) * P], xl2[:, j, 0:D],
                                              start=(j == 0), stop=(j == NB - 1))
                    mm.then_inc(s_out2, 1)

            def head(b, h, two):
                g = HEADS * b + h
                pe.wait_ge(s_wt, NB * (g + 1))

                def turn_j(j):
                    if j >= 2:
                        pe.wait_ge(s_wtT, NB * g + j - 1)
                    elif h == 1 and two:
                        pe.wait_ge(s_wtT2, NB * b - 1 + j)
                    elif h or two:
                        pe.wait_ge(s_wtT, NB * g - 1 + j)
                    turn_tile(wt_head(h), j, s_turn)

                turn_j(0)
                turn_j(1)
                if h >= 2:
                    pe.wait_ge(s_hT, g - 1)
                elif h == 0:
                    pe.wait_ge(s_xl, NB * (b + 1))
                for j in range(NB):
                    pe.wait_ge(s_wtT, NB * g + j + 1)
                    nc.tensor.matmul(ps_acc[:, h % 2, :], xl[:, j, h * FH:(h + 1) * FH], wtT[:, j, :],
                                     start=(j == 0), stop=(j == NB - 1)).then_inc(s_mm, 1)
                    if j + 2 < NB:
                        turn_j(j + 2)

            def turn(b, a, two, heads, more):
                if heads:
                    head_row(b, 2)
                    project(b, 0, two)
                if two:
                    row_two(b - 1, 3, two)
                    project_two(b - 1, heads)
                if heads:
                    for i in range(1, NB):
                        project(b, i, two)
                    head(b, 0, two)
                    head_row(b, 3)
                if two:
                    layer_two(b - 1, heads)
                if heads:
                    head(b, 1, two)
                if more:
                    terms(b + 1, two)
                if heads:
                    head(b, 2, two)
                    row_two(b, 0, two)
                    row_two(b, 1, two)
                if more:
                    head_row(b + 1, 0)
                if heads:
                    head(b, 3, two)
                if more:
                    head_row(b + 1, 1)
                if heads:
                    row_two(b, 2, two)

            terms(0, False, first=True)
            head_row(0, 0)
            head_row(0, 1, first=True)
            turns(pe, turn)


def transformer_pass(nc, t, x1_dram, allocator, w_hi, w_lo, w1, w2, ident, ones, off_diag):
    B, N, D = t["x"].shape
    L, FF = t["ff_b1"].shape
    NB, DB, FB = N // P, D // P, FF // P
    STEPS = 2 * L
    TURNS = B // 2

    def thread(s):
        return s % 2

    def layer(s):
        return s % STEPS // 2

    with ExitStack() as ctx:
        sb = allocator(ctx)

        def psum(name, shape, dt=F32):
            return ctx.enter_context(nc.psum_tensor(name, shape, dt))

        def sem(name):
            return ctx.enter_context(nc.semaphore(name))

        att_w = sb("att_w", [P, L, 2, D])
        att_b = sb("att_b", [P, L])
        g1r = sb("g1r", [P, L, D])
        b1r = sb("b1r", [P, L, D])
        g2r = sb("g2r", [P, L, D])
        b2r = sb("b2r", [P, L, D])
        g1c = sb("g1c", [P, L * DB])
        b1c = sb("b1c", [P, L * DB])
        ffb = sb("ffb", [P, L * FB])
        x = sb("x_state", [P, 2, NB, D])
        maskb = sb("mask_bias", [P, 2 * NB * N + NB * P], BF16)
        fin = sb("fin", [P, NB, D])
        adj_in = sb("adj_blocks", [P, 2, N], I32)
        wt = sb("wt", [P, NB, N])
        low = sb("low_part", [P, 2, N])
        wtT = sb("wt_turned", [P, NB, N])
        h_hi = sb("h_hi", [P, DB, N], F32R)
        h_lo = sb("h_lo", [P, DB, N], F32R)
        whole = sb("whole", [P, 2, N])
        g_hi = sb("g_hi", [P, FB, N], F32R)
        g_lo = sb("g_lo", [P, FB, N], F32R)
        col = sb("col", [P, 2, 2, NB])
        query = sb("query", [P, NB])
        top = sb("top_q", [P, NB])
        tmp = sb("tmp_q", [P, NB])
        shift = sb("shift_q", [P, NB])
        sh_hi = sb("sh_hi_q", [P, NB])
        sh_lo = sb("sh_lo_q", [P, NB])
        total = sb("total_q", [P, NB])
        inv = sb("inv_q", [P, NB])
        scrap = sb("scrap", [P, D])
        stats = sb("stats_q", [P, 3, NB, 6])
        mv = sb("mv_q", [P, 3, NB, 2])
        var = sb("var_q", [P, 3, NB])
        rstd = sb("rstd_q", [P, 3, NB])
        half = sb("half_q", [P, NB])

        b2_in = wt[:, 0:2, :].rearrange("p i n -> p (i n)")[:, 0:L * D]
        sums = wt[:, 0:2, :].rearrange("p i n -> p (i n)").rearrange("p (i n) -> p i n", i=NB)
        diag = low[:, 0, :].rearrange("p (i n) -> p i n", i=NB)
        mask = [maskb[:, a * NB * N:(a + 1) * NB * N].rearrange("p (i n) -> p i n", i=NB) for a in range(2)]
        mask_diag = [maskb[:, a * NB * N:a * NB * N + NB * (N + P)].rearrange("p (i n) -> p i n", i=NB)[:, :, 0:P]
                     for a in range(2)]

        ps_ff = psum("ps_ff", [P, 2, N])
        ps_y = psum("ps_y", [P, 2, N])
        ps_agg = psum("ps_agg", [P, 2, N])
        ps_turn = psum("ps_turned", [P, 2, N])

        q_const = sem("q_const")
        q_half = sem("q_half")
        q_b1r = sem("q_b1r")
        q_x = [sem(f"q_x{a}") for a in range(2)]
        q_adj = [sem(f"q_adj{i}") for i in range(2)]
        q_fin = sem("q_fin")
        q_mask = sem("q_mask")
        q_dot = sem("q_dot")
        q_diag = sem("q_diag")
        q_query = sem("q_query")
        q_row = sem("q_row")
        q_top = sem("q_top")
        q_shift = sem("q_shift")
        q_low = sem("q_low")
        q_arg = sem("q_arg")
        q_exp = sem("q_exp")
        q_inv = sem("q_inv")
        q_turn = sem("q_turn")
        q_wtT = sem("q_wtT")
        q_agg = sem("q_agg")
        q_r1 = sem("q_r1")
        q_st1 = sem("q_st1")
        q_mv1 = sem("q_mv1")
        q_var1 = sem("q_var1")
        q_rstd1 = sem("q_rstd1")
        q_n1 = sem("q_n1")
        q_nT = sem("q_nT")
        q_whole = sem("q_whole")
        q_hhi = sem("q_hhi")
        q_hlo = sem("q_hlo")
        q_h = sem("q_h")
        q_ff = sem("q_ff")
        q_gelu = sem("q_gelu")
        q_glo = sem("q_glo")
        q_y = sem("q_y")
        q_r2 = sem("q_r2")
        q_st2 = sem("q_st2")
        q_mv2 = sem("q_mv2")
        q_var2 = sem("q_var2")
        q_rstd2 = sem("q_rstd2")
        q_n2 = sem("q_n2")
        q_xn = sem("q_xn")
        q_r3 = sem("q_r3")
        q_st3 = sem("q_st3")
        q_mv3 = sem("q_mv3")
        q_var3 = sem("q_var3")
        q_rstd3 = sem("q_rstd3")
        q_out = sem("q_out")
        q_past = sem("q_past")
        q_past_pool = sem("q_past_pool")
        q_store = sem("q_store")

        block = ctx.enter_context(nc.Block())
        VECTORS = 10

        @block.sync
        def _(sp):
            sp.dma_start(att_w[:].rearrange("p l j d -> p (l j d)"),
                         t["attn_w"].rearrange("l d -> (l d)").partition_broadcast(P)).then_inc(q_const, 16)
            sp.dma_start(att_b[:], t["attn_b"].partition_broadcast(P)).then_inc(q_const, 16)
            for dst, name in ((g1r, "g1"), (b1r, "beta1"), (g2r, "g2"), (b2r, "beta2")):
                sp.dma_start(dst[:].rearrange("p l d -> p (l d)"),
                             t[name].rearrange("l d -> (l d)").partition_broadcast(P)).then_inc(q_const, 16)
            sp.dma_start(b2_in, t["ff_b2"].rearrange("l d -> (l d)").partition_broadcast(P)).then_inc(q_const, 16)
            for dst, name in ((g1c, "g1T"), (b1c, "beta1T"), (ffb, "ff_b1T")):
                sp.dma_start(dst[:], t[name]).then_inc(q_const, 16)

            def load_x(b, a):
                sp.dma_start(x[:, a], x1_dram[b].rearrange("(i p) n -> p i n", p=P)).then_inc(q_x[a], 16)

            def load_adj(b, blocks, first=False):
                for i in blocks:
                    if i >= 2:
                        sp.wait_ge(q_mask, (NB + 1) * b + i - 1)
                    elif not first:
                        sp.wait_ge(q_mask, (NB + 1) * b - 2 + i)
                    sp.dma_start(adj_in[:, i % 2, :], t["adj"][b, i * P:(i + 1) * P, :])\
                        .then_inc(q_adj[i % 2], 16)

            def load_fin(b):
                sp.dma_start(fin[:], x1_dram[b].rearrange("(i p) n -> p i n", p=P)).then_inc(q_fin, 16)

            def store(b):
                sp.wait_ge(q_out, NB * b + NB)
                sp.dma_start(t["out"][b].rearrange("(i p) n -> p i n", p=P), fin[:]).then_inc(q_store, 16)

            def turn(n, last):
                for a in range(2):
                    b = 2 * n + a
                    if not last:
                        load_adj(b + 2, range(0, 2))
                        sp.wait_ge(q_r3, 2 * b + 2)
                        load_x(b + 2, a)
                        load_adj(b + 2, range(2, NB))
                    store(b)
                    if not (last and a):
                        sp.wait_ge(q_store, 16 * (b + 1))
                        load_fin(b + 1)

            load_x(0, 0)
            load_adj(0, range(NB), first=True)
            load_x(1, 1)
            load_adj(1, range(NB))
            load_fin(0)
            with sp.Fori(0, TURNS - 1) as n:
                turn(n, False)
            turn(TURNS - 1, True)
            sp.wait_ge(q_store, 16 * B)

        @block.gpsimd
        def _(pool):
            nc.gpsimd.memset(half[:], -0.5).then_inc(q_half, 1)
            pool.wait_ge(q_half, 1)

            def low_parts(q):
                pool.wait_ge(q_shift, 4 * q + 4)
                for i in range(NB):
                    if i >= 2:
                        pool.wait_ge(q_arg, NB * q + i - 1)
                    pool.sem_inc(q_past_pool, 1)
                    nc.gpsimd.tensor_scalar(low[:, i % 2, :], wt[:, i, :], SLOPE, sh_lo[:, i:i + 1],
                                            ALU.mult, ALU.add).then_inc(q_low, 1)

            def gelu_lo(q, c):
                pool.wait_ge(q_gelu, 2 * (FB * q + c + 1))
                nc.gpsimd.tensor_tensor(g_lo[:, c, :], whole[:, c % 2, :], g_hi[:, c, :].bitcast(F32),
                                        ALU.subtract).then_inc(q_glo, 1)

            def inverse_deviation(which, blocks, ready, value, done):
                pool.wait_ge(ready, value)
                nc.gpsimd.tensor_tensor(rstd[:, which, blocks], var[:, which, blocks], half[:, blocks], ALU.pow)\
                    .then_inc(done, 1)

            def feed_forward_half(q, s, b, f):
                blocks = slice(2 * f, 2 * f + 2)
                inverse_deviation(1, blocks, q_var2, 2 * q + f + 1, q_rstd2)
                if layer(s) == L - 1:
                    inverse_deviation(2, blocks, q_var3, 2 * b + f + 1, q_rstd3)

            def attention_norm(q):
                for f in range(2):
                    inverse_deviation(0, slice(2 * f, 2 * f + 2), q_var1, 2 * q + f + 1, q_rstd1)

            def turn(n, last):
                for s in range(STEPS):
                    q, b = STEPS * n + s, 2 * n + thread(s)
                    more = not (last and s == STEPS - 1)
                    for c in range(FB):
                        gelu_lo(q, c)
                    if more:
                        low_parts(q + 1)
                    feed_forward_half(q, s, b, 0)
                    if more:
                        attention_norm(q + 1)
                    feed_forward_half(q, s, b, 1)

            low_parts(0)
            attention_norm(0)
            with pool.Fori(0, TURNS - 1) as n:
                turn(n, False)
            turn(TURNS - 1, True)

        @block.vector
        def _(dve):
            dve.wait_ge(q_const, 16 * VECTORS)
            nc.vector.tensor_tensor(b1r[:].rearrange("p l d -> p (l d)"), b1r[:].rearrange("p l d -> p (l d)"), b2_in,
                                    ALU.add).then_inc(q_b1r, 1)

            def make_mask(b, a):
                for i in range(NB):
                    dve.wait_ge(q_adj[i % 2], 16 * (NB // 2 * b + i // 2 + 1))
                    nc.vector.tensor_scalar(mask[a][:, i, :], adj_in[:, i % 2, :], 0, MASKED, ALU.is_le, ALU.mult)\
                        .then_inc(q_mask, 1)
                dve.wait_ge(q_mask, (NB + 1) * b + NB)
                nc.vector.tensor_tensor(mask_diag[a], mask_diag[a], off_diag[:].unsqueeze(1).to_broadcast([P, NB, P]),
                                        ALU.mult).then_inc(q_mask, 1)

            def dots(q, s, f):
                a, l = thread(s), layer(s)
                for i in range(2 * f, 2 * f + 2):
                    for j in range(2):
                        at = 2 * NB * q + 2 * i + j
                        if 2 * i + j:
                            dve.wait_ge(q_dot, at)
                        nc.vector.tensor_tensor_reduce(out=scrap[:], in0=x[:, a, i, :], in1=att_w[:, l, j, :], scale=1.0,
                                                       scalar=0.0, op0=ALU.mult, op1=ALU.add,
                                                       accum_out=col[:, a, j, i:i + 1]).then_inc(q_dot, 1)

            def diagonal(q, s):
                a, l = thread(s), layer(s)
                dve.wait_ge(q_dot, 2 * NB * (q + 1))
                for i in range(NB):
                    nc.vector.tensor_scalar(diag[:, i, :], ident[:], col[:, a, 1, i:i + 1], None, ALU.mult)\
                        .then_inc(q_diag, 1)
                nc.vector.tensor_scalar(query[:], col[:, a, 0, :], att_b[:, l:l + 1], None, ALU.add).then_inc(q_query, 1)

            def first_terms(q, s, n):
                a = thread(s)
                b = 2 * n + a
                make_mask(b, a)
                dve.wait_ge(q_x[a], 16 * (n + 1))
                dots(q, s, 0)
                dots(q, s, 1)
                dve.wait_ge(q_mask, (NB + 1) * (b + 1))
                diagonal(q, s)

            def prepare(q, s):
                a = thread(s)
                dve.wait_ge(q_row, q + 1)
                dve.sem_inc(q_past, 1)
                for i in range(NB):
                    nc.vector.tensor_tensor_reduce(out=wt[:, i, :], in0=ps_turn[:, 0, :], in1=mask[a][:, i, :], scale=1.0,
                                                   scalar=LOWEST, op0=ALU.add, op1=ALU.max,
                                                   accum_out=top[:, i:i + 1]).then_inc(q_top, 1)
                dve.wait_ge(q_top, NB * (q + 1))
                dve.wait_ge(q_query, q + 1)
                nc.vector.tensor_tensor(tmp[:], top[:], query[:], ALU.add).then_inc(q_shift, 1)
                dve.wait_ge(q_shift, 4 * q + 1)
                nc.vector.scalar_tensor_tensor(out=shift[:], in0=tmp[:], scalar=SLOPE, in1=tmp[:],
                                               op0=ALU.mult, op1=ALU.max).then_inc(q_shift, 1)
                dve.wait_ge(q_shift, 4 * q + 2)
                nc.vector.scalar_tensor_tensor(out=sh_lo[:], in0=query[:], scalar=SLOPE, in1=shift[:],
                                               op0=ALU.mult, op1=ALU.subtract).then_inc(q_shift, 1)
                nc.vector.tensor_tensor(sh_hi[:], query[:], shift[:], ALU.subtract).then_inc(q_shift, 1)

            def exponents(q):
                dve.wait_ge(q_shift, 4 * q + 4)
                for i in range(NB):
                    dve.wait_ge(q_low, NB * q + i + 1)
                    nc.vector.scalar_tensor_tensor(out=wt[:, i, :], in0=wt[:, i, :], scalar=sh_hi[:, i:i + 1],
                                                   in1=low[:, i % 2, :], op0=ALU.add, op1=ALU.max).then_inc(q_arg, 1)

            def moments(data, which, blocks, before, ready, st, mvs, vs):
                for n, i in enumerate(blocks):
                    dve.wait_ge(ready[0], ready[1](n))
                    nc.vector.bn_stats(stats[:, which, i, :], data[:, i, :]).then_inc(st, 1)
                for n, i in enumerate(blocks):
                    dve.wait_ge(st, before + n + 1)
                    dve.sem_inc(q_past, 1)
                    nc.vector.bn_aggr(mv[:, which, i, :], stats[:, which, i, :]).then_inc(mvs, 1)
                dve.wait_ge(mvs, before + len(blocks))
                cols = slice(blocks[0], blocks[-1] + 1)
                nc.vector.tensor_scalar(var[:, which, cols], mv[:, which, cols, 1], EPS, None, ALU.add).then_inc(vs, 1)

            def scaled(out, which, blocks, done, data=None):
                data = out if data is None else data
                for i in blocks:
                    nc.vector.tensor_scalar(out[:, i, :], data[:, i, :], mv[:, which, i, 0:1], rstd[:, which, i:i + 1],
                                            ALU.subtract, ALU.mult).then_inc(done, 1)

            def attention_residual(q, s):
                a = thread(s)
                dve.wait_ge(q_exp, NB * (q + 1))
                nc.vector.reciprocal(inv[:], total[:]).then_inc(q_inv, 1)
                dve.wait_ge(q_inv, q + 1)
                for f in range(2):
                    blocks = range(2 * f, 2 * f + 2)
                    dve.wait_ge(q_agg, 2 * q + f + 1)
                    for i in blocks:
                        nc.vector.scalar_tensor_tensor(out=sums[:, i, :],
                                                       in0=ps_agg[:, i // 2, (i % 2) * D:(i % 2 + 1) * D],
                                                       scalar=inv[:, i:i + 1], in1=x[:, a, i, :],
                                                       op0=ALU.mult, op1=ALU.add).then_inc(q_r1, 1)
                    moments(sums, 0, blocks, NB * q + 2 * f, (q_r1, lambda n: NB * q + 2 * f + n + 1),
                            q_st1, q_mv1, q_var1)

            def attention_norm(q, s):
                a = thread(s)
                for f in range(2):
                    dve.wait_ge(q_rstd1, 2 * q + f + 1)
                    scaled(x[:, a], 0, range(2 * f, 2 * f + 2), q_n1, sums)

            def h_parts(q, s):
                l = layer(s)
                for k in range(DB):
                    dve.wait_ge(q_nT, DB * q + k + 1)
                    nc.vector.tensor_scalar(whole[:, k, :], ps_turn[:, (k + 1) % 2, :], g1c[:, l * DB + k:l * DB + k + 1],
                                            b1c[:, l * DB + k:l * DB + k + 1], ALU.mult, ALU.add).then_inc(q_whole, 1)
                    dve.wait_ge(q_whole, DB * q + k + 1)
                    dve.wait_ge(q_hhi, DB * q + k + 1)
                    nc.vector.tensor_tensor(h_lo[:, k, :], whole[:, k, :], h_hi[:, k, :].bitcast(F32),
                                            ALU.subtract).then_inc(q_hlo, 1)

            def residual_h(q, s):
                a, l = thread(s), layer(s)
                dve.wait_ge(q_nT, DB * (q + 1))
                nc.vector.tensor_tensor(x[:, a], x[:, a], g1r[:, l:l + 1, :].to_broadcast([P, NB, D]), ALU.mult)\
                    .then_inc(q_h, 1)
                dve.wait_ge(q_h, 2 * q + 1)
                nc.vector.tensor_tensor(x[:, a], x[:, a], b1r[:, l:l + 1, :].to_broadcast([P, NB, D]), ALU.add)\
                    .then_inc(q_h, 1)

            def feed_forward_half(q, s, b, f):
                a, l = thread(s), layer(s)
                blocks = range(2 * f, 2 * f + 2)
                rows = slice(2 * f, 2 * f + 2)
                dve.wait_ge(q_y, 2 * q + f + 1)
                dve.wait_ge(q_h, 2 * q + 2)
                nc.vector.tensor_tensor(x[:, a, rows, :], ps_y[:, f, :].rearrange("p (i n) -> p i n", i=2),
                                        x[:, a, rows, :], ALU.add).then_inc(q_r2, 1)
                moments(x[:, a], 1, blocks, NB * q + 2 * f, (q_r2, lambda n: 2 * q + f + 1), q_st2, q_mv2, q_var2)
                dve.wait_ge(q_rstd2, 2 * q + f + 1)
                scaled(x[:, a], 1, blocks, q_n2)
                dve.wait_ge(q_n2, NB * q + 2 * f + 2)
                nc.vector.tensor_tensor(x[:, a, rows, :], x[:, a, rows, :],
                                        g2r[:, l:l + 1, :].to_broadcast([P, 2, D]), ALU.mult).then_inc(q_xn, 1)
                dve.wait_ge(q_xn, 4 * q + 2 * f + 1)
                nc.vector.tensor_tensor(x[:, a, rows, :], x[:, a, rows, :],
                                        b2r[:, l:l + 1, :].to_broadcast([P, 2, D]), ALU.add).then_inc(q_xn, 1)
                dve.wait_ge(q_xn, 4 * q + 2 * f + 2)
                if l == L - 1:
                    dve.wait_ge(q_fin, 16 * (b + 1))
                    nc.vector.tensor_tensor(fin[:, rows, :], fin[:, rows, :], x[:, a, rows, :], ALU.add).then_inc(q_r3, 1)
                    moments(fin, 2, blocks, NB * b + 2 * f, (q_r3, lambda n: 2 * b + f + 1), q_st3, q_mv3, q_var3)
                    dve.wait_ge(q_rstd3, 2 * b + f + 1)
                    scaled(fin, 2, blocks, q_out)

            def turn(n, last):
                for s in range(STEPS):
                    q, b = STEPS * n + s, 2 * n + thread(s)
                    more = not (last and s == STEPS - 1)
                    again = layer(s) < L - 1
                    if more:
                        prepare(q + 1, s + 1)
                        exponents(q + 1)
                    feed_forward_half(q, s, b, 0)
                    if again:
                        dots(q + 2, s + 2, 0)
                    if more:
                        attention_residual(q + 1, s + 1)
                        attention_norm(q + 1, s + 1)
                        h_parts(q + 1, s + 1)
                    feed_forward_half(q, s, b, 1)
                    if again:
                        dots(q + 2, s + 2, 1)
                        diagonal(q + 2, s + 2)
                    elif not last:
                        first_terms(q + 2, s + 2, n + 1)
                    if more:
                        residual_h(q + 1, s + 1)

            first_terms(0, 0, 0)
            prepare(0, 0)
            exponents(0)
            attention_residual(0, 0)
            attention_norm(0, 0)
            h_parts(0, 0)
            first_terms(1, 1, 0)
            dve.wait_ge(q_b1r, 1)
            residual_h(0, 0)
            with dve.Fori(0, TURNS - 1) as n:
                turn(n, False)
            turn(TURNS - 1, True)

        @block.scalar
        def _(act):
            act.wait_ge(q_const, 16 * VECTORS)

            def exps(q):
                for i in range(NB):
                    act.wait_ge(q_arg, NB * q + i + 1)
                    nc.scalar.activation(wt[:, i, :], wt[:, i, :], ACT.Exp, accum_out=total[:, i:i + 1]).then_inc(q_exp, 1)

            def keep_turned(q):
                for j in range(NB):
                    act.wait_ge(q_turn, NB * q + j + 1)
                    nc.scalar.copy(wtT[:, j, :], ps_turn[:, (j + 1) % 2, :]).then_inc(q_wtT, 1)

            def keep_h(q):
                for k in range(DB):
                    act.wait_ge(q_whole, DB * q + k + 1)
                    nc.scalar.copy(h_hi[:, k, :], whole[:, k, :]).then_inc(q_hhi, 1)

            def gelu(q, s, c):
                l = layer(s)
                act.wait_ge(q_ff, FB * q + c + 1)
                if c >= 2:
                    act.wait_ge(q_glo, FB * q + c - 1)
                for out in (whole[:, c % 2, :], g_hi[:, c, :]):
                    nc.scalar.activation(out, ps_ff[:, c % 2, :], ACT.Gelu,
                                         bias=ffb[:, l * FB + c:l * FB + c + 1]).then_inc(q_gelu, 1)

            def turn(n, last):
                for s in range(STEPS):
                    q = STEPS * n + s
                    for c in range(FB):
                        gelu(q, s, c)
                    if not (last and s == STEPS - 1):
                        exps(q + 1)
                        keep_turned(q + 1)
                        keep_h(q + 1)

            exps(0)
            keep_turned(0)
            keep_h(0)
            with act.Fori(0, TURNS - 1) as n:
                turn(n, False)
            turn(TURNS - 1, True)

        @block.tensor
        def _(pe):
            def key_row(q):
                pe.wait_ge(q_diag, NB * (q + 1))
                for i in range(NB):
                    mm = nc.tensor.matmul(ps_turn[:, 0, i * P:(i + 1) * P], ones[:], diag[:, i, :], start=True, stop=True)
                mm.then_inc(q_row, 1)

            def attend(q, s):
                a = thread(s)
                pe.wait_ge(q_exp, NB * (q + 1))
                for j in range(NB):
                    if j >= 2:
                        pe.wait_ge(q_wtT, NB * q + j - 1)
                    for i in range(NB):
                        mm = nc.tensor.transpose(ps_turn[:, (j + 1) % 2, i * P:(i + 1) * P], wt[:, i, j * P:(j + 1) * P],
                                                 ident[:])
                    mm.then_inc(q_turn, 1)
                pe.wait_ge(q_wtT, NB * (q + 1))
                for i in range(NB):
                    for j in range(NB):
                        mm = nc.tensor.matmul(ps_agg[:, i // 2, (i % 2) * D:(i % 2 + 1) * D],
                                              wtT[:, j, i * P:(i + 1) * P], x[:, a, j, :],
                                              start=(j == 0), stop=(j == NB - 1))
                    if i % 2:
                        mm.then_inc(q_agg, 1)

            def turn_n(q, s):
                a = thread(s)
                pe.wait_ge(q_n1, NB * (q + 1))
                for k in range(DB):
                    for i in range(NB):
                        mm = nc.tensor.transpose(ps_turn[:, (k + 1) % 2, i * P:(i + 1) * P], x[:, a, i, k * P:(k + 1) * P],
                                                 ident[:])
                    mm.then_inc(q_nT, 1)

            def first_product(q, s, c):
                l = layer(s)
                if c >= 2:
                    pe.wait_ge(q_gelu, 2 * (FB * q + c - 1))
                for k in range(DB):
                    if c == 0:
                        pe.wait_ge(q_hhi, DB * q + k + 1)
                    for w in (w_hi, w_lo):
                        nc.tensor.matmul(ps_ff[:, c % 2, :], w1(w, l, k, c), h_hi[:, k, :],
                                         start=(k == 0 and w is w_hi), stop=False)
                for k in range(DB):
                    if c == 0:
                        pe.wait_ge(q_hlo, DB * q + k + 1)
                    mm = nc.tensor.matmul(ps_ff[:, c % 2, :], w1(w_hi, l, k, c), h_lo[:, k, :],
                                          start=False, stop=(k == DB - 1))
                mm.then_inc(q_ff, 1)

            def second_product(q, s, f):
                l = layer(s)
                for i in range(2 * f, 2 * f + 2):
                    for c in range(FB):
                        if i == 0:
                            pe.wait_ge(q_glo, FB * q + c + 1)
                        for n, (g, w) in enumerate([(g_hi, w_hi), (g_hi, w_lo), (g_lo, w_hi)]):
                            mm = nc.tensor.matmul(ps_y[:, f, (i % 2) * D:(i % 2 + 1) * D],
                                                  g[:, c, i * P:(i + 1) * P], w2(w, l, c),
                                                  start=(c == 0 and n == 0), stop=(c == FB - 1 and n == 2))
                mm.then_inc(q_y, 1)

            def turn(n, last):
                for s in range(STEPS):
                    q = STEPS * n + s
                    more = not (last and s == STEPS - 1)
                    for c in range(FB):
                        if c == FB - 2 and more:
                            key_row(q + 1)
                        first_product(q, s, c)
                    second_product(q, s, 0)
                    if more:
                        attend(q + 1, s + 1)
                    second_product(q, s, 1)
                    if more:
                        turn_n(q + 1, s + 1)

            key_row(0)
            attend(0, 0)
            turn_n(0, 0)
            with pe.Fori(0, TURNS - 1) as n:
                turn(n, False)
            turn(TURNS - 1, True)


_INS = ("x", "xT", "adj", "adjT", "gat_w1", "att_src1", "att_dst1", "gat_b1T", "gat_w2", "att_src2", "att_dst2",
        "gat_b2", "attn_w", "attn_b", "ff_w", "ff_b1", "ff_b1T", "ff_b2", "g1", "beta1", "g1T", "beta1T", "g2", "beta2")


def layouts(a):
    import numpy as np
    L, D = a["L1_gnn_g1"].shape
    B = a["x"].shape[0]
    heads = a["L0_gnn_att_src1"].shape[0]
    FF = a["L1_gnn_b1"].shape[1]

    def on_partitions(v):
        v = v.reshape(v.shape[:-1] + (-1, P))
        return v.reshape(-1, P).T

    w1 = a["L1_gnn_W1"].reshape(L, D // P, P, FF).transpose(2, 0, 1, 3).reshape(P, -1)
    w2 = a["L1_gnn_W2"].reshape(L, FF // P, P, D).transpose(2, 0, 1, 3).reshape(P, -1)
    ff_w = np.concatenate([w1, w2], axis=1).reshape(P, B, -1).transpose(1, 0, 2)
    return {
        "x": a["x"], "xT": a["x"].transpose(0, 2, 1), "adj": a["adj"], "adjT": a["adj"].transpose(0, 2, 1),
        "gat_w1": a["L0_gnn_W1"], "att_src1": a["L0_gnn_att_src1"], "att_dst1": a["L0_gnn_att_dst1"],
        "gat_b1T": on_partitions(a["L0_gnn_b1"]), "gat_w2": a["L0_gnn_W2"],
        "att_src2": a["L0_gnn_att_src2"], "att_dst2": a["L0_gnn_att_dst2"], "gat_b2": a["L0_gnn_b2"],
        "attn_w": a["L1_gnn_attn_w"], "attn_b": a["L1_gnn_attn_b"], "ff_w": ff_w,
        "ff_b1": a["L1_gnn_b1"], "ff_b1T": on_partitions(a["L1_gnn_b1"]), "ff_b2": a["L1_gnn_b2"],
        "g1": a["L1_gnn_g1"], "beta1": a["L1_gnn_beta1"], "g1T": on_partitions(a["L1_gnn_g1"]),
        "beta1T": on_partitions(a["L1_gnn_beta1"]), "g2": a["L1_gnn_g2"], "beta2": a["L1_gnn_beta2"],
    }


def kernel(**inputs):
    import numpy as np
    import concourse.bacc as bacc
    from concourse.bass_utils import run_bass_kernel_spmd

    nc = bacc.Bacc("TRN2", target_bir_lowering=False, num_devices=1)
    arrays, tensors = {}, {}
    laid_out = layouts({k: np.asarray(v) for k, v in inputs.items()})
    for name in _INS:
        a = np.ascontiguousarray(laid_out[name])
        arrays["in_" + name] = a
        tensors[name] = nc.dram_tensor("in_" + name, a.shape, mybir.dt.from_np(a.dtype), kind="ExternalInput").ap()
    shape = laid_out["x"].shape
    tensors["out"] = nc.dram_tensor("out_0", shape, F32, kind="ExternalOutput").ap()
    graph_kernel(nc, tensors)
    r = run_bass_kernel_spmd(nc, [arrays], core_ids=[0])
    return r.results[0]["out_0"]
```

```python
from contextlib import ExitStack

import concourse.bass as bass
from concourse import mybir

F32 = mybir.dt.float32
F32R = mybir.dt.float32r
BF16 = mybir.dt.bfloat16
I32 = mybir.dt.int32
ALU = mybir.AluOpType
ACT = mybir.ActivationFunctionType

P = 128
SLOPE = 0.2
EPS = 1e-5
MASKED = -1e30
LOWEST = -3e38


def graph_kernel(nc: bass.Bass, t):
    B, N, D = t["x"].shape
    HEADS, FH = t["att_src1"].shape
    L = t["attn_w"].shape[0]
    FF = t["ff_b1"].shape[1]
    NB = N // P
    DB = D // P
    FB = FF // P
    WCOLS = t["ff_w"].shape[2]
    W1_COLS = L * DB * FF
    assert FH == P and B % 2 == 0 and HEADS * P == N and t["ff_w"].shape[0] == B

    x1_dram = nc.dram_tensor("x1_scratch", (B, N, D), F32).ap()

    outer = ExitStack()
    with outer:
        def allocator(stack):
            def sb(name, shape, dt=F32):
                return stack.enter_context(nc.sbuf_tensor(name, shape, dt))
            return sb

        sb = allocator(outer)
        w_hi = sb("w_hi", [P, B * WCOLS], F32R)
        w_lo = sb("w_lo", [P, B * WCOLS], F32R)
        ident = sb("ident", [P, P])
        ones = sb("ones", [P, P])
        off_diag = sb("off_diag", [P, P], BF16)
        first_col = sb("first_col", [P, B * 2 * NB])
        setup_done = outer.enter_context(nc.semaphore("setup_done"))

        def w1(part, layer, k, c):
            at = (layer * DB + k) * FF + c * P
            return part[:, at:at + P]

        def w2(part, layer, c):
            at = W1_COLS + (layer * FB + c) * D
            return part[:, at:at + D]

        gat_pass(nc, t, x1_dram, allocator, w_hi, w_lo, ident, ones, off_diag, first_col, setup_done)
        transformer_pass(nc, t, x1_dram, allocator, w_hi, w_lo, w1, w2, ident, ones, off_diag, first_col)


def gat_pass(nc, t, x1_dram, allocator, w_hi, w_lo, ident, ones, off_diag, first_col, setup_done):
    B, N, D = t["x"].shape
    HEADS, FH = t["att_src1"].shape
    NB, DB, WCOLS = N // P, D // P, t["ff_w"].shape[2]
    HF = HEADS * FH
    TERMS = 2 * HEADS
    LO_AT = 32

    with ExitStack() as ctx:
        sb = allocator(ctx)

        def psum(name, shape, dt=F32):
            return ctx.enter_context(nc.psum_tensor(name, shape, dt))

        def sem(name):
            return ctx.enter_context(nc.semaphore(name))

        wg1 = sb("wg1", [P, DB, HF])
        wg2 = sb("wg2", [P, HEADS, D + 2])
        att1 = sb("att1", [P, 2, HF])
        att2 = sb("att2", [P, 2, D])
        bias1 = sb("bias1", [P, HEADS])
        bias2 = sb("bias2", [P, D])
        att0 = sb("att0", [P, 2, D])
        v1 = sb("v1", [P, DB, TERMS])
        scrap = sb("scrap_gat", [P, D])
        pick = sb("pick", [LO_AT + TERMS, TERMS], F32R)
        xT = sb("xT", [P, DB, N])
        x_in = sb("x_in", [P, NB, D])
        adj_in = sb("adj_in", [P, 2, N], I32)
        maskb = sb("maskb", [P, 2 * NB * N + NB * P], BF16)
        rows = sb("rows", [LO_AT + TERMS, N], F32R)
        xl = sb("xl", [P, NB, HF])
        hT = sb("hT", [P, HEADS, N])
        xl2 = sb("xl2", [P, NB, D + 2])
        res = sb("res", [P, NB, D])
        wt = sb("wt_gat", [P, 3, NB, N])
        wt_two = wt[:, 1]
        low = sb("low", [P, 2, N])
        wtT = sb("wtT", [P, NB, N])
        elu_t = sb("elu_t", [P, 2, N])
        w_stage = sb("w_stage", [P, WCOLS])
        dst1 = sb("dst1", [P, NB, HEADS])
        top = sb("top", [P, 3, NB])
        tmp = sb("tmp", [P, 3, NB])
        shift = sb("shift", [P, 3, NB])
        sh_hi = sb("sh_hi", [P, 3, NB])
        sh_lo = sb("sh_lo", [P, 3, NB])
        total = sb("total", [P, 3, NB])
        inv = sb("inv", [P, 3, NB])
        x1_col = sb("x1_col", [P, 2, NB])
        stats = sb("stats", [P, NB, 6])
        mv = sb("mv", [P, NB, 2])
        var = sb("var", [P, NB])
        rstd = sb("rstd", [P, NB])
        half = sb("half", [P, NB])

        mask = [maskb[:, a * NB * N:(a + 1) * NB * N].rearrange("p (i n) -> p i n", i=NB) for a in range(2)]
        mask_diag = [maskb[:, a * NB * N:a * NB * N + NB * (N + P)].rearrange("p (i n) -> p i n", i=NB)[:, :, 0:P]
                     for a in range(2)]

        def wt_head(h):
            return wt[:, (0, 2, 0, 1)[h]]

        ps_turn = psum("ps_turn", [P, 2, N])
        ps_row = psum("ps_row", [P, 2, N])
        ps_acc = psum("ps_acc", [P, 2, N])
        ps_two = psum("ps_two", [P, 2, N])
        ps_row2 = ps_two[:, 0]
        ps_dst = ps_two[:, 1, 0:NB * HEADS]

        s_first_in = sem("s_first_in")
        def turned_two(j):
            return (ps_turn[:, 0], ps_turn[:, 1], ps_two[:, 0], ps_two[:, 1])[j]

        s_const = sem("s_const")
        s_v = sem("s_v")
        s_zero = sem("s_zero")
        s_xT = sem("s_xT")
        s_x = sem("s_x")
        s_adj = [sem(f"s_adj{i}") for i in range(2)]
        s_wst = sem("s_wst")
        s_wsp = sem("s_wsp")
        s_mask = sem("s_mask")
        s_dst_ps = sem("s_dst_ps")
        s_dst = sem("s_dst")
        s_rows_ps = sem("s_rows_ps")
        s_rows_hi = sem("s_rows_hi")
        s_rows_lo = sem("s_rows_lo")
        s_row = sem("s_row")
        s_xl_ps = sem("s_xl_ps")
        s_xl = sem("s_xl")
        s_top = sem("s_top")
        s_shift = sem("s_shift")
        s_low = sem("s_low")
        s_arg = sem("s_arg")
        s_exp = sem("s_exp")
        s_inv = sem("s_inv")
        s_wt = sem("s_wt")
        s_turn = sem("s_turn")
        s_wtT = sem("s_wtT")
        s_mm = sem("s_mm")
        s_eluexp = sem("s_eluexp")
        s_elum = sem("s_elum")
        s_hT = sem("s_hT")
        s_xl2_ps = sem("s_xl2_ps")
        s_xl2 = sem("s_xl2")
        s_row2 = sem("s_row2")
        s_top2 = sem("s_top2")
        s_shift2 = sem("s_shift2")
        s_low2 = sem("s_low2")
        s_arg2 = sem("s_arg2")
        s_exp2 = sem("s_exp2")
        s_inv2 = sem("s_inv2")
        s_turn2 = sem("s_turn2")
        s_wtT2 = sem("s_wtT2")
        s_out2 = sem("s_out2")
        s_xb = sem("s_xb")
        s_res = sem("s_res")
        s_stats = sem("s_stats")
        s_mv = sem("s_mv")
        s_var = sem("s_var")
        s_rstd = sem("s_rstd")
        s_x1 = sem("s_x1")
        s_first = sem("s_first")
        s_kept = sem("s_kept")
        s_past = sem("s_past")
        s_past_pool = sem("s_past_pool")
        s_store = sem("s_store")

        block = ctx.enter_context(nc.Block())
        N_CONST = 6
        N_V1, N_V2 = 2 * DB * HEADS, 2 * HEADS
        FIRST, LAST = dict(two=False, heads=True, more=True), dict(two=True, heads=True, more=False)
        INNER, END = dict(two=True, heads=True, more=True), dict(two=True, heads=False, more=False)

        def turns(engine, turn):
            turn(0, 0, **FIRST)
            with engine.Fori(0, B // 2 - 1) as m:
                for a in (1, 0):
                    turn(2 * m + 2 - a, a, **INNER)
            turn(B - 1, 1, **LAST)
            turn(B, 0, **END)

        @block.sync
        def _(sp):
            def load_xT(b):
                sp.dma_start(xT[:], t["xT"][b].rearrange("(k p) n -> p k n", p=P)).then_inc(s_xT, 16)

            def load_adj(b, blocks, first=False):
                for i in blocks:
                    if i >= 2:
                        sp.wait_ge(s_mask, (NB + 1) * b + i - 1)
                    elif not first:
                        sp.wait_ge(s_mask, (NB + 1) * b - 2 + i)
                    sp.dma_start(adj_in[:, i % 2, :], t["adjT"][b, i * P:(i + 1) * P, :]).then_inc(s_adj[i % 2], 16)

            sp.dma_start(wg1[:], t["gat_w1"].rearrange("(k p) n -> p k n", p=P)).then_inc(s_first_in, 16)
            for j, name in enumerate(("att_src1", "att_dst1")):
                row = t[name].rearrange("h f -> (h f)")
                sp.dma_start(att1[:, j, :], row.partition_broadcast(P)).then_inc(s_first_in, 16)
            load_xT(0)
            load_adj(0, range(0, 2), first=True)
            sp.dma_start(bias1[:], t["gat_b1T"]).then_inc(s_const, 16)
            sp.dma_start(wg2[:, :, 0:D], t["gat_w2"].rearrange("(k p) n -> p k n", p=P)).then_inc(s_const, 16)
            for j, name in enumerate(("att_dst2", "att_src2")):
                row = t[name].rearrange("h f -> (h f)")
                sp.dma_start(att2[:, j, :], row.partition_broadcast(P)).then_inc(s_const, 16)
            sp.dma_start(bias2[:], t["gat_b2"].partition_broadcast(P)).then_inc(s_const, 16)
            sp.dma_start(att0[:].rearrange("p j d -> p (j d)"), t["attn_w"][0].partition_broadcast(P)).then_inc(s_const, 16)
            load_adj(0, range(2, NB))

            def turn(b, a, two, heads, more):
                if more:
                    load_adj(b + 1, range(0, 2))
                if more:
                    sp.wait_ge(s_xl_ps, NB * b + NB)
                    load_xT(b + 1)
                if heads:
                    if two:
                        sp.wait_ge(s_xb, b)
                    sp.dma_start(x_in[:], t["x"][b].rearrange("(i p) n -> p i n", p=P)).then_inc(s_x, 16)
                    if two:
                        sp.wait_ge(s_wsp, 2 * b)
                    sp.dma_start(w_stage[:], t["ff_w"][b]).then_inc(s_wst, 16)
                if more:
                    load_adj(b + 1, range(2, NB))
                if two:
                    sp.wait_ge(s_x1, NB * b)
                    sp.dma_start(x1_dram[b - 1].rearrange("(i p) n -> p i n", p=P), res[:]).then_inc(s_store, 16)

            turns(sp, turn)
            sp.wait_ge(s_store, 16 * B)

        @block.gpsimd
        def _(pool):
            nc.gpsimd.memset(ident[:], 0.0).then_inc(setup_done, 1)
            nc.gpsimd.memset(ones[:], 1.0).then_inc(setup_done, 1)
            nc.gpsimd.memset(off_diag[:], 1.0).then_inc(setup_done, 1)
            nc.gpsimd.memset(half[:], -0.5).then_inc(setup_done, 1)
            pool.wait_ge(setup_done, 4)
            nc.gpsimd.affine_select(out=ident[:], in_=ident[:], compare_op=ALU.not_equal, fill=1.0, base=0,
                                    pattern=[[-1, P]], channel_multiplier=1).then_inc(setup_done, 1)
            nc.gpsimd.affine_select(out=off_diag[:], in_=off_diag[:], compare_op=ALU.not_equal, fill=0.0, base=0,
                                    pattern=[[-1, P]], channel_multiplier=1).then_inc(setup_done, 1)

            def low_of(weights, j, i, slot, ready):
                pool.sem_inc(s_past_pool, 1)
                nc.gpsimd.tensor_scalar(low[:, slot, :], weights[:, i, :], SLOPE, sh_lo[:, j, i:i + 1],
                                        ALU.mult, ALU.add).then_inc(ready, 1)

            def low_head(b, h, two, first=False):
                g = HEADS * b + h
                pool.wait_ge(s_shift, 4 * g + 4)
                for i in range(NB):
                    if i >= 2:
                        pool.wait_ge(s_arg, NB * g + i - 1)
                    elif h == 2 and two:
                        pool.wait_ge(s_arg2, NB * b - 1 + i)
                    elif not first:
                        pool.wait_ge(s_arg, NB * g - 1 + i)
                    low_of(wt_head(h), h % 2, i, i % 2, s_low)

            def low_two(b, heads):
                pool.wait_ge(s_shift2, 4 * b + 4)
                for i in range(NB):
                    if i >= 2:
                        pool.wait_ge(s_arg2, NB * b + i - 1)
                    elif heads:
                        pool.wait_ge(s_arg, NB * (HEADS * (b + 1) + 2) - 1 + i)
                    low_of(wt_two, 2, i, i % 2, s_low2)

            def normalise(b, h):
                pool.wait_ge(s_inv, HEADS * b + h + 1)
                pool.sem_inc(s_past_pool, 1)
                for i in range(NB):
                    nc.gpsimd.tensor_scalar(wt_head(h)[:, i, :], wt_head(h)[:, i, :],
                                            inv[:, h % 2, i:i + 1], 1.0, ALU.mult, ALU.mult).then_inc(s_wt, 1)

            def split_weights(b):
                pool.wait_ge(s_wst, 16 * b + 16)
                nc.gpsimd.tensor_copy(w_hi[:, bass.ds(b * WCOLS, WCOLS)], w_stage[:]).then_inc(s_wsp, 1)
                pool.wait_ge(s_wsp, 2 * b + 1)
                nc.gpsimd.tensor_tensor(w_lo[:, bass.ds(b * WCOLS, WCOLS)], w_stage[:],
                                        w_hi[:, bass.ds(b * WCOLS, WCOLS)].bitcast(F32),
                                        ALU.subtract).then_inc(s_wsp, 1)

            def add_bias(b):
                pool.wait_ge(s_x, 16 * b + 16)
                nc.gpsimd.tensor_tensor(res[:], x_in[:], bias2[:].unsqueeze(1).to_broadcast([P, NB, D]),
                                        ALU.add).then_inc(s_xb, 1)

            def inverse_deviation(b):
                pool.wait_ge(s_var, b + 1)
                nc.gpsimd.tensor_tensor(rstd[:], var[:], half[:], ALU.pow).then_inc(s_rstd, 1)

            def turn(b, a, two, heads, more, stored=True):
                if heads:
                    normalise(b, 0)
                    low_head(b, 1, two)
                if two:
                    low_two(b - 1, heads)
                if heads:
                    normalise(b, 1)
                    low_head(b, 2, two)
                if two:
                    if stored:
                        pool.wait_ge(s_store, 16 * (b - 1))
                        pool.wait_ge(s_first, 2 * NB * (b - 1))
                    add_bias(b - 1)
                if heads:
                    low_head(b, 3, two)
                    normalise(b, 2)
                if two:
                    inverse_deviation(b - 1)
                if heads:
                    normalise(b, 3)
                    split_weights(b)
                if more:
                    low_head(b + 1, 0, two)

            low_head(0, 0, False, first=True)
            turn(0, 0, **FIRST)
            pool.wait_ge(s_const, 16 * N_CONST)
            turn(1, 1, **INNER, stored=False)
            with pool.Fori(2, B - 1) as b:
                turn(b, 0, **INNER)
            turn(B - 1, 1, **LAST)
            turn(B, 0, **END)

        @block.vector
        def _(dve):
            nc.vector.memset(rows[:].bitcast(F32), 0.0).then_inc(s_zero, 1)
            nc.vector.memset(pick[:].bitcast(F32), 0.0).then_inc(s_zero, 1)
            dve.wait_ge(setup_done, 6)
            dve.wait_ge(s_zero, 2)
            for at in (0, LO_AT):
                nc.vector.tensor_copy(pick[at:at + TERMS, :], ident[at:at + TERMS, at:at + TERMS]).then_inc(s_zero, 1)

            def dot_products(products, n):
                for out, weights, att in products:
                    if n:
                        dve.wait_ge(s_v, n)
                    nc.vector.tensor_tensor_reduce(out=scrap[:, 0:att.shape[-1]], in0=weights, in1=att, scale=1.0,
                                                   scalar=0.0, op0=ALU.mult, op1=ALU.add, accum_out=out).then_inc(s_v, 1)
                    n += 1

            dve.wait_ge(s_first_in, 16 * 3)
            dot_products([(v1[:, k, j * HEADS + h:j * HEADS + h + 1], wg1[:, k, h * FH:(h + 1) * FH], att1[:, j, h * FH:(h + 1) * FH])
                          for j in range(2) for k in range(DB) for h in range(HEADS)], 0)

            def make_mask(b, a, blocks):
                for i in blocks:
                    dve.wait_ge(s_adj[i % 2], 16 * (NB // 2 * b + i // 2 + 1))
                    nc.vector.tensor_scalar(mask[a][:, i, :], adj_in[:, i % 2, :], 0, MASKED, ALU.is_le, ALU.mult)\
                        .then_inc(s_mask, 1)

            def clear_diagonal(b, a):
                dve.wait_ge(s_mask, (NB + 1) * b + NB)
                nc.vector.tensor_tensor(mask_diag[a], mask_diag[a], off_diag[:].unsqueeze(1).to_broadcast([P, NB, P]),
                                        ALU.mult).then_inc(s_mask, 1)

            def keep_rows(b):
                dve.wait_ge(s_rows_hi, b + 1)
                nc.vector.tensor_tensor(rows[LO_AT:LO_AT + TERMS, :], ps_row[0:TERMS, 0, :],
                                        rows[0:TERMS, :].bitcast(F32), ALU.subtract).then_inc(s_rows_lo, 1)

            def keep_destination(b):
                dve.wait_ge(s_dst_ps, b + 1)
                nc.vector.tensor_copy(dst1[:], ps_dst.rearrange("p (i h) -> p i h", i=NB)).then_inc(s_dst, 1)

            def biased(row, weights, j, a, i, done):
                nc.vector.tensor_tensor_reduce(out=weights[:, i, :], in0=row, in1=mask[a][:, i, :], scale=1.0,
                                               scalar=LOWEST, op0=ALU.add, op1=ALU.max,
                                               accum_out=top[:, j, i:i + 1]).then_inc(done, 1)

            def shifts(query, j, sem, at):
                nc.vector.tensor_tensor(tmp[:, j, :], top[:, j, :], query, ALU.add).then_inc(sem, 1)
                dve.wait_ge(sem, at + 1)
                nc.vector.scalar_tensor_tensor(out=shift[:, j, :], in0=tmp[:, j, :], scalar=SLOPE, in1=tmp[:, j, :],
                                               op0=ALU.mult, op1=ALU.max).then_inc(sem, 1)
                dve.wait_ge(sem, at + 2)
                nc.vector.scalar_tensor_tensor(out=sh_lo[:, j, :], in0=query, scalar=SLOPE, in1=shift[:, j, :],
                                               op0=ALU.mult, op1=ALU.subtract).then_inc(sem, 1)
                nc.vector.tensor_tensor(sh_hi[:, j, :], query, shift[:, j, :], ALU.subtract).then_inc(sem, 1)

            def exponents(weights, j, i, slot, done):
                nc.vector.scalar_tensor_tensor(out=weights[:, i, :], in0=weights[:, i, :], scalar=sh_hi[:, j, i:i + 1],
                                               in1=low[:, slot, :], op0=ALU.add, op1=ALU.max).then_inc(done, 1)

            def prepare_head(b, a, h, two, first=False):
                g = HEADS * b + h
                dve.wait_ge(s_row, g + 1)
                if h == 0:
                    dve.wait_ge(s_mask, (NB + 1) * (b + 1))
                if h == 0 and not first:
                    dve.wait_ge(s_turn, NB * (g - 1))
                elif h == 1 and two:
                    dve.wait_ge(s_turn, NB * (g - HEADS + 1))
                elif h == 2:
                    dve.wait_ge(s_turn, NB * (g - 1))
                elif h == 3 and two:
                    dve.wait_ge(s_turn2, NB * b)
                dve.sem_inc(s_past, 1)
                for i in range(NB):
                    biased(ps_row[:, h % 2, :], wt_head(h), h % 2, a, i, s_top)
                if h == 0:
                    keep_destination(b)
                    dve.wait_ge(s_dst, b + 1)
                dve.wait_ge(s_top, NB * g + NB)
                shifts(dst1[:, :, h], h % 2, s_shift, 4 * g)

            def exponents_head(b, h, blocks=range(NB)):
                g = HEADS * b + h
                dve.wait_ge(s_shift, 4 * g + 4)
                for i in blocks:
                    dve.wait_ge(s_low, NB * g + i + 1)
                    exponents(wt_head(h), h % 2, i, i % 2, s_arg)

            def invert_head(b, h):
                g = HEADS * b + h
                dve.wait_ge(s_exp, NB * g + NB)
                if h == 3:
                    dve.wait_ge(s_wt, NB * (g - 1))
                nc.vector.reciprocal(inv[:, h % 2, :], total[:, h % 2, :]).then_inc(s_inv, 1)

            def elu(b, h):
                g = HEADS * b + h
                dve.wait_ge(s_eluexp, g + 1)
                nc.vector.tensor_scalar(elu_t[:, h % 2, :], elu_t[:, h % 2, :], 1.0, -1.0, ALU.min, ALU.add)\
                    .then_inc(s_elum, 1)
                dve.wait_ge(s_elum, g + 1)
                nc.vector.scalar_tensor_tensor(out=hT[:, h, :], in0=ps_acc[:, h % 2, :], scalar=bias1[:, h:h + 1],
                                               in1=elu_t[:, h % 2, :], op0=ALU.add, op1=ALU.max).then_inc(s_hT, 1)

            def biased_two(b, a):
                dve.wait_ge(s_row2, b + 1)
                dve.sem_inc(s_past, 1)
                for i in range(NB):
                    biased(ps_row2, wt_two, 2, a, i, s_top2)

            def shifts_two(b):
                dve.wait_ge(s_top2, NB * (b + 1))
                dve.wait_ge(s_xl2, NB * (b + 1))
                shifts(xl2[:, :, D], 2, s_shift2, 4 * b)

            def exponents_two(b):
                dve.wait_ge(s_shift2, 4 * b + 4)
                for i in range(NB):
                    dve.wait_ge(s_low2, NB * b + i + 1)
                    exponents(wt_two, 2, i, i % 2, s_arg2)

            def norm(b):
                dve.wait_ge(s_exp2, NB * (b + 1))
                nc.vector.reciprocal(inv[:, 2, :], total[:, 2, :]).then_inc(s_inv2, 1)
                dve.wait_ge(s_inv2, b + 1)
                dve.wait_ge(s_xb, b + 1)
                for i in range(NB):
                    if i % 2 == 0:
                        dve.wait_ge(s_out2, NB * b + i + 2)
                    nc.vector.scalar_tensor_tensor(out=res[:, i, :], in0=ps_two[:, i // 2, (i % 2) * D:(i % 2 + 1) * D],
                                                   scalar=inv[:, 2, i:i + 1], in1=res[:, i, :],
                                                   op0=ALU.mult, op1=ALU.add).then_inc(s_res, 1)
                for i in range(NB):
                    dve.wait_ge(s_res, NB * b + i + 1)
                    nc.vector.bn_stats(stats[:, i, :], res[:, i, :]).then_inc(s_stats, 1)
                for i in range(NB):
                    dve.wait_ge(s_stats, NB * b + i + 1)
                    dve.sem_inc(s_past, 1)
                    nc.vector.bn_aggr(mv[:, i, :], stats[:, i, :]).then_inc(s_mv, 1)
                dve.wait_ge(s_mv, NB * (b + 1))
                nc.vector.tensor_scalar(var[:], mv[:, :, 1], EPS, None, ALU.add).then_inc(s_var, 1)

            def norm_end(b):
                dve.wait_ge(s_rstd, b + 1)
                for i in range(NB):
                    nc.vector.tensor_scalar(res[:, i, :], res[:, i, :], mv[:, i, 0:1], rstd[:, i:i + 1],
                                            ALU.subtract, ALU.mult).then_inc(s_x1, 1)

            def first_terms(b):
                for i in range(NB):
                    dve.wait_ge(s_x1, NB * b + i + 1)
                    for j in range(2):
                        if i or j:
                            dve.wait_ge(s_first, 2 * NB * b + 2 * i + j)
                        nc.vector.tensor_tensor_reduce(out=scrap[:], in0=res[:, i, :], in1=att0[:, j, :], scale=1.0,
                                                       scalar=0.0, op0=ALU.mult, op1=ALU.add,
                                                       accum_out=x1_col[:, j, i:i + 1]).then_inc(s_first, 1)
                dve.wait_ge(s_first, 2 * NB * (b + 1))
                nc.vector.tensor_copy(first_col[:, bass.ds(2 * NB * b, 2 * NB)], x1_col[:].rearrange("p j i -> p (j i)"))\
                    .then_inc(s_kept, 1)

            def turn(b, a, two, heads, more):
                if two:
                    biased_two(b - 1, 1 - a)
                if heads:
                    invert_head(b, 0)
                    prepare_head(b, a, 1, two)
                    exponents_head(b, 1)
                if not two:
                    dve.wait_ge(s_const, 16 * N_CONST)
                    dot_products([(wg2[:, h, D + j:D + j + 1], wg2[:, h, 0:D], att2[:, j, :])
                                  for j in range(2) for h in range(HEADS)], N_V1)
                if two:
                    shifts_two(b - 1)
                    exponents_two(b - 1)
                if heads:
                    invert_head(b, 1)
                    prepare_head(b, a, 2, two)
                    exponents_head(b, 2)
                    elu(b, 0)
                    prepare_head(b, a, 3, two)
                    invert_head(b, 2)
                    exponents_head(b, 3)
                if two:
                    norm(b - 1)
                if heads:
                    invert_head(b, 3)
                if more:
                    make_mask(b + 1, 1 - a, range(0, 2))
                    keep_rows(b + 1)
                if two:
                    norm_end(b - 1)
                if heads:
                    elu(b, 1)
                if more:
                    make_mask(b + 1, 1 - a, range(2, NB))
                    clear_diagonal(b + 1, 1 - a)
                if two:
                    first_terms(b - 1)
                if more:
                    prepare_head(b + 1, 1 - a, 0, two)
                if heads:
                    elu(b, 2)
                if more:
                    exponents_head(b + 1, 0, range(0, 2))
                if heads:
                    elu(b, 3)
                if more:
                    exponents_head(b + 1, 0, range(2, NB))

            keep_rows(0)
            make_mask(0, 0, range(NB))
            clear_diagonal(0, 0)
            prepare_head(0, 0, 0, False, first=True)
            exponents_head(0, 0)
            turns(dve, turn)

        @block.scalar
        def _(act):
            def keep_row_parts(b):
                act.wait_ge(s_rows_ps, b + 1)
                nc.scalar.copy(rows[0:TERMS, :], ps_row[0:TERMS, 0, :]).then_inc(s_rows_hi, 1)

            def keep_xl(b, i, two):
                act.wait_ge(s_xl_ps, NB * b + i + 1)
                if i == 0 and two:
                    act.wait_ge(s_mm, NB * HEADS * b)
                nc.scalar.copy(xl[:, i, :], ps_acc[:, i % 2, :]).then_inc(s_xl, 1)

            def keep_xl2(b, i):
                act.wait_ge(s_xl2_ps, NB * b + i + 1)
                nc.scalar.copy(xl2[:, i, :], ps_acc[:, (i + 1) % 2, 0:D + 2]).then_inc(s_xl2, 1)

            def exp_block(weights, j, i, done):
                nc.scalar.activation(weights[:, i, :], weights[:, i, :], ACT.Exp,
                                     accum_out=total[:, j, i:i + 1]).then_inc(done, 1)

            def exp_head(b, h, i):
                act.wait_ge(s_arg, NB * (HEADS * b + h) + i + 1)
                exp_block(wt_head(h), h % 2, i, s_exp)

            def exp_two(b, i):
                act.wait_ge(s_arg2, NB * b + i + 1)
                exp_block(wt_two, 2, i, s_exp2)

            def keep_turned(b, h, i, two):
                g = HEADS * b + h
                act.wait_ge(s_turn, NB * g + i + 1)
                if h == 1 and two:
                    act.wait_ge(s_out2, NB * b)
                elif h or two:
                    act.wait_ge(s_mm, NB * (g - 1) + i + 1)
                nc.scalar.copy(wtT[:, i, :], ps_turn[:, i % 2, :]).then_inc(s_wtT, 1)

            def keep_turned_two(b, i, heads):
                if heads:
                    act.wait_ge(s_mm, NB * HEADS * (b + 1) + i + 1)
                act.wait_ge(s_turn2, NB * b + i + 1)
                nc.scalar.copy(wtT[:, i, :], turned_two(i)).then_inc(s_wtT2, 1)

            def elu_exp(b, h, two):
                g = HEADS * b + h
                act.wait_ge(s_mm, NB * (g + 1))
                if h >= 2 or two:
                    act.wait_ge(s_hT, g - 1)
                nc.scalar.activation(elu_t[:, h % 2, :], ps_acc[:, h % 2, :], ACT.Exp,
                                     bias=bias1[:, h:h + 1]).then_inc(s_eluexp, 1)

            def turn(b, a, two, heads, more):
                if two:
                    elu_exp(b - 1, 3, two)
                if heads:
                    keep_xl(b, 0, two)
                    for i in range(NB):
                        exp_head(b, 0, i)
                if two:
                    for i in range(NB):
                        keep_xl2(b - 1, i)
                if heads:
                    keep_xl(b, 1, two)
                    exp_head(b, 1, 0)
                    keep_xl(b, 2, two)
                    exp_head(b, 1, 1)
                    exp_head(b, 1, 2)
                    keep_turned(b, 0, 0, two)
                    keep_turned(b, 0, 1, two)
                    keep_xl(b, 3, two)
                    exp_head(b, 1, 3)
                for i in range(NB):
                    if two:
                        exp_two(b - 1, i)
                    if heads and i < 2:
                        keep_turned(b, 0, i + 2, two)
                if not two:
                    act.wait_ge(s_const, 16 * N_CONST)
                if heads:
                    elu_exp(b, 0, two)
                if two:
                    for i in range(NB):
                        keep_turned_two(b - 1, i, heads)
                if heads:
                    for i in range(NB):
                        exp_head(b, 2, i)
                    keep_turned(b, 1, 0, two)
                    for i in range(1, NB):
                        keep_turned(b, 1, i, two)
                        exp_head(b, 3, i - 1)
                    exp_head(b, 3, NB - 1)
                if more:
                    keep_row_parts(b + 1)
                if heads:
                    elu_exp(b, 1, two)
                    for i in range(NB):
                        keep_turned(b, 2, i, two)
                    elu_exp(b, 2, two)
                    for i in range(NB):
                        keep_turned(b, 3, i, two)

            keep_row_parts(0)
            turns(act, turn)

        @block.tensor
        def _(pe):
            pe.wait_ge(s_v, N_V1)

            def row_terms(b, first=False):
                pe.wait_ge(s_xT, 16 * b + 16)
                if not first:
                    pe.wait_ge(s_top, NB * (HEADS * b - 1))
                for k in range(DB):
                    mm = nc.tensor.matmul(ps_row[0:TERMS, 0, :], v1[:, k, :], xT[:, k, :],
                                          start=(k == 0), stop=(k == DB - 1))
                mm.then_inc(s_rows_ps, 1)

            def destination_terms(b, two, first=False):
                pe.wait_ge(s_rows_lo, b + 1)
                if two:
                    pe.wait_ge(s_res, NB * (b - 1))
                elif not first:
                    pe.wait_ge(s_dst, b)
                for i in range(NB):
                    mm = nc.tensor.matmul(ps_dst[:, HEADS * i:HEADS * (i + 1)], rows[:, i * P:(i + 1) * P],
                                          pick[:, HEADS:TERMS], start=True, stop=True)
                mm.then_inc(s_dst_ps, 1)

            def head_row(b, h, first=False):
                g = HEADS * b + h
                if h == 0:
                    pe.wait_ge(s_rows_lo, b + 1)
                elif h > 1 or not first:
                    pe.wait_ge(s_top, NB * (g - 1))
                nc.tensor.matmul(ps_row[:, h % 2, :], pick[:, h:h + 1].to_broadcast([LO_AT + TERMS, P]), rows[:],
                                 start=True, stop=True).then_inc(s_row, 1)

            def project(b, i, two):
                if two:
                    if i == 0:
                        pe.wait_ge(s_hT, HEADS * b - 1)
                    elif i < 3:
                        pe.wait_ge(s_xl2, NB * b - 2 + i)
                    else:
                        pe.wait_ge(s_xl, NB * b + i - 1)
                elif i >= 2:
                    pe.wait_ge(s_xl, NB * b + i - 1)
                for k in range(DB):
                    mm = nc.tensor.matmul(ps_acc[:, i % 2, :], xT[:, k, i * P:(i + 1) * P], wg1[:, k, :],
                                          start=(k == 0), stop=(k == DB - 1))
                mm.then_inc(s_xl_ps, 1)

            def row_two(b, h, two):
                pe.wait_ge(s_hT, HEADS * b + h + 1)
                if h == 0 and two:
                    pe.wait_ge(s_res, NB * b - 2)
                mm = nc.tensor.matmul(ps_row2, wg2[:, h, D + 1:D + 2].to_broadcast([P, P]), hT[:, h, :],
                                      start=(h == 0), stop=(h == HEADS - 1))
                if h == HEADS - 1:
                    mm.then_inc(s_row2, 1)

            def project_two(b, heads):
                for i in range(NB):
                    if i >= 2:
                        pe.wait_ge(s_xl2, NB * b + i - 1)
                    elif i == 1 and heads:
                        pe.wait_ge(s_xl, NB * (b + 1) + 1)
                    for h in range(HEADS):
                        mm = nc.tensor.matmul(ps_acc[:, (i + 1) % 2, 0:D + 2], hT[:, h, i * P:(i + 1) * P], wg2[:, h, :],
                                              start=(h == 0), stop=(h == HEADS - 1))
                    mm.then_inc(s_xl2_ps, 1)

            def turn_tile(weights, j, out, done):
                for i in range(NB):
                    mm = nc.tensor.transpose(out[:, i * P:(i + 1) * P], weights[:, i, j * P:(j + 1) * P],
                                             ident[:])
                mm.then_inc(done, 1)

            def layer_two(b, heads):
                pe.wait_ge(s_exp2, NB * (b + 1))
                for j in range(NB):
                    if j == 2:
                        pe.wait_ge(s_top2, NB * (b + 1))
                    elif j < 2 and heads:
                        pe.wait_ge(s_wtT, NB * HEADS * (b + 1) + 3 + j)
                    turn_tile(wt_two, j, turned_two(j), s_turn2)
                pe.wait_ge(s_wtT2, NB * (b + 1))
                for i in range(NB):
                    for j in range(NB):
                        mm = nc.tensor.matmul(ps_two[:, i // 2, (i % 2) * D:(i % 2 + 1) * D],
                                              wtT[:, j, i * P:(i + 1) * P], xl2[:, j, 0:D],
                                              start=(j == 0), stop=(j == NB - 1))
                    mm.then_inc(s_out2, 1)

            def head(b, h, two, meanwhile=()):
                g = HEADS * b + h
                pe.wait_ge(s_wt, NB * (g + 1))

                def turn_j(j):
                    if j >= 2:
                        pe.wait_ge(s_wtT, NB * g + j - 1)
                    elif h == 1 and two:
                        pe.wait_ge(s_wtT2, NB * (b - 1) + j + 1)
                    elif h or two:
                        pe.wait_ge(s_wtT, NB * g - 1 + j)
                    turn_tile(wt_head(h), j, ps_turn[:, j % 2], s_turn)

                turn_j(0)
                turn_j(1)
                for work in meanwhile:
                    work()
                if h >= 2:
                    pe.wait_ge(s_hT, g - 1)
                for j in range(NB):
                    if h == 0:
                        pe.wait_ge(s_xl, NB * b + max(j + 1, 3))
                    pe.wait_ge(s_wtT, NB * g + j + 1)
                    nc.tensor.matmul(ps_acc[:, h % 2, :], xl[:, j, h * FH:(h + 1) * FH], wtT[:, j, :],
                                     start=(j == 0), stop=(j == NB - 1)).then_inc(s_mm, 1)
                    if j + 2 < NB:
                        turn_j(j + 2)

            def turn(b, a, two, heads, more):
                if heads:
                    head_row(b, 2)
                    project(b, 0, two)
                if two:
                    row_two(b - 1, 3, two)
                    project_two(b - 1, heads)
                if heads:
                    for i in range(1, NB - 1):
                        project(b, i, two)
                    head(b, 0, two, [lambda: project(b, NB - 1, two)])
                    head_row(b, 3)
                if two:
                    layer_two(b - 1, heads)
                if heads:
                    head(b, 1, two, [lambda: row_terms(b + 1)] if more else [])
                    if not two:
                        pe.wait_ge(s_v, N_V1 + N_V2)
                    head(b, 2, two, [lambda: row_two(b, 0, two)])
                    if more:
                        head_row(b + 1, 0)
                        destination_terms(b + 1, two)
                    head(b, 3, two, [lambda: row_two(b, 1, two)])
                if more:
                    head_row(b + 1, 1)
                if heads:
                    row_two(b, 2, two)

            row_terms(0, first=True)
            pe.wait_ge(s_zero, 4)
            destination_terms(0, False, first=True)
            head_row(0, 0)
            head_row(0, 1, first=True)
            pe.wait_ge(setup_done, 6)
            turns(pe, turn)


def transformer_pass(nc, t, x1_dram, allocator, w_hi, w_lo, w1, w2, ident, ones, off_diag, first_col):
    B, N, D = t["x"].shape
    L, FF = t["ff_b1"].shape
    NB, DB, FB = N // P, D // P, FF // P
    STEPS = 2 * L
    TURNS = B // 2
    ROW_AT = 5

    def thread(s):
        return s % 2

    def layer(s):
        return s % STEPS // 2

    def normed(n, s):
        return (STEPS - 2) * (n + s // STEPS) + s % STEPS

    with ExitStack() as ctx:
        sb = allocator(ctx)

        def psum(name, shape, dt=F32):
            return ctx.enter_context(nc.psum_tensor(name, shape, dt))

        def sem(name):
            return ctx.enter_context(nc.semaphore(name))

        att_w = sb("att_w", [P, L, 2, D])
        att_b = sb("att_b", [P, L])
        beta_w = sb("beta_w", [P, L - 1, 2])
        g1r = sb("g1r", [P, L, D])
        b1r = sb("b1r", [P, L, D])
        g2r = sb("g2r", [P, L, D])
        b2r = sb("b2r", [P, L, D])
        g1c = sb("g1c", [P, L * DB])
        b1c = sb("b1c", [P, L * DB])
        ffb = sb("ffb", [P, L * FB])
        x = sb("x_state", [P, 2, NB, D])
        maskb = sb("mask_bias", [P, 2 * NB * N + NB * P], BF16)
        fin = sb("fin", [P, 2, NB, D])
        adj_in = sb("adj_blocks", [P, 2, N], I32)
        wt = sb("wt", [P, NB, N])
        wtT = sb("wt_turned", [P, NB, N])
        low = wtT
        diag = sb("diag", [P, NB, P])
        h_hi = sb("h_hi", [P, DB, N], F32R)
        h_lo = sb("h_lo", [P, DB, N], F32R)
        whole = sb("whole", [P, 2, N])
        g_hi = sb("g_hi", [P, FB, N], F32R)
        g_lo = sb("g_lo", [P, FB, N], F32R)
        col = sb("col", [P, 2, 2, NB])
        query = sb("query", [P, NB])
        top = sb("top_q", [P, NB])
        tmp = sb("tmp_q", [P, NB])
        shift = sb("shift_q", [P, NB])
        sh_hi = sb("sh_hi_q", [P, NB])
        sh_lo = sb("sh_lo_q", [P, NB])
        total = sb("total_q", [P, NB])
        inv = sb("inv_q", [P, NB])
        stats = sb("stats_q", [P, 3, NB, 6])
        mv = sb("mv_q", [P, 3, NB, 2])
        var = sb("var_q", [P, 3, NB])
        rstd = sb("rstd_q", [P, 3, NB])
        half = sb("half_q", [P, NB])

        b2_in = fin[:, 1].rearrange("p i d -> p (i d)")[:, 0:L * D]
        sums = wt[:, 0:2, :].rearrange("p i n -> p (i n)").rearrange("p (i n) -> p i n", i=NB)
        scrap = diag[:, NB - D // P:NB, :].rearrange("p i n -> p (i n)")
        mask = [maskb[:, a * NB * N:(a + 1) * NB * N].rearrange("p (i n) -> p i n", i=NB) for a in range(2)]
        mask_diag = [maskb[:, a * NB * N:a * NB * N + NB * (N + P)].rearrange("p (i n) -> p i n", i=NB)[:, :, 0:P]
                     for a in range(2)]

        ps_ff = psum("ps_ff", [P, 2, N])
        ps_y = psum("ps_y", [P, 2, N])
        ps_agg = psum("ps_agg", [P, 2, N])
        ps_turn = psum("ps_turned", [P, 2, N])

        def ff_bank(c):
            return (ps_ff[:, 0], ps_ff[:, 1], ps_turn[:, 1])[c % 3]

        q_small = sem("q_small")
        q_const = sem("q_const")
        q_half = sem("q_half")
        q_b1r = sem("q_b1r")
        q_beta_w = sem("q_beta_w")
        q_att_w = sem("q_att_w")
        q_x = [sem(f"q_x{a}") for a in range(2)]
        q_adj = [sem(f"q_adj{i}") for i in range(2)]
        q_fin = [sem(f"q_fin{a}") for a in range(2)]
        q_mask = sem("q_mask")
        q_dot = sem("q_dot")
        q_first = sem("q_first")
        q_diag = sem("q_diag")
        q_query = sem("q_query")
        q_row = sem("q_row")
        q_top = sem("q_top")
        q_shift = sem("q_shift")
        q_low = sem("q_low")
        q_arg = sem("q_arg")
        q_exp = sem("q_exp")
        q_inv = sem("q_inv")
        q_turn = sem("q_turn")
        q_wtT = sem("q_wtT")
        q_agg = sem("q_agg")
        q_r1 = sem("q_r1")
        q_st1 = sem("q_st1")
        q_mv1 = sem("q_mv1")
        q_var1 = sem("q_var1")
        q_rstd1 = sem("q_rstd1")
        q_n1 = sem("q_n1")
        q_nT = sem("q_nT")
        q_whole = sem("q_whole")
        q_hhi = sem("q_hhi")
        q_hlo = sem("q_hlo")
        q_h = sem("q_h")
        q_ff = sem("q_ff")
        q_gelu = sem("q_gelu")
        q_glo = sem("q_glo")
        q_y = sem("q_y")
        q_r2 = sem("q_r2")
        q_st2 = sem("q_st2")
        q_mv2 = sem("q_mv2")
        q_var2 = sem("q_var2")
        q_rstd2 = sem("q_rstd2")
        q_n2 = sem("q_n2")
        q_next = sem("q_next")
        q_last = [sem(f"q_last{f}") for f in range(2)]
        q_r3 = [sem(f"q_r3_{f}") for f in range(2)]
        q_st3 = sem("q_st3")
        q_mv3 = sem("q_mv3")
        q_var3 = sem("q_var3")
        q_rstd3 = sem("q_rstd3")
        q_out = sem("q_out")
        q_past = sem("q_past")
        q_store = sem("q_store")

        block = ctx.enter_context(nc.Block())
        SMALL, VECTORS = 4, 6

        @block.sync
        def _(sp):
            def load_x(b, a):
                sp.dma_start(x[:, a], x1_dram[b].rearrange("(i p) n -> p i n", p=P)).then_inc(q_x[a], 16)

            def load_adj(b, blocks, first=False):
                for i in blocks:
                    if i >= 2:
                        sp.wait_ge(q_mask, (NB + 1) * b + i - 1)
                    elif not first:
                        sp.wait_ge(q_mask, (NB + 1) * b - 2 + i)
                    sp.dma_start(adj_in[:, i % 2, :], t["adj"][b, i * P:(i + 1) * P, :])\
                        .then_inc(q_adj[i % 2], 16)

            def load_fin(b, a):
                sp.dma_start(fin[:, a], x1_dram[b].rearrange("(i p) n -> p i n", p=P)).then_inc(q_fin[a], 16)

            def store(b, a):
                sp.wait_ge(q_out, NB * b + NB)
                sp.dma_start(t["out"][b].rearrange("(i p) n -> p i n", p=P), fin[:, a]).then_inc(q_store, 16)

            def next_x(b, a):
                sp.wait_ge(q_r3[0], b + 1)
                sp.wait_ge(q_r3[1], b + 1)
                load_x(b + 2, a)

            def next_fin(b, a):
                sp.wait_ge(q_store, 16 * (b + 1))
                load_fin(b + 2, a)

            def turn(n, last):
                b = 2 * n
                if not last:
                    load_adj(b + 2, range(NB))
                    next_x(b, 0)
                    load_adj(b + 3, range(NB))
                store(b, 0)
                if not last:
                    next_fin(b, 0)
                    next_x(b + 1, 1)
                store(b + 1, 1)
                if not last:
                    next_fin(b + 1, 1)

            load_adj(0, range(0, 2), first=True)
            sp.dma_start(att_b[:], t["attn_b"].partition_broadcast(P)).then_inc(q_small, 16)
            for dst, name in ((g1c, "g1T"), (b1c, "beta1T"), (ffb, "ff_b1T")):
                sp.dma_start(dst[:], t[name]).then_inc(q_small, 16)
            load_x(0, 0)
            load_adj(0, range(2, NB))
            for dst, name in ((b1r, "beta1"), (g1r, "g1"), (g2r, "g2"), (b2r, "beta2")):
                sp.dma_start(dst[:].rearrange("p l d -> p (l d)"),
                             t[name].rearrange("l d -> (l d)").partition_broadcast(P)).then_inc(q_const, 16)
            sp.dma_start(b2_in, t["ff_b2"].rearrange("l d -> (l d)").partition_broadcast(P)).then_inc(q_const, 16)
            sp.dma_start(att_w[:].rearrange("p l j d -> p (l j d)"),
                         t["attn_w"].rearrange("l d -> (l d)").partition_broadcast(P)).then_inc(q_const, 16)
            load_x(1, 1)
            load_adj(1, range(NB))
            load_fin(0, 0)
            sp.wait_ge(q_b1r, 1)
            load_fin(1, 1)
            with sp.Fori(0, TURNS - 1) as n:
                turn(n, False)
            turn(TURNS - 1, True)
            sp.wait_ge(q_store, 16 * B)

        @block.gpsimd
        def _(pool):
            nc.gpsimd.memset(half[:], -0.5).then_inc(q_half, 1)
            pool.wait_ge(q_half, 1)

            def gelu_lo(q, c):
                pool.wait_ge(q_gelu, 2 * (FB * q + c + 1))
                nc.gpsimd.tensor_tensor(g_lo[:, c, :], whole[:, c % 2, :], g_hi[:, c, :].bitcast(F32),
                                        ALU.subtract).then_inc(q_glo, 1)

            def inverse_deviation(which, cols, ready, value, done):
                pool.wait_ge(ready, value)
                nc.gpsimd.tensor_tensor(rstd[:, which, cols], var[:, which, cols], half[:, cols], ALU.pow)\
                    .then_inc(done, 1)

            def affine(a, l, f, gains, shifts, done, before, data=None):
                rows = x[:, a, 2 * f:2 * f + 2, :]
                data = rows if data is None else data
                nc.gpsimd.tensor_tensor(rows, data, gains[:, l:l + 1, :].to_broadcast([P, 2, D]), ALU.mult)\
                    .then_inc(done, 1)
                pool.wait_ge(done, before + 1)
                nc.gpsimd.tensor_tensor(rows, rows, shifts[:, l:l + 1, :].to_broadcast([P, 2, D]), ALU.add)\
                    .then_inc(done, 1)

            def residual_h(q, s, f):
                pool.wait_ge(q_nT, 2 * q + f + 1)
                affine(thread(s), layer(s), f, g1r, b1r, q_h, 4 * q + 2 * f, None if f else sums[:, 0:2, :])

            def next_x(n, s, f):
                k = normed(n, s)
                pool.wait_ge(q_dot, 2 * NB * k + NB * (f + 1))
                affine(thread(s), layer(s), f, g2r, b2r, q_next, 4 * k + 2 * f)

            def last_x(q, n, s, b):
                a, rows = thread(s), slice(0, 2)
                pool.wait_ge(q_n2, NB * q + 2)
                affine(a, layer(s), 0, g2r, b2r, q_last[0], 2 * b)
                pool.wait_ge(q_last[0], 2 * b + 2)
                pool.wait_ge(q_fin[a], 16 * (n + 1))
                nc.gpsimd.tensor_tensor(fin[:, a, rows, :], fin[:, a, rows, :], x[:, a, rows, :], ALU.add)\
                    .then_inc(q_r3[0], 1)

            def turn(n, first, last):
                first_half, second_half, all_nodes = slice(0, 2), slice(2, NB), slice(0, NB)
                for s in range(STEPS):
                    q, b = STEPS * n + s, 2 * n + thread(s)
                    more = not (last and s == STEPS - 1)
                    if s or not first:
                        inverse_deviation(1, second_half, q_var2, 2 * q, q_rstd2)
                    for c in range(FB):
                        gelu_lo(q, c)
                    if s and layer(s - 1) < L - 1:
                        next_x(n, s - 1, 1)
                    residual_h(q, s, 1)
                    if s == STEPS - 1 or s == 0 and not first:
                        inverse_deviation(2, all_nodes, q_var3, b, q_rstd3)
                    inverse_deviation(1, first_half, q_var2, 2 * q + 1, q_rstd2)
                    if layer(s) < L - 1:
                        next_x(n, s, 0)
                    else:
                        last_x(q, n, s, b)
                    if more:
                        inverse_deviation(0, first_half, q_var1, 2 * q + 3, q_rstd1)
                        inverse_deviation(0, second_half, q_var1, 2 * q + 4, q_rstd1)
                        pool.wait_ge(q_agg, 2 * q + 4)
                        residual_h(q + 1, s + 1, 0)
                if last:
                    inverse_deviation(1, second_half, q_var2, 2 * (q + 1), q_rstd2)
                    inverse_deviation(2, all_nodes, q_var3, B, q_rstd3)

            inverse_deviation(0, slice(0, 2), q_var1, 1, q_rstd1)
            inverse_deviation(0, slice(2, NB), q_var1, 2, q_rstd1)
            pool.wait_ge(q_b1r, 1)
            residual_h(0, 0, 0)
            turn(0, True, False)
            with pool.Fori(1, TURNS - 1) as n:
                turn(n, False, False)
            turn(TURNS - 1, False, True)

        @block.vector
        def _(dve):
            def prepare_vectors():
                dve.wait_ge(q_const, 16 * VECTORS)
                nc.vector.tensor_tensor(b1r[:].rearrange("p l d -> p (l d)"), b1r[:].rearrange("p l d -> p (l d)"), b2_in,
                                        ALU.add).then_inc(q_b1r, 1)
                for l in range(L - 1):
                    for j in range(2):
                        if l or j:
                            dve.wait_ge(q_beta_w, 2 * l + j)
                        nc.vector.tensor_tensor_reduce(out=scrap, in0=b2r[:, l, :], in1=att_w[:, l + 1, j, :], scale=1.0,
                                                       scalar=0.0, op0=ALU.mult, op1=ALU.add,
                                                       accum_out=beta_w[:, l, j:j + 1]).then_inc(q_beta_w, 1)
                for j in range(2):
                    dve.wait_ge(q_beta_w, 2 * (L - 1) + j)
                    nc.vector.tensor_tensor(att_b[:, 1:L], att_b[:, 1:L], beta_w[:, :, j], ALU.add).then_inc(q_beta_w, 1)
                    nc.vector.tensor_tensor(att_w[:, 1:L, j, :], att_w[:, 1:L, j, :], g2r[:, 0:L - 1, :], ALU.mult)\
                        .then_inc(q_att_w, 1)
                dve.wait_ge(q_beta_w, 2 * L)
                dve.wait_ge(q_att_w, 2)

            def make_mask(b, a, blocks):
                for i in blocks:
                    dve.wait_ge(q_adj[i % 2], 16 * (NB // 2 * b + i // 2 + 1))
                    nc.vector.tensor_scalar(mask[a][:, i, :], adj_in[:, i % 2, :], 0, MASKED, ALU.is_le, ALU.mult)\
                        .then_inc(q_mask, 1)

            def clear_diagonal(b, a):
                dve.wait_ge(q_mask, (NB + 1) * b + NB)
                nc.vector.tensor_tensor(mask_diag[a], mask_diag[a], off_diag[:].unsqueeze(1).to_broadcast([P, NB, P]),
                                        ALU.mult).then_inc(q_mask, 1)

            def dots(n, s, f):
                a, l = thread(s), layer(s) + 1
                q, k = STEPS * n + s, normed(n, s)
                for i in range(2 * f, 2 * f + 2):
                    dve.wait_ge(q_n2, NB * q + i + 1)
                    for j in range(2):
                        at = 2 * NB * k + 2 * i + j
                        if 2 * i + j:
                            dve.wait_ge(q_dot, at)
                        nc.vector.tensor_tensor_reduce(out=scrap, in0=x[:, a, i, :], in1=att_w[:, l, j, :], scale=1.0,
                                                       scalar=0.0, op0=ALU.mult, op1=ALU.add,
                                                       accum_out=col[:, a, j, i:i + 1]).then_inc(q_dot, 1)
                dve.wait_ge(q_dot, 2 * NB * k + NB * (f + 1))

            def diagonal(s, blocks):
                a, l = thread(s), layer(s)
                for i in blocks:
                    nc.vector.tensor_scalar(diag[:, i, :], ident[:], col[:, a, 1, i:i + 1], None, ALU.mult)\
                        .then_inc(q_diag, 1)
                if NB - 1 in blocks:
                    nc.vector.tensor_scalar(query[:], col[:, a, 0, :], att_b[:, l:l + 1], None, ALU.add)\
                        .then_inc(q_query, 1)

            def first_terms(b, s):
                nc.vector.tensor_copy(col[:, thread(s)].rearrange("p j i -> p (j i)"),
                                      first_col[:, bass.ds(2 * NB * b, 2 * NB)]).then_inc(q_first, 1)
                dve.wait_ge(q_first, b + 1)
                diagonal(s, range(NB))

            def prepare(q, s):
                a = thread(s)
                dve.wait_ge(q_row, q + 1)
                if s:
                    dve.wait_ge(q_h, 4 * q - 3)
                dve.sem_inc(q_past, 1)
                for i in range(NB):
                    nc.vector.tensor_tensor_reduce(out=wt[:, i, :], in0=ps_turn[:, 0, :], in1=mask[a][:, i, :], scale=1.0,
                                                   scalar=LOWEST, op0=ALU.add, op1=ALU.max,
                                                   accum_out=top[:, i:i + 1]).then_inc(q_top, 1)
                dve.wait_ge(q_top, NB * (q + 1))
                dve.wait_ge(q_query, q + 1)
                nc.vector.tensor_tensor(tmp[:], top[:], query[:], ALU.add).then_inc(q_shift, 1)
                dve.wait_ge(q_shift, 4 * q + 1)
                nc.vector.scalar_tensor_tensor(out=shift[:], in0=tmp[:], scalar=SLOPE, in1=tmp[:],
                                               op0=ALU.mult, op1=ALU.max).then_inc(q_shift, 1)
                dve.wait_ge(q_shift, 4 * q + 2)
                nc.vector.scalar_tensor_tensor(out=sh_lo[:], in0=query[:], scalar=SLOPE, in1=shift[:],
                                               op0=ALU.mult, op1=ALU.subtract).then_inc(q_shift, 1)
                nc.vector.tensor_tensor(sh_hi[:], query[:], shift[:], ALU.subtract).then_inc(q_shift, 1)

            def exponents(q):
                def low_part(i):
                    nc.vector.tensor_scalar(low[:, i, :], wt[:, i, :], SLOPE, sh_lo[:, i:i + 1],
                                            ALU.mult, ALU.add).then_inc(q_low, 1)

                dve.wait_ge(q_shift, 4 * q + 3)
                low_part(0)
                dve.wait_ge(q_shift, 4 * q + 4)
                for i in range(NB):
                    if i + 1 < NB:
                        low_part(i + 1)
                    dve.wait_ge(q_low, NB * q + i + 1)
                    nc.vector.scalar_tensor_tensor(out=wt[:, i, :], in0=wt[:, i, :], scalar=sh_hi[:, i:i + 1],
                                                   in1=low[:, i, :], op0=ALU.add, op1=ALU.max).then_inc(q_arg, 1)

            def moments(data, which, blocks, before, ready, st, mvs, vs):
                for n, i in enumerate(blocks):
                    dve.wait_ge(ready[0], ready[1](n))
                    nc.vector.bn_stats(stats[:, which, i, :], data[:, i, :]).then_inc(st, 1)
                for n, i in enumerate(blocks):
                    dve.wait_ge(st, before + n + 1)
                    dve.sem_inc(q_past, 1)
                    nc.vector.bn_aggr(mv[:, which, i, :], stats[:, which, i, :]).then_inc(mvs, 1)
                dve.wait_ge(mvs, before + len(blocks))
                cols = slice(blocks[0], blocks[-1] + 1)
                nc.vector.tensor_scalar(var[:, which, cols], mv[:, which, cols, 1], EPS, None, ALU.add).then_inc(vs, 1)

            def scaled(out, which, blocks, done, data=None):
                data = out if data is None else data
                for i in blocks:
                    nc.vector.tensor_scalar(out[:, i, :], data[:, i, :], mv[:, which, i, 0:1], rstd[:, which, i:i + 1],
                                            ALU.subtract, ALU.mult).then_inc(done, 1)

            def attention_inverse(q):
                dve.wait_ge(q_exp, NB * (q + 1))
                nc.vector.reciprocal(inv[:], total[:]).then_inc(q_inv, 1)
                dve.wait_ge(q_inv, q + 1)

            def attention_residual(q, s, f):
                a = thread(s)
                blocks = range(2 * f, 2 * f + 2)
                dve.wait_ge(q_agg, 2 * q + f + 1)
                for i in blocks:
                    nc.vector.scalar_tensor_tensor(out=sums[:, i, :],
                                                   in0=ps_agg[:, i // 2, (i % 2) * D:(i % 2 + 1) * D],
                                                   scalar=inv[:, i:i + 1], in1=x[:, a, i, :],
                                                   op0=ALU.mult, op1=ALU.add).then_inc(q_r1, 1)
                moments(sums, 0, blocks, NB * q + 2 * f, (q_r1, lambda n: NB * q + 2 * f + n + 1),
                        q_st1, q_mv1, q_var1)

            def attention_norm(q, s, f):
                dve.wait_ge(q_rstd1, 2 * q + f + 1)
                scaled(x[:, thread(s)] if f else sums, 0, range(2 * f, 2 * f + 2), q_n1, sums)

            def h_whole(q, s, f):
                l, nodes = layer(s), N // 2
                dve.wait_ge(q_nT, 2 * q + f + 1)
                for k in range(DB):
                    nc.vector.tensor_scalar(whole[:, f, k * nodes:(k + 1) * nodes],
                                            ps_turn[:, (f + 1) % 2, k * nodes:(k + 1) * nodes],
                                            g1c[:, l * DB + k:l * DB + k + 1], b1c[:, l * DB + k:l * DB + k + 1],
                                            ALU.mult, ALU.add).then_inc(q_whole, 1)

            def h_lo_part(q, f):
                nodes = N // 2
                for k in range(DB):
                    dve.wait_ge(q_whole, DB * (2 * q + f) + k + 1)
                    dve.wait_ge(q_hhi, DB * (2 * q + f) + k + 1)
                    nc.vector.tensor_tensor(h_lo[:, k, f * nodes:(f + 1) * nodes], whole[:, f, k * nodes:(k + 1) * nodes],
                                            h_hi[:, k, f * nodes:(f + 1) * nodes].bitcast(F32),
                                            ALU.subtract).then_inc(q_hlo, 1)

            def feed_forward_residual(q, s, f):
                a = thread(s)
                rows = slice(2 * f, 2 * f + 2)
                dve.wait_ge(q_y, 2 * q + f + 1)
                dve.wait_ge(q_h, 4 * q + 2 * f + 2)
                nc.vector.tensor_tensor(x[:, a, rows, :], ps_y[:, f, :].rearrange("p (i n) -> p i n", i=2),
                                        x[:, a, rows, :], ALU.add).then_inc(q_r2, 1)
                moments(x[:, a], 1, range(2 * f, 2 * f + 2), NB * q + 2 * f, (q_r2, lambda n: 2 * q + f + 1),
                        q_st2, q_mv2, q_var2)

            def feed_forward_norm(q, s, f):
                dve.wait_ge(q_rstd2, 2 * q + f + 1)
                scaled(x[:, thread(s)], 1, range(2 * f, 2 * f + 2), q_n2)

            def last_residual(q, n, s, b):
                a, l = thread(s), layer(s)
                rows = slice(2, NB)
                dve.wait_ge(q_n2, NB * q + NB)
                nc.vector.tensor_tensor(x[:, a, rows, :], x[:, a, rows, :],
                                        g2r[:, l:l + 1, :].to_broadcast([P, 2, D]), ALU.mult).then_inc(q_last[1], 1)
                dve.wait_ge(q_last[1], 2 * b + 1)
                nc.vector.tensor_tensor(x[:, a, rows, :], x[:, a, rows, :],
                                        b2r[:, l:l + 1, :].to_broadcast([P, 2, D]), ALU.add).then_inc(q_last[1], 1)
                dve.wait_ge(q_last[1], 2 * b + 2)
                dve.wait_ge(q_fin[a], 16 * (n + 1))
                nc.vector.tensor_tensor(fin[:, a, rows, :], fin[:, a, rows, :], x[:, a, rows, :], ALU.add)\
                    .then_inc(q_r3[1], 1)

            def last_moments(a, b):
                dve.wait_ge(q_r3[0], b + 1)
                moments(fin[:, a], 2, range(NB), NB * b, (q_r3[1], lambda n: b + 1), q_st3, q_mv3, q_var3)

            def last_norm(a, b):
                dve.wait_ge(q_rstd3, b + 1)
                scaled(fin[:, a], 2, range(NB), q_out)

            def turn(n, first, last):
                for s in range(STEPS):
                    q, a, b = STEPS * n + s, thread(s), 2 * n + thread(s)
                    more = not (last and s == STEPS - 1)
                    inner = layer(s) < L - 1
                    ahead = not inner and not last
                    ended = s == STEPS - 1 or s == 0 and not first
                    if more:
                        prepare(q + 1, s + 1)
                        exponents(q + 1)
                    if ahead:
                        make_mask(b + 2, a, range(0, 2))
                    if ended:
                        last_moments(1 - a, b - 1)
                    feed_forward_residual(q, s, 0)
                    feed_forward_norm(q, s, 0)
                    if ended:
                        last_norm(1 - a, b - 1)
                    if inner:
                        dots(n, s, 0)
                        diagonal(s + 2, range(0, 2))
                    elif ahead:
                        make_mask(b + 2, a, range(2, NB))
                        clear_diagonal(b + 2, a)
                    if more:
                        attention_inverse(q + 1)
                        attention_residual(q + 1, s + 1, 0)
                        attention_norm(q + 1, s + 1, 0)
                        attention_residual(q + 1, s + 1, 1)
                        h_whole(q + 1, s + 1, 0)
                        attention_norm(q + 1, s + 1, 1)
                        h_lo_part(q + 1, 0)
                        h_whole(q + 1, s + 1, 1)
                        h_lo_part(q + 1, 1)
                    feed_forward_residual(q, s, 1)
                    if ahead:
                        first_terms(b + 2, s + 2)
                        dve.wait_ge(q_mask, (NB + 1) * (b + 3))
                    feed_forward_norm(q, s, 1)
                    if inner:
                        dots(n, s, 1)
                        diagonal(s + 2, range(2, NB))
                    else:
                        last_residual(q, n, s, b)
                if last:
                    last_moments(1, B - 1)
                    last_norm(1, B - 1)

            dve.wait_ge(q_small, 16 * SMALL)
            first_terms(0, 0)
            make_mask(0, 0, range(NB))
            clear_diagonal(0, 0)
            dve.wait_ge(q_mask, NB + 1)
            prepare(0, 0)
            exponents(0)
            prepare_vectors()
            attention_inverse(0)
            attention_residual(0, 0, 0)
            attention_norm(0, 0, 0)
            attention_residual(0, 0, 1)
            h_whole(0, 0, 0)
            attention_norm(0, 0, 1)
            h_lo_part(0, 0)
            h_whole(0, 0, 1)
            h_lo_part(0, 1)
            first_terms(1, 1)
            make_mask(1, 1, range(NB))
            clear_diagonal(1, 1)
            dve.wait_ge(q_mask, 2 * (NB + 1))
            turn(0, True, False)
            with dve.Fori(1, TURNS - 1) as n:
                turn(n, False, False)
            turn(TURNS - 1, False, True)

        @block.scalar
        def _(act):
            act.wait_ge(q_small, 16 * SMALL)

            def exps(q):
                for i in range(NB):
                    act.wait_ge(q_arg, NB * q + i + 1)
                    nc.scalar.activation(wt[:, i, :], wt[:, i, :], ACT.Exp, accum_out=total[:, i:i + 1]).then_inc(q_exp, 1)

            def keep_turned(q):
                for j in range(NB):
                    act.wait_ge(q_turn, NB * q + j + 1)
                    nc.scalar.copy(wtT[:, j, :], ps_turn[:, (j + 1) % 2, :]).then_inc(q_wtT, 1)

            def keep_h(q):
                nodes = N // 2
                for f in range(2):
                    for k in range(DB):
                        act.wait_ge(q_whole, DB * (2 * q + f) + k + 1)
                        nc.scalar.copy(h_hi[:, k, f * nodes:(f + 1) * nodes],
                                       whole[:, f, k * nodes:(k + 1) * nodes]).then_inc(q_hhi, 1)

            def gelu(q, s, c):
                l = layer(s)
                act.wait_ge(q_ff, FB * q + c + 1)
                for n, out in enumerate((g_hi[:, c, :], whole[:, c % 2, :])):
                    if n and c >= 2:
                        act.wait_ge(q_glo, FB * q + c - 1)
                    nc.scalar.activation(out, ff_bank(c), ACT.Gelu,
                                         bias=ffb[:, l * FB + c:l * FB + c + 1]).then_inc(q_gelu, 1)

            def turn(n, last):
                for s in range(STEPS):
                    q = STEPS * n + s
                    for c in range(FB):
                        gelu(q, s, c)
                    if not (last and s == STEPS - 1):
                        exps(q + 1)
                        keep_turned(q + 1)
                        keep_h(q + 1)

            exps(0)
            keep_turned(0)
            keep_h(0)
            with act.Fori(0, TURNS - 1) as n:
                turn(n, False)
            turn(TURNS - 1, True)

        @block.tensor
        def _(pe):
            def key_row(q):
                pe.wait_ge(q_diag, NB * (q + 1))
                for i in range(NB):
                    mm = nc.tensor.matmul(ps_turn[:, 0, i * P:(i + 1) * P], ones[:], diag[:, i, :], start=True, stop=True)
                mm.then_inc(q_row, 1)

            def turn_weights(q, tiles):
                for i in range(NB):
                    if tiles[0] == 0:
                        pe.wait_ge(q_exp, NB * q + i + 1)
                    for j in tiles:
                        if j >= 2 and i == 0:
                            pe.wait_ge(q_wtT, NB * q + j - 1)
                        mm = nc.tensor.transpose(ps_turn[:, (j + 1) % 2, i * P:(i + 1) * P], wt[:, i, j * P:(j + 1) * P],
                                                 ident[:])
                        if i == NB - 1:
                            mm.then_inc(q_turn, 1)

            def attend(q, n, s):
                a = thread(s)
                if s % STEPS < 2:
                    pe.wait_ge(q_x[a], 16 * (n + s // STEPS + 1))
                else:
                    pe.wait_ge(q_next, 4 * normed(n, s - 2) + 4)
                pe.wait_ge(q_wtT, NB * (q + 1))
                for i in range(NB):
                    for j in range(NB):
                        mm = nc.tensor.matmul(ps_agg[:, i // 2, (i % 2) * D:(i % 2 + 1) * D],
                                              wtT[:, j, i * P:(i + 1) * P], x[:, a, j, :],
                                              start=(j == 0), stop=(j == NB - 1))
                    if i % 2:
                        mm.then_inc(q_agg, 1)

            def turn_n(q, s, f):
                a, nodes = thread(s), N // 2
                pe.wait_ge(q_n1, NB * q + 2 * f + 2)
                for k in range(DB):
                    for i in range(2):
                        mm = nc.tensor.transpose(ps_turn[:, (f + 1) % 2, k * nodes + i * P:k * nodes + (i + 1) * P],
                                                 (x[:, a] if f else sums)[:, 2 * f + i, k * P:(k + 1) * P], ident[:])
                mm.then_inc(q_nT, 1)

            def first_product(q, s, c, halves=(None,), row=False):
                l = layer(s)
                if c >= 3:
                    pe.wait_ge(q_gelu, 2 * (FB * q + c - 2))
                for f in halves:
                    nodes = slice(0, N) if f is None else slice(f * N // 2, (f + 1) * N // 2)
                    out = ff_bank(c)[:, nodes]
                    for k in range(DB):
                        if c == 0:
                            pe.wait_ge(q_hhi, DB * (2 * q + f) + k + 1)
                        for w in (w_hi, w_lo):
                            nc.tensor.matmul(out, w1(w, l, k, c), h_hi[:, k, nodes],
                                             start=(k == 0 and w is w_hi), stop=False)
                    if row:
                        key_row(q + 1)
                    for k in range(DB):
                        if c == 0:
                            pe.wait_ge(q_hlo, DB * (2 * q + f) + k + 1)
                        mm = nc.tensor.matmul(out, w1(w_hi, l, k, c), h_lo[:, k, nodes],
                                              start=False, stop=(k == DB - 1))
                if f != 0:
                    mm.then_inc(q_ff, 1)

            def hi_products(q, s, i, chunks=range(FB)):
                for c in chunks:
                    if i == 0:
                        pe.wait_ge(q_gelu, 2 * (FB * q + c) + 1)
                    for w in (w_hi, w_lo):
                        nc.tensor.matmul(ps_y[:, i // 2, (i % 2) * D:(i % 2 + 1) * D], g_hi[:, c, i * P:(i + 1) * P],
                                         w2(w, layer(s), c), start=(c == 0 and w is w_hi), stop=False)

            def lo_products(q, s, i):
                for c in range(FB):
                    if i == 0:
                        pe.wait_ge(q_glo, FB * q + c + 1)
                    mm = nc.tensor.matmul(ps_y[:, i // 2, (i % 2) * D:(i % 2 + 1) * D], g_lo[:, c, i * P:(i + 1) * P],
                                          w2(w_hi, layer(s), c), start=False, stop=(c == FB - 1))
                if i % 2:
                    mm.then_inc(q_y, 1)

            def turn(n, last):
                for s in range(STEPS):
                    q = STEPS * n + s
                    more = not (last and s == STEPS - 1)
                    for f in range(2):
                        for c in range(2):
                            first_product(q, s, c, (f,))
                    for c in range(2, FB):
                        first_product(q, s, c, row=c == ROW_AT and more)
                    hi_products(q, s, 0)
                    hi_products(q, s, 2, range(0, FB // 4))
                    lo_products(q, s, 0)
                    hi_products(q, s, 1)
                    if more:
                        turn_weights(q + 1, range(0, 2))
                    lo_products(q, s, 1)
                    if more:
                        turn_weights(q + 1, range(2, NB))
                    hi_products(q, s, 2, range(FB // 4, FB))
                    if more:
                        attend(q + 1, n, s + 1)
                    lo_products(q, s, 2)
                    if more:
                        turn_n(q + 1, s + 1, 0)
                    hi_products(q, s, 3)
                    lo_products(q, s, 3)
                    if more:
                        turn_n(q + 1, s + 1, 1)

            key_row(0)
            turn_weights(0, range(0, 2))
            turn_weights(0, range(2, NB))
            attend(0, 0, 0)
            turn_n(0, 0, 0)
            turn_n(0, 0, 1)
            with pe.Fori(0, TURNS - 1) as n:
                turn(n, False)
            turn(TURNS - 1, True)


_INS = ("x", "xT", "adj", "adjT", "gat_w1", "att_src1", "att_dst1", "gat_b1T", "gat_w2", "att_src2", "att_dst2",
        "gat_b2", "attn_w", "attn_b", "ff_w", "ff_b1", "ff_b1T", "ff_b2", "g1", "beta1", "g1T", "beta1T", "g2", "beta2")


def layouts(a):
    import numpy as np
    L, D = a["L1_gnn_g1"].shape
    B = a["x"].shape[0]
    heads = a["L0_gnn_att_src1"].shape[0]
    FF = a["L1_gnn_b1"].shape[1]

    def on_partitions(v):
        v = v.reshape(v.shape[:-1] + (-1, P))
        return v.reshape(-1, P).T

    w1 = a["L1_gnn_W1"].reshape(L, D // P, P, FF).transpose(2, 0, 1, 3).reshape(P, -1)
    w2 = a["L1_gnn_W2"].reshape(L, FF // P, P, D).transpose(2, 0, 1, 3).reshape(P, -1)
    ff_w = np.concatenate([w1, w2], axis=1).reshape(P, B, -1).transpose(1, 0, 2)
    return {
        "x": a["x"], "xT": a["x"].transpose(0, 2, 1), "adj": a["adj"], "adjT": a["adj"].transpose(0, 2, 1),
        "gat_w1": a["L0_gnn_W1"], "att_src1": a["L0_gnn_att_src1"], "att_dst1": a["L0_gnn_att_dst1"],
        "gat_b1T": on_partitions(a["L0_gnn_b1"]), "gat_w2": a["L0_gnn_W2"],
        "att_src2": a["L0_gnn_att_src2"], "att_dst2": a["L0_gnn_att_dst2"], "gat_b2": a["L0_gnn_b2"],
        "attn_w": a["L1_gnn_attn_w"], "attn_b": a["L1_gnn_attn_b"], "ff_w": ff_w,
        "ff_b1": a["L1_gnn_b1"], "ff_b1T": on_partitions(a["L1_gnn_b1"]), "ff_b2": a["L1_gnn_b2"],
        "g1": a["L1_gnn_g1"], "beta1": a["L1_gnn_beta1"], "g1T": on_partitions(a["L1_gnn_g1"]),
        "beta1T": on_partitions(a["L1_gnn_beta1"]), "g2": a["L1_gnn_g2"], "beta2": a["L1_gnn_beta2"],
    }


def kernel(**inputs):
    import numpy as np
    import concourse.bacc as bacc
    from concourse.bass_utils import run_bass_kernel_spmd

    nc = bacc.Bacc("TRN2", target_bir_lowering=False, num_devices=1)
    arrays, tensors = {}, {}
    laid_out = layouts({k: np.asarray(v) for k, v in inputs.items()})
    for name in _INS:
        a = np.ascontiguousarray(laid_out[name])
        arrays["in_" + name] = a
        tensors[name] = nc.dram_tensor("in_" + name, a.shape, mybir.dt.from_np(a.dtype), kind="ExternalInput").ap()
    shape = laid_out["x"].shape
    tensors["out"] = nc.dram_tensor("out_0", shape, F32, kind="ExternalOutput").ap()
    graph_kernel(nc, tensors)
    r = run_bass_kernel_spmd(nc, [arrays], core_ids=[0])
    return r.results[0]["out_0"]
```
